# Optimizing a Trainium2 kernel written in Bass

```python
import numpy as np
import jax
import jax.numpy as jnp

def _softmax(x, axis=-1):
    return jax.nn.softmax(x, axis=axis)

def _gelu(x):
    return jax.nn.gelu(x, approximate=True)

def _silu(x):
    return jax.nn.silu(x)

def _sigmoid(x):
    return jax.nn.sigmoid(x)

def _layernorm(x, axis=-1, eps=1e-05):
    m = jnp.mean(x, axis=axis, keepdims=True)
    v = jnp.var(x, axis=axis, keepdims=True)
    return (x - m) / jnp.sqrt(v + eps)

def _scatter_add(tgt, idx, src, axis=0):
    return tgt.at[idx].add(src)

def _segment_sum(src, seg, n):
    return jax.ops.segment_sum(src, seg, n)
kernel_name = 'mk_xattn_ffn_d1_seqx_r4_02fcbf'

def setup_inputs(seed: int=0):
    np.random.seed(seed)
    _w = jnp.asarray

    def _rec_inputs():
        import jax
        import jax.numpy as jnp
        _rk = jax.random.key(seed)
        x = 7.22e-05 + 1 * jax.random.normal(jax.random.fold_in(_rk, 1), (8, 256, 256), jnp.float32)
        _lenS = 256 - jax.random.randint(jax.random.fold_in(_rk, 7), (8,), 0, max(1, 256 // 4) + 1, jnp.int32)
        _lenS2 = 77 - jax.random.randint(jax.random.fold_in(_rk, 8), (8,), 0, max(1, 77 // 4) + 1, jnp.int32)
        _ctx_1024P = jax.random.normal(jax.random.fold_in(_rk, 11), (8, 16, 256), jnp.float32)
        _ctx_1024c = jax.random.dirichlet(jax.random.fold_in(_rk, 511), 0.3 * jnp.ones((16,), jnp.float32), (8, 77))
        _ctx_1024t = jnp.einsum('bsk,bkd->bsd', _ctx_1024c, _ctx_1024P)
        _ctx_1024t = _ctx_1024t * jax.lax.rsqrt(jnp.mean(jnp.square(_ctx_1024t)) + 1e-12) * 0.953939
        ctx_1024 = 4.13588e-05 + 0.999923 * (_ctx_1024t + 0.3 * jax.random.normal(jax.random.fold_in(_rk, 611), (8, 77, 256), jnp.float32))
        return (x, ctx_1024)
    x, ctx_1024 = _rec_inputs()

    def _L0_xattn_setup():
        import jax, jax.numpy as jnp
        import numpy as np
        DIM = 256
        HEADS = 16
        DIM_HEAD = 64
        INNER = HEADS * DIM_HEAD
        MLP = 1024
        EPS = 1e-05

        def _layernorm(x, g, b):
            mu = jnp.mean(x, axis=-1, keepdims=True)
            var = jnp.mean(jnp.square(x - mu), axis=-1, keepdims=True)
            return (x - mu) * jax.lax.rsqrt(var + EPS) * g + b

        def _l2norm(x):
            n = jnp.sqrt(jnp.sum(jnp.square(x), axis=-1, keepdims=True))
            return x / jnp.maximum(n, 1e-12)

        def _split_heads(x, B, N):
            return x.reshape(B, N, HEADS, DIM_HEAD).transpose(0, 2, 1, 3)
        key = jax.random.key(seed)
        ks = jax.random.split(key, 16)
        B, N = (4, 512)
        s = 0.02
        return {'Q': jax.random.normal(ks[0], (B, N, DIM), jnp.float32), 'K': jax.random.normal(ks[1], (B, N, DIM), jnp.float32), 'V': jax.random.normal(ks[2], (B, N, DIM), jnp.float32), 'wq': jax.random.normal(ks[3], (DIM, INNER), jnp.float32) * s, 'wk': jax.random.normal(ks[4], (DIM, INNER), jnp.float32) * s, 'wv': jax.random.normal(ks[5], (DIM, INNER), jnp.float32) * s, 'wo': jax.random.normal(ks[6], (INNER, DIM), jnp.float32) * s, 'bo': jnp.zeros((DIM,), jnp.float32), 'w1': jax.random.normal(ks[7], (DIM, MLP), jnp.float32) * s, 'b1': jnp.zeros((MLP,), jnp.float32), 'w2': jax.random.normal(ks[8], (MLP, DIM), jnp.float32) * s, 'b2': jnp.zeros((DIM,), jnp.float32), 'ln1_g': jnp.ones((DIM,), jnp.float32), 'ln1_b': jnp.zeros((DIM,), jnp.float32), 'ln2_g': jnp.ones((DIM,), jnp.float32), 'ln2_b': jnp.zeros((DIM,), jnp.float32)}
    _L0_xattn_all = _L0_xattn_setup()
    _L0_xattn_in = {k: v for k, v in _L0_xattn_all.items() if k in ('wq', 'wk', 'wv', 'wo', 'bo', 'w1', 'b1', 'w2', 'b2', 'ln1_g', 'ln1_b', 'ln2_g', 'ln2_b')}
    del _L0_xattn_all

    def _L0_ffn_setup():
        import jax, jax.numpy as jnp
        import numpy as np
        B, S, H = (1, 512, 256)
        E, K = (16, 4)
        G, TG = (4, 2)
        I_MOE = 128
        N_SH = 2
        SCALE = 2.5

        def _mlp(x, gw, uw, dw):
            return jax.nn.silu(x @ gw.T) * (x @ uw.T) @ dw.T

        def _route(x2d, router_weight, e_bias):
            T = x2d.shape[0]
            scores = jax.nn.sigmoid(x2d @ router_weight.T)
            sc = scores + e_bias[None, :]
            group_scores = jnp.sum(jax.lax.top_k(sc.reshape(T, G, E // G), 2)[0], axis=-1)
            _, gidx = jax.lax.top_k(group_scores, TG)
            gmask = jnp.zeros((T, G), sc.dtype).at[jnp.arange(T)[:, None], gidx].set(1.0)
            smask = jnp.repeat(gmask, E // G, axis=1)
            masked = jnp.where(smask > 0, sc, 0.0)
            _, tidx = jax.lax.top_k(masked, K)
            tw = jnp.take_along_axis(scores, tidx, axis=1)
            tw = tw / (jnp.sum(tw, axis=-1, keepdims=True) + 1e-20)
            tw = tw * SCALE
            return (tidx, tw)

        def _moe_forward(hidden_states, router_weight, e_bias, gate_w, up_w, down_w, sh_gate_w, sh_up_w, sh_down_w):
            orig_shape = hidden_states.shape
            x = hidden_states.reshape(-1, H)
            T = x.shape[0]
            tidx, tw = _route(x, router_weight, e_bias)
            g = jnp.einsum('th,eih->tei', x, gate_w)
            u = jnp.einsum('th,eih->tei', x, up_w)
            h = jax.nn.silu(g) * u
            yo = jnp.einsum('tei,ehi->teh', h, down_w)
            combine = jnp.zeros((T, E), tw.dtype).at[jnp.arange(T)[:, None], tidx].add(tw)
            routed = jnp.einsum('te,teh->th', combine, yo)
            shared = _mlp(hidden_states.reshape(-1, H), sh_gate_w, sh_up_w, sh_down_w)
            return (routed + shared).reshape(orig_shape)
        key = jax.random.key(seed)
        ks = jax.random.split(key, 9)
        s = 0.02
        return {'hidden_states': jax.random.normal(ks[0], (B, S, H), jnp.float32), 'router_weight': jax.random.normal(ks[1], (E, H), jnp.float32) * s, 'e_bias': jnp.zeros((E,), jnp.float32), 'gate_w': jax.random.normal(ks[2], (E, I_MOE, H), jnp.float32) * s, 'up_w': jax.random.normal(ks[3], (E, I_MOE, H), jnp.float32) * s, 'down_w': jax.random.normal(ks[4], (E, H, I_MOE), jnp.float32) * s, 'sh_gate_w': jax.random.normal(ks[5], (N_SH * I_MOE, H), jnp.float32) * s, 'sh_up_w': jax.random.normal(ks[6], (N_SH * I_MOE, H), jnp.float32) * s, 'sh_down_w': jax.random.normal(ks[7], (H, N_SH * I_MOE), jnp.float32) * s}
    _L0_ffn_all = _L0_ffn_setup()
    _L0_ffn_in = {k: v for k, v in _L0_ffn_all.items() if k in ('router_weight', 'e_bias', 'gate_w', 'up_w', 'down_w', 'sh_gate_w', 'sh_up_w', 'sh_down_w')}
    del _L0_ffn_all
    return {'x': x, 'ctx_1024': ctx_1024, 'L0_xattn_wq': _L0_xattn_in['wq'], 'L0_xattn_wk': _L0_xattn_in['wk'], 'L0_xattn_wv': _L0_xattn_in['wv'], 'L0_xattn_wo': _L0_xattn_in['wo'], 'L0_xattn_bo': _L0_xattn_in['bo'], 'L0_xattn_w1': _L0_xattn_in['w1'], 'L0_xattn_b1': _L0_xattn_in['b1'], 'L0_xattn_w2': _L0_xattn_in['w2'], 'L0_xattn_b2': _L0_xattn_in['b2'], 'L0_xattn_ln1_g': _L0_xattn_in['ln1_g'], 'L0_xattn_ln1_b': _L0_xattn_in['ln1_b'], 'L0_xattn_ln2_g': _L0_xattn_in['ln2_g'], 'L0_xattn_ln2_b': _L0_xattn_in['ln2_b'], 'L0_ffn_router_weight': _L0_ffn_in['router_weight'], 'L0_ffn_e_bias': _L0_ffn_in['e_bias'], 'L0_ffn_gate_w': _L0_ffn_in['gate_w'], 'L0_ffn_up_w': _L0_ffn_in['up_w'], 'L0_ffn_down_w': _L0_ffn_in['down_w'], 'L0_ffn_sh_gate_w': _L0_ffn_in['sh_gate_w'], 'L0_ffn_sh_up_w': _L0_ffn_in['sh_up_w'], 'L0_ffn_sh_down_w': _L0_ffn_in['sh_down_w']}

def reference(x, ctx_1024, L0_xattn_wq, L0_xattn_wk, L0_xattn_wv, L0_xattn_wo, L0_xattn_bo, L0_xattn_w1, L0_xattn_b1, L0_xattn_w2, L0_xattn_b2, L0_xattn_ln1_g, L0_xattn_ln1_b, L0_xattn_ln2_g, L0_xattn_ln2_b, L0_ffn_router_weight, L0_ffn_e_bias, L0_ffn_gate_w, L0_ffn_up_w, L0_ffn_down_w, L0_ffn_sh_gate_w, L0_ffn_sh_up_w, L0_ffn_sh_down_w):
    import jax
    import jax.numpy as jnp

    def _L0_xattn_ref(Q, K, V, wq, wk, wv, wo, bo, w1, b1, w2, b2, ln1_g, ln1_b, ln2_g, ln2_b):
        import jax, jax.numpy as jnp
        import numpy as np
        DIM = 256
        HEADS = 16
        DIM_HEAD = 64
        INNER = HEADS * DIM_HEAD
        MLP = 1024
        EPS = 1e-05

        def _layernorm(x, g, b):
            mu = jnp.mean(x, axis=-1, keepdims=True)
            var = jnp.mean(jnp.square(x - mu), axis=-1, keepdims=True)
            return (x - mu) * jax.lax.rsqrt(var + EPS) * g + b

        def _l2norm(x):
            n = jnp.sqrt(jnp.sum(jnp.square(x), axis=-1, keepdims=True))
            return x / jnp.maximum(n, 1e-12)

        def _split_heads(x, B, N):
            return x.reshape(B, N, HEADS, DIM_HEAD).transpose(0, 2, 1, 3)
        B, Nq, _ = Q.shape
        Nk = K.shape[1]
        Qn = _layernorm(Q, ln1_g, ln1_b)
        Kn = _layernorm(K, ln1_g, ln1_b)
        Vn = _layernorm(V, ln1_g, ln1_b)
        q = _split_heads(Qn @ wq, B, Nq)
        k = _split_heads(Kn @ wk, B, Nk)
        v = _split_heads(Vn @ wv, B, Nk)
        qn = _l2norm(q)
        kn = _l2norm(k)
        attn = jnp.einsum('bhqd,bhkd->bhqk', qn, kn)
        out = jnp.einsum('bhqk,bhkd->bhqd', attn, v)
        out = out.transpose(0, 2, 1, 3).reshape(B, Nq, INNER)
        x = Q + out @ wo + bo
        xn = _layernorm(x, ln2_g, ln2_b)
        h = jax.nn.gelu(xn @ w1 + b1, approximate=False)
        return x + h @ w2 + b2

    def _L0_ffn_ref(hidden_states, router_weight, e_bias, gate_w, up_w, down_w, sh_gate_w, sh_up_w, sh_down_w):
        import jax, jax.numpy as jnp
        import numpy as np
        B, S, H = (1, 512, 256)
        E, K = (16, 4)
        G, TG = (4, 2)
        I_MOE = 128
        N_SH = 2
        SCALE = 2.5

        def _mlp(x, gw, uw, dw):
            return jax.nn.silu(x @ gw.T) * (x @ uw.T) @ dw.T

        def _route(x2d, router_weight, e_bias):
            T = x2d.shape[0]
            scores = jax.nn.sigmoid(x2d @ router_weight.T)
            sc = scores + e_bias[None, :]
            group_scores = jnp.sum(jax.lax.top_k(sc.reshape(T, G, E // G), 2)[0], axis=-1)
            _, gidx = jax.lax.top_k(group_scores, TG)
            gmask = jnp.zeros((T, G), sc.dtype).at[jnp.arange(T)[:, None], gidx].set(1.0)
            smask = jnp.repeat(gmask, E // G, axis=1)
            masked = jnp.where(smask > 0, sc, 0.0)
            _, tidx = jax.lax.top_k(masked, K)
            tw = jnp.take_along_axis(scores, tidx, axis=1)
            tw = tw / (jnp.sum(tw, axis=-1, keepdims=True) + 1e-20)
            tw = tw * SCALE
            return (tidx, tw)

        def _moe_forward(hidden_states, router_weight, e_bias, gate_w, up_w, down_w, sh_gate_w, sh_up_w, sh_down_w):
            orig_shape = hidden_states.shape
            x = hidden_states.reshape(-1, H)
            T = x.shape[0]
            tidx, tw = _route(x, router_weight, e_bias)
            g = jnp.einsum('th,eih->tei', x, gate_w)
            u = jnp.einsum('th,eih->tei', x, up_w)
            h = jax.nn.silu(g) * u
            yo = jnp.einsum('tei,ehi->teh', h, down_w)
            combine = jnp.zeros((T, E), tw.dtype).at[jnp.arange(T)[:, None], tidx].add(tw)
            routed = jnp.einsum('te,teh->th', combine, yo)
            shared = _mlp(hidden_states.reshape(-1, H), sh_gate_w, sh_up_w, sh_down_w)
            return (routed + shared).reshape(orig_shape)
        return _moe_forward(hidden_states, router_weight, e_bias, gate_w, up_w, down_w, sh_gate_w, sh_up_w, sh_down_w)
    x = x + _L0_xattn_ref(_layernorm(x, axis=-1), ctx_1024, ctx_1024, L0_xattn_wq, L0_xattn_wk, L0_xattn_wv, L0_xattn_wo, L0_xattn_bo, L0_xattn_w1, L0_xattn_b1, L0_xattn_w2, L0_xattn_b2, L0_xattn_ln1_g, L0_xattn_ln1_b, L0_xattn_ln2_g, L0_xattn_ln2_b)
    x = x + _L0_ffn_ref(_layernorm(x, axis=-1), L0_ffn_router_weight, L0_ffn_e_bias, L0_ffn_gate_w, L0_ffn_up_w, L0_ffn_down_w, L0_ffn_sh_gate_w, L0_ffn_sh_up_w, L0_ffn_sh_down_w)
    return x

_drawn_inputs = setup_inputs


def setup_inputs(seed=0):
    import zlib

    import numpy as np

    out = dict(_drawn_inputs(seed))
    spreads = {'L0_xattn_bo': (0.0, 0.1),
     'L0_xattn_b1': (0.0, 0.528),
     'L0_xattn_b2': (0.0, 0.1),
     'L0_xattn_ln1_g': (1.0, 0.2),
     'L0_xattn_ln1_b': (0.0, 0.1),
     'L0_xattn_ln2_g': (1.0, 0.6),
     'L0_xattn_ln2_b': (0.0, 0.8),
     'L0_ffn_e_bias': (0.0, 0.8)}
    factors = {'L0_ffn_router_weight': 8.0,
     'L0_ffn_gate_w': 8.0,
     'L0_ffn_up_w': 7.952,
     'L0_ffn_down_w': 7.956,
     'L0_ffn_sh_gate_w': 7.118,
     'L0_ffn_sh_up_w': 7.069,
     'L0_ffn_sh_down_w': 7.01}
    for name, (base, spread) in spreads.items():
        noise = np.random.default_rng([zlib.crc32(name.encode()), seed]).standard_normal(out[name].shape)
        drawn = base * np.exp(spread * noise) if base else spread * noise
        out[name] = jnp.asarray(drawn.astype(out[name].dtype))
    for name, factor in factors.items():
        out[name] = (out[name] * factor).astype(out[name].dtype)
    return out
```

```python
from contextlib import ExitStack

import concourse.bass as bass
from concourse import mybir

ALU = mybir.AluOpType
ACT = mybir.ActivationFunctionType
AX = mybir.AxisListType
F32 = mybir.dt.float32
F32R = mybir.dt.float32r

P = 128
LOOP_BATCHES = False


class Batch:

    def __init__(self, offset, register=None):
        self.offset, self.register = offset, register

    def __add__(self, n):
        return Batch(self.offset + n, self.register)

    @property
    def index(self):
        return self.offset if self.register is None else self.register * 2 + self.offset

    @property
    def first(self):
        return self.register is None and self.offset == 0

    @property
    def parity(self):
        return self.offset % 2

    def count(self, per, done):
        value = per * self.offset + done
        if self.register is None:
            return value
        assert value > 0
        return self.register * (2 * per) + value


def bass_cross_attention_ffn_moe_kernel(nc, x, context, wq, wk, wv, wo, w1, w2, router_t, columns, rows, experts, out):
    NB, NQ, D = x.shape
    _, NK, _ = context.shape
    INNER = wq.shape[1]
    MLP = w1.shape[1]
    E = router_t.shape[1]
    NX = experts.shape[0]
    SH = NX - E
    HEAD = 64
    NH = INNER // HEAD
    KC = D // P
    IC = INNER // P
    MC = MLP // P
    TT = NQ // P
    NT = NB * TT
    CROWS = NB * NK
    CT = (CROWS + P - 1) // P
    CLAST = CROWS - (CT - 1) * P
    BLK = 512
    TB = NB * NQ // BLK
    TPB = BLK // P
    BB = BLK // NQ
    GROUPS, TOPG, TOPK, SCALE = 4, 2, 4, 2.5
    EG = E // GROUPS
    EPS = 1e-5
    assert D == 256 and INNER == 1024 and MLP == 1024 and TT == 2 and NB == 8 and SH == 2 and TOPG == 2

    x_v = x.rearrange("b (t p) d -> p b t d", p=P)
    out_v = out.rearrange("b (t p) d -> p b t d", p=P)
    ctx_v = context.rearrange("b s d -> (b s) d")

    with ExitStack() as ctx:
        def sb(name, shape, dt=F32):
            return ctx.enter_context(nc.sbuf_tensor(name, shape, dt))

        def sem(name):
            return ctx.enter_context(nc.semaphore(name))

        w_io = [sb(f"w_io_{s}", [P, 2, IC * D], F32R) for s in ("hi", "lo")]
        w_mlp = [sb(f"w_mlp_{s}", [P, 2, MC * D], F32R) for s in ("hi", "lo")]
        W = [sb(f"W_{s}", [P, IC, D], F32R) for s in ("hi", "lo")]
        kvd = [sb(f"kvd_{s}", [P, IC, P], F32R) for s in ("hi", "lo")]
        qnT = [sb(f"qnT_{s}", [P, IC, NQ], F32R) for s in ("hi", "lo")]
        h = [sb(f"h_{s}", [P, MC, NQ], F32R) for s in ("hi", "lo")]
        QnT = [sb(f"QnT_{s}", [P, KC, NQ], F32R) for s in ("hi", "lo")]
        xnT = [sb(f"xnT_{s}", [P, KC, NQ], F32R) for s in ("hi", "lo")]
        rw = [sb(f"rw_{s}", [P, KC, E], F32R) for s in ("hi", "lo")]
        acc = sb("acc", [P, NB, TT * D])
        kv_z = sb("kv_z", [P, NB, TT * D])
        hf = sb("hf", [P, 4, BLK])
        qn = sb("qn", [P, TT, INNER])
        sq = sb("sq", [P, INNER])
        arena = sb("arena", [P, 9 * 512])
        ident = sb("ident", [P, P])
        cols = sb("cols", [P, columns.shape[1]])
        rowsb = sb("rowsb", [P, rows.shape[1]])
        rwf = sb("rwf", [P, KC, E])
        stat = sb("stat", [P, CT, 6])
        mv = sb("mv", [P, CT, 2])
        st_x, mv_x = sb("st_x", [P, TT, 6]), sb("mv_x", [P, TT, 2])
        st_q, mv_q = sb("st_q", [P, TT, 6]), sb("mv_q", [P, TT, 2])
        st_1, mv_1 = sb("st_1", [P, TT, 6]), sb("mv_1", [P, TT, 2])
        st_3, mv_3 = sb("st_3", [P, TT, 6]), sb("mv_3", [P, TT, 2])
        rs_c = sb("rs_c", [P, CT])
        rs_x, rs_q2, rs_1, rs_3 = (sb(n, [P, TT]) for n in ("rs_x", "rs_q2", "rs_1", "rs_3"))
        ss = sb("ss", [P, TT, NH])
        rs_n = sb("rs_n", [P, TT, NH])
        half = sb("half", [P, 32])

        g1, b1l, g2, b2l = (cols[:, KC * i:KC * i + KC] for i in range(4))
        b1c = cols[:, 4 * KC:4 * KC + MC]
        bo_r, b2_r = rowsb[:, 0:D], rowsb[:, D:2 * D]
        ebias = rowsb[:, 2 * D:2 * D + E]

        def part(i, n=1):
            return arena[:, 512 * i:512 * (i + n)]
        Q = [part(0), part(1)]
        x1 = [part(2), part(3)]
        xn0, z0, Qn0, QnTf, xnTf = (part(i) for i in range(4, 9))
        kn = part(2, 2)
        vc = part(4, 2)
        wq_s = [w[:, 0, :].rearrange("p (k n) -> p k n", k=KC) for w in w_io]
        wo_s = [w[:, 1, :].rearrange("p (c n) -> p c n", c=IC) for w in w_io]
        w1_s = [w[:, 0, :].rearrange("p (k n) -> p k n", k=KC) for w in w_mlp]
        w2_s = [w[:, 1, :].rearrange("p (c n) -> p c n", c=MC) for w in w_mlp]
        wk_s = [w[:].rearrange("p c n -> p (c n)").rearrange("p (k n) -> p k n", k=KC) for w in qnT]
        wv_s = [w[:].rearrange("p c n -> p (c n)").rearrange("p (k n) -> p k n", k=KC) for w in h]
        kvf = kv_z[:].rearrange("p b n -> p (b n)")
        c0 = kvf[:, 5 * 512:5 * 512 + CT * D].rearrange("p (c n) -> p c n", c=CT)
        cTf = kvf[:, 1280:1280 + KC * CROWS].rearrange("p (k n) -> p k n", k=KC)
        cT = [w[:].rearrange("p c n -> p (c n)")[:, 0:KC * CROWS].rearrange("p (k n) -> p k n", k=KC) for w in W]
        stage = [qn[:].rearrange("p t n -> p (t n)"), hf[:].rearrange("p t n -> p (t n)")]
        z = [w[:].rearrange("p a n -> p (a n)").rearrange("p (b k n) -> p b k n", b=NB, k=KC) for w in w_io]
        EW = 3 * D
        e_raw = [stage[0][:, s * EW:(s + 1) * EW] for s in range(2)]
        e_w = [[w[:].rearrange("p c n -> p (c n)")[:, (s % 2) * EW:(s % 2 + 1) * EW] for w in (qnT, W)[s // 2]] for s in range(4)]
        hT = [w[:].rearrange("p c n -> p (c n)").rearrange("p (s n) -> p s n", s=4) for w in h]
        sT = part(0, 4)
        C_all = part(4)[:, 0:NT * E].rearrange("p (e t) -> p e t", e=E)
        score = part(5)[:, 0:256].rearrange("p (t e) -> p t e", e=E)
        biased = part(5)[:, 256:512].rearrange("p (t e) -> p t e", e=E)
        rank = part(6)[:, 0:256].rearrange("p (t e) -> p t e", e=E)
        cmp = part(6)[:, 256:512].rearrange("p (t e) -> p t e", e=E)
        hi2 = part(7)[:, 0:128].rearrange("p (t g a) -> p t g a", g=GROUPS, a=2)
        lo2 = part(7)[:, 128:256].rearrange("p (t g a) -> p t g a", g=GROUPS, a=2)
        gs = part(7)[:, 256:320].rearrange("p (t g) -> p t g", g=GROUPS)
        g_b = part(7)[:, 320:384].rearrange("p (t g) -> p t g", g=GROUPS)
        grank = part(7)[:, 384:448].rearrange("p (t g) -> p t g", g=GROUPS)
        gcmp = part(7)[:, 448:512].rearrange("p (t g) -> p t g", g=GROUPS)
        wsum = part(8)[:, 0:NT]
        winv = part(8)[:, NT:2 * NT]
        c_now = [part(8)[:, (2 + s) * NT:(3 + s) * NT] for s in range(2)]

        bank = [ctx.enter_context(nc.psum_tensor(f"bank{i}", [P, 2, 512], F32)) for i in range(4)]

        def bk(i):
            return bank[i // 2][:, i % 2, :]

        def bk2(i):
            return bank[i // 2][:].rearrange("p a n -> p (a n)")
        ring = [bk(4 + i) for i in range(4)]

        ctx_loaded = sem("ctx_loaded")
        small_in = sem("small_in")
        x_in = sem("x_in")
        stage_in = [sem(f"stage_in{i}") for i in range(2)]
        ident_zero = sem("ident_zero")
        ident_made = sem("ident_made")
        c_stats = sem("c_stats")
        c_part = sem("c_part")
        c_rstd = sem("c_rstd")
        c_norm = sem("c_norm")
        cT_raw = sem("cT_raw")
        cTf_made = sem("cTf_made")
        cT_hi = sem("cT_hi")
        cT_split = sem("cT_split")
        w_hi = sem("w_hi")
        w_split = sem("w_split")
        rw_split = sem("rw_split")
        k_raw = sem("k_raw")
        v_raw = sem("v_raw")
        m_raw = sem("m_raw")
        k_sq = sem("k_sq")
        k_ss = sem("k_ss")
        k_rs = sem("k_rs")
        kn_made = sem("kn_made")
        v_made = sem("v_made")
        kv_made = sem("kv_made")
        p_chain = sem("p_chain")
        d_chain = sem("d_chain")
        x_stats = sem("x_stats")
        x_rstd = sem("x_rstd")
        Q_made = sem("Q_made")
        q_stats = sem("q_stats")
        Qn0_made = sem("Qn0_made")
        Qb_made = sem("Qb_made")
        acc_b2 = sem("acc_b2")
        a_raw = sem("a_raw")
        QnTf_made = sem("QnTf_made")
        QnT_hi = sem("QnT_hi")
        QnT_split = sem("QnT_split")
        q_raw = sem("q_raw")
        q_sq = sem("q_sq")
        q_ss = sem("q_ss")
        q_rs = sem("q_rs")
        qn_made = sem("qn_made")
        qnT_raw = sem("qnT_raw")
        qnT_hi = sem("qnT_hi")
        qnT_split = sem("qnT_split")
        kvd_zero = sem("kvd_zero")
        kvd_hi = sem("kvd_hi")
        kvd_split = sem("kvd_split")
        w_raw = sem("w_raw")
        W_hi = sem("W_hi")
        W_split = sem("W_split")
        attn_raw = sem("attn_raw")
        x1_made = sem("x1_made")
        x1_stats = sem("x1_stats")
        xn0_made = sem("xn0_made")
        acc_x1 = sem("acc_x1")
        x1_rstd = sem("x1_rstd")
        q2_rstd = sem("q2_rstd")
        xnT_raw = sem("xnT_raw")
        xnTf_made = sem("xnTf_made")
        xnT_hi = sem("xnT_hi")
        xnT_split = sem("xnT_split")
        mlp_raw = sem("mlp_raw")
        gelu = sem("gelu")
        h_hi = sem("h_hi")
        h_split = sem("h_split")
        y_raw = sem("y_raw")
        x3_made = sem("x3_made")
        x3_stats = sem("x3_stats")
        x3_rstd = sem("x3_rstd")
        z0_made = sem("z0_made")
        z_raw = sem("z_raw")
        zT_made = sem("zT_made")
        z_hi = sem("z_hi")
        z_split = sem("z_split")
        e_in = [sem(f"e_in{i}") for i in range(2)]
        e_hi = sem("e_hi")
        e_split = sem("e_split")
        router_raw = sem("router_raw")
        sig_made = sem("sig_made")
        scoreT_raw = sem("scoreT_raw")
        score_made = sem("score_made")
        c_made = sem("c_made")
        c_copied = sem("c_copied")
        r_chain = sem("r_chain")
        g_raw = sem("g_raw")
        u_raw = sem("u_raw")
        silu = sem("silu")
        hf_made = sem("hf_made")
        hT_hi = sem("hT_hi")
        hT_split = sem("hT_split")
        dn_raw = sem("dn_raw")
        y_added = sem("y_added")
        out_done = sem("out_done")

        def split_lo(eng, out_lo, full, hi):
            return eng.tensor_tensor(out_lo, full, hi.bitcast(F32), ALU.subtract)

        def passes(pair_l, pair_r):
            return ((pair_l[0], pair_r[0]), (pair_l[0], pair_r[1]), (pair_l[1], pair_r[0]))

        def over_batches(eng, step):
            for b in (-2, -1, 0, 1):
                step(Batch(b))
            if LOOP_BATCHES:
                with eng.Fori(0, (NB - 4) // 2) as i:
                    step(Batch(2, i))
                    step(Batch(3, i))
            else:
                for b in range(2, NB - 2):
                    step(Batch(b))
            for b in (NB - 2, NB - 1, NB, NB + 1):
                step(Batch(b))

        def live(b):
            return b.register is not None or 0 <= b.offset < NB

        block = ctx.enter_context(nc.Block())

        @block.sync
        def _(sp):
            sp.dma_start(c0[:, 0:CT - 1, :], ctx_v[0:(CT - 1) * P, :].rearrange("(c p) d -> p c d", p=P)).then_inc(ctx_loaded, 16)
            sp.dma_start(c0[0:CLAST, CT - 1, :], ctx_v[(CT - 1) * P:CROWS, :]).then_inc(ctx_loaded, 16)
            sp.dma_start(cols[:], columns).then_inc(small_in, 16)
            for n, (w, kc) in enumerate(((wk, KC), (wv, KC), (wq, KC), (w1, KC), (wo, IC), (w2, MC))):
                if n > 1:
                    sp.wait_ge(w_split, n - 1)
                sp.dma_start(stage[n % 2].rearrange("p (k n) -> p k n", k=kc),
                             w.rearrange("(k p) n -> p k n", p=P)).then_inc(stage_in[n % 2], 16)
                if n == 1:
                    for b in range(0, NB, 2):
                        sp.dma_start(acc[:, b:b + 2, :].rearrange("p b (t d) -> p b t d", t=TT),
                                     x_v[:, b:b + 2]).then_inc(x_in, 16)
            sp.wait_ge(qnT_raw, 4 * NB)
            for n in range(SH):
                sp.dma_start(e_raw[n % 2], experts[n]).then_inc(e_in[n % 2], 16)
            with sp.Fori(0, E // 2) as i:
                for s in range(2):
                    sp.wait_ge(e_split, i * 2 + (s + 1))
                    sp.dma_start(e_raw[s], experts[i * 2 + (SH + s)]).then_inc(e_in[s], 16)
            for tb in range(TB):
                sp.wait_ge(y_added, TB + E * TB - TB + tb + 1)
                sp.dma_start(out_v[:, BB * tb:BB * (tb + 1)],
                             acc[:, BB * tb:BB * (tb + 1), :].rearrange("p b (t d) -> p b t d", t=TT)).then_inc(out_done, 16)
            sp.wait_ge(out_done, 16 * TB)

        @block.tensor
        def _(pe):
            def product(out_, lhs, rhs, chunks):
                for n, c in enumerate(chunks):
                    for m, (a, b) in enumerate(passes(lhs(c), rhs(c))):
                        last = pe.matmul(out_, a, b, start=(n == 0 and m == 0), stop=(n == len(chunks) - 1 and m == 2))
                return last

            pe.wait_ge(ident_made, 1)
            for c in range(CT):
                pe.wait_ge(c_norm, c + 1)
                r = P if c < CT - 1 else CLAST
                for k in range(KC):
                    last = pe.transpose(bk2(2 * k)[:, c * P:c * P + r], c0[0:r, c, k * P:(k + 1) * P], ident[0:r, 0:r])
            last.then_inc(cT_raw, 1)

            def keys(b):
                if b > 1:
                    pe.wait_ge(kn_made, b - 1)
                for n in range(2):
                    product(bk(2 * (b % 2) + n)[0:NK, :], lambda k: [t[:, k, b * NK:(b + 1) * NK] for t in cT],
                            lambda k: [t[:, k, n * 512:(n + 1) * 512] for t in wk_s], range(KC)).then_inc(k_raw, 1)

            def values(b):
                if b:
                    pe.wait_ge(v_made, b)
                for n in range(2):
                    product(bk(4 + n)[0:NK, :], lambda k: [t[:, k, b * NK:(b + 1) * NK] for t in cT],
                            lambda k: [t[:, k, n * 512:(n + 1) * 512] for t in wv_s], range(KC)).then_inc(v_raw, 1)

            def values_keys(b):
                pe.wait_ge(kn_made, b + 1)
                pe.wait_ge(v_made, b + 1)
                if b:
                    pe.wait_ge(kv_made, b)
                for c in range(IC):
                    last = pe.matmul(bk2(6)[:, c * P:(c + 1) * P], vc[0:NK, c * P:(c + 1) * P],
                                     kn[0:NK, c * P:(c + 1) * P], start=True, stop=True)
                last.then_inc(m_raw, 1)

            pe.wait_ge(cT_split, 1)
            pe.wait_ge(w_split, 1)
            for b in range(NB):
                keys(b)
                if b:
                    values_keys(b - 1)
                if b == 0:
                    pe.wait_ge(w_split, 2)
                values(b)
            values_keys(NB - 1)

            def q_transposes(b, t):
                pe.wait_ge(qn_made, b.count(TT, t + 1))
                for j in range(2 * t, 2 * t + 2):
                    pe.wait_ge(W_split, b.count(4, j + 1))
                    for c in range(4):
                        last = pe.transpose(ring[j][:, c * P:(c + 1) * P],
                                            qn[:, t, (4 * (j % 2) + c) * P:(4 * (j % 2) + c + 1) * P], ident[:])
                    last.then_inc(qnT_raw, 1)

            def mlp_up(b):
                pe.wait_ge(xnT_split, b.count(1, 1))
                for j in range(4):
                    if live(b + 1):
                        pe.wait_ge(qnT_split, (b + 1).count(4, j + 1))
                    elif j == 0:
                        pe.wait_ge(zT_made, NB - 2)
                    elif j == 2:
                        pe.wait_ge(x3_made, NB - 1)
                    for c in range(2 * j, 2 * j + 2):
                        last = product(ring[j][:, (c % 2) * NQ:(c % 2 + 1) * NQ],
                                       lambda k: [t[:, k, c * P:(c + 1) * P] for t in w1_s],
                                       lambda k: [t[:, k, :] for t in xnT], range(KC))
                    last.then_inc(mlp_raw, 1)

            def first_transposes(b):
                pe.wait_ge(Qn0_made, b.count(1, 1))
                if not live(b + -1):
                    pe.wait_ge(kn_made, NB)
                for k in range(KC):
                    for t in range(TT):
                        last = pe.transpose(bk(0)[:, k * NQ + t * P:k * NQ + (t + 1) * P],
                                            Qn0[:, t * D + k * P:t * D + (k + 1) * P], ident[:])
                last.then_inc(a_raw, 1)

            def last_transposes(b):
                pe.wait_ge(z0_made, b.count(1, 1))
                pe.wait_ge(gelu, b.count(4, 5) if live(b + 1) else 4 * NB)
                if not live(b + 1):
                    pe.wait_ge(zT_made, NB - 1)
                for k in range(KC):
                    for t in range(TT):
                        last = pe.transpose(ring[0][:, k * NQ + t * P:k * NQ + (t + 1) * P],
                                            z0[:, t * D + k * P:t * D + (k + 1) * P], ident[:])
                last.then_inc(z_raw, 1)

            def attend(b):
                pe.wait_ge(qnT_split, b.count(4, 4))
                if live(b + -1):
                    pe.wait_ge(gelu, b.count(4, -2))
                for t in range(TT):
                    last = product(ring[1][:, t * D:(t + 1) * D], lambda c: [u[:, c, t * P:(t + 1) * P] for u in qnT],
                                   lambda c: [u[:, c, :] for u in W], range(IC))
                last.then_inc(attn_raw, 1)

            def queries(b):
                pe.wait_ge(QnT_split, b.count(1, 1))
                if not live(b + -1):
                    pe.wait_ge(w_split, 3)
                for t in range(TT):
                    for n in range(2):
                        last = product(bk(2 * t + n), lambda k: [u[:, k, t * P:(t + 1) * P] for u in QnT],
                                       lambda k: [u[:, k, n * 512:(n + 1) * 512] for u in wq_s], range(KC))
                    last.then_inc(q_raw, 1)

            def mlp_down(b):
                pe.wait_ge(gelu, b.count(4, 3))
                for t in range(TT):
                    for j in range(4):
                        if t == 0:
                            pe.wait_ge(h_split, b.count(4, j + 1))
                        for c in range(2 * j, 2 * j + 2):
                            for m, (a, w) in enumerate(passes([u[:, c, t * P:(t + 1) * P] for u in h], [u[:, c, :] for u in w2_s])):
                                last = pe.matmul(ring[2][:, t * D:(t + 1) * D], a, w, start=(c == 0 and m == 0),
                                                 stop=(c == MC - 1 and m == 2))
                last.then_inc(y_raw, 1)

            def middle_transposes(b):
                pe.wait_ge(xn0_made, b.count(1, 1))
                if live(b + -1):
                    pe.wait_ge(gelu, b.count(4, 0))
                for k in range(KC):
                    for t in range(TT):
                        last = pe.transpose(ring[3][:, k * NQ + t * P:k * NQ + (t + 1) * P],
                                            xn0[:, t * D + k * P:t * D + (k + 1) * P], ident[:])
                last.then_inc(xnT_raw, 1)

            def fold_wo(b):
                pe.wait_ge(kvd_split, b.count(1, 1))
                if not live(b + -1):
                    pe.wait_ge(w_split, 5)
                    pe.wait_ge(kv_made, NB)
                for j in range(4):
                    if live(b + -1):
                        if j == 0 and live(b + -3):
                            pe.wait_ge(zT_made, (b + -3).count(1, 1))
                        if j == 1:
                            pe.wait_ge(x1_made, (b + -1).count(1, 1))
                        if j == 2 and live(b + -2):
                            pe.wait_ge(x3_made, (b + -2).count(1, 1))
                        if j == 3:
                            pe.wait_ge(xnTf_made, (b + -1).count(1, 1))
                    for c in range(2 * j, 2 * j + 2):
                        last = product(ring[j][:, (c % 2) * D:(c % 2 + 1) * D], lambda c_: [u[:, c_, :] for u in kvd],
                                       lambda c_: [u[:, c_, :] for u in wo_s], [c])
                    last.then_inc(w_raw, 1)

            def step(b):
                if live(b):
                    q_transposes(b, 0)
                    q_transposes(b, 1)
                if live(b + -1):
                    if b.register is None and b.offset == 1:
                        pe.wait_ge(w_split, 6)
                    mlp_up(b + -1)
                if live(b + 1):
                    first_transposes(b + 1)
                if live(b + -2):
                    last_transposes(b + -2)
                if live(b):
                    attend(b)
                if live(b + 1):
                    queries(b + 1)
                if live(b + -1):
                    mlp_down(b + -1)
                if live(b):
                    middle_transposes(b)
                if live(b + 1):
                    fold_wo(b + 1)
            over_batches(pe, step)

            pe.wait_ge(rw_split, 1)
            pe.wait_ge(zT_made, NB)
            for tb in range(TB):
                pe.wait_ge(z_split, tb + 1)
                product(ring[tb][0:E, :], lambda k: [u[:, k, :] for u in rw],
                        lambda k: [u[:, BB * tb:BB * (tb + 1), k, :] for u in z], range(KC)).then_inc(router_raw, 1)

            def up(u, wait_w):
                if wait_w is not None:
                    pe.wait_ge(e_split, wait_w)
                if u.register is not None or u.offset > 1:
                    pe.wait_ge(hf_made, u(-1))
                for m, done in ((0, g_raw), (1, u_raw)):
                    product(bk(2 * u.parity + m),
                            lambda k: [w[:, m * D + k * P:m * D + (k + 1) * P] for w in e_w[u.slot]],
                            lambda k: [v[:, BB * u.tb:BB * (u.tb + 1), k, :] for v in z], range(KC)).then_inc(done, 1)

            def down(d, slots, tb):
                pe.wait_ge(hT_split, d.units)
                if d.register is not None or d.offset > 1:
                    pe.wait_ge(y_added, d.count(-1))
                for t in range(TPB):
                    last = product(bk2(4 + 2 * (tb % 2))[:, t * D:(t + 1) * D],
                                   lambda i: [w[:, i[1], t * P:(t + 1) * P] for w in hT],
                                   lambda i: [w[:, 2 * D:3 * D] for w in e_w[i[0]]], slots)
                last.then_inc(dn_raw, 1)

            class Unit:

                def __init__(self, offset, slot, tb, register):
                    self.offset, self.slot, self.tb, self.register = offset, slot, tb, register
                    self.parity = offset % 2

                def __call__(self, n):
                    value = self.offset + n
                    return value if self.register is None else self.register * (2 * TB) + value

            class Down:
                def __init__(self, offset, units, register=None):
                    self.offset, self.register, self._units = offset, register, units

                @property
                def units(self):
                    return self._units if self.register is None else self.register * (2 * TB) + self._units

                def count(self, n):
                    value = self.offset + n
                    return value if self.register is None else self.register * (2 * TB) + value

            for tb in range(TB):
                for s in range(SH):
                    up(Unit(SH * tb + s, 2 + s, tb, None), s + 1 if tb == 0 else None)
                if tb == 0:
                    for t in range(NT):
                        pe.wait_ge(sig_made, t // TPB + 1)
                        last = pe.transpose(ring[0][:, t * E:(t + 1) * E], sT[0:E, t * P:(t + 1) * P], ident[0:E, 0:E])
                    last.then_inc(scoreT_raw, 1)
                    pe.wait_ge(score_made, 1)
                if tb:
                    down(Down(tb - 1, SH * tb), [(2 + s, (SH * (tb - 1) + s) % 4) for s in range(SH)], tb - 1)

            def expert(s, first, register):
                for tb in range(TB):
                    o = SH * TB + TB * s + tb
                    up(Unit(o, s, tb, register),
                       None if tb else (SH + 1 + s if register is None else register * 2 + (SH + 1 + s)))
                    if first and tb == 0:
                        down(Down(TB - 1, SH * TB), [(2 + n, (SH * (TB - 1) + n) % 4) for n in range(SH)], TB - 1)
                    else:
                        p = (o - 1) % (2 * TB)
                        down(Down(TB + (o - 1 - SH * TB), o, register), [(p // TB, (o - 1) % 4)], p % TB)
            assert SH * TB % (2 * TB) == 0
            expert(0, True, None)
            expert(1, False, None)
            with pe.Fori(1, E // 2) as i:
                expert(0, False, i)
                expert(1, False, i)
            o = SH * TB + E * TB
            down(Down(TB + E * TB - 1, o), [(1, (o - 1) % 4)], TB - 1)

        @block.scalar
        def _(act):
            act.dma_start(rowsb[:], rows.broadcast_to([P, rows.shape[1]])).then_inc(small_in, 16)
            act.dma_start(rwf[:], router_t.rearrange("(k p) e -> p k e", p=P)).then_inc(small_in, 16)

            act.wait_ge(small_in, 48)
            act.wait_ge(cT_raw, 1)
            for k in range(KC):
                act.activation(cTf[:, k, :], bk2(2 * k)[:, 0:CROWS], ACT.Identity,
                               bias=b1l[:, k:k + 1], scale=g1[:, k:k + 1]).then_inc(cTf_made, 1)

            def weight_hi(n, dst):
                act.wait_ge(stage_in[n % 2], 16 * (n // 2 + 1))
                act.activation(dst, stage[n % 2], ACT.Copy).then_inc(w_hi, 1)

            flat = [w[:].rearrange("p c n -> p (c n)") for w in (qnT[0], h[0])]
            flat += [w_io[0][:, 0, :], w_mlp[0][:, 0, :], w_io[0][:, 1, :], w_mlp[0][:, 1, :]]
            weight_hi(0, flat[0])
            weight_hi(1, flat[1])

            def kv_out(b):
                act.wait_ge(m_raw, b + 1)
                act.wait_ge(cT_split, 1)
                m = bk2(6).rearrange("p (c d) -> p c d", c=IC)
                for s in (0, HEAD):
                    last = act.activation(kv_z[s:s + HEAD, b, :].rearrange("p (c d) -> p c d", c=IC),
                                          m[s:s + HEAD, :, s:s + HEAD], ACT.Copy)
                last.then_inc(kv_made, 1)

            for b in range(NB):
                act.wait_ge(k_raw, 2 * (b + 1))
                if b:
                    act.wait_ge(k_ss, b)
                act.activation(sq[0:NK, :], bk2(2 * (b % 2))[0:NK, :], ACT.Square).then_inc(k_sq, 1)
                act.wait_ge(v_raw, 2 * (b + 1))
                if b:
                    act.wait_ge(m_raw, b)
                act.activation(vc[0:NK, :], bk2(4)[0:NK, :], ACT.Copy).then_inc(v_made, 1)
                if b:
                    kv_out(b - 1)
                if b in (1, 2, 3, 4):
                    weight_hi(b + 1, flat[b + 1])
            kv_out(NB - 1)

            def step(b):
                if live(b):
                    for j in range(4):
                        act.wait_ge(qnT_raw, b.count(4, j + 1))
                        if b.register is None and b.offset == 0 and j == 0:
                            act.wait_ge(k_raw, 2 * NB)
                        t = j // 2
                        act.activation(qnT[0][:, 4 * (j % 2):4 * (j % 2) + 4, t * P:(t + 1) * P],
                                       ring[j].rearrange("p (c n) -> p c n", c=4), ACT.Copy).then_inc(qnT_hi, 1)
                if live(b + -1):
                    a = b + -1
                    for j in range(4):
                        act.wait_ge(mlp_raw, a.count(4, j + 1))
                        if a.register is not None or a.offset:
                            act.wait_ge(h_split, a.count(4, j - 3))
                        for c in range(2 * j, 2 * j + 2):
                            last = act.activation(hf[:, j, (c % 2) * NQ:(c % 2 + 1) * NQ], ring[j][:, (c % 2) * NQ:(c % 2 + 1) * NQ],
                                                  ACT.Gelu, bias=b1c[:, c:c + 1])
                        last.then_inc(gelu, 1)
                if live(b + 1):
                    a = b + 1
                    act.wait_ge(a_raw, a.count(1, 1))
                    if not a.first:
                        act.wait_ge(QnT_split, a.count(1, 0))
                    for k in range(KC):
                        last = act.activation(QnTf[:, k * NQ:(k + 1) * NQ], bk(0)[:, k * NQ:(k + 1) * NQ], ACT.Identity,
                                              bias=b1l[:, k:k + 1], scale=g1[:, k:k + 1])
                    last.then_inc(QnTf_made, 1)
                    if a.register is None and a.offset == 0:
                        act.wait_ge(kvd_zero, 1)
                        act.wait_ge(kv_made, NB)
                    if not a.first:
                        act.wait_ge(w_raw, a.count(4, 0))
                    for s in (0, HEAD):
                        last = act.activation(kvd[0][s:s + HEAD, :, s:s + HEAD],
                                              kv_z[s:s + HEAD, a.index, :].rearrange("p (c d) -> p c d", c=IC), ACT.Copy)
                    last.then_inc(kvd_hi, 1)
                if live(b + -2):
                    a = b + -2
                    act.wait_ge(z_raw, a.count(1, 1))
                    act.wait_ge(kvd_split, a.count(1, 1))
                    act.activation(kv_z[:, a.index, :], ring[0], ACT.Copy).then_inc(zT_made, 1)
                if live(b + 1):
                    a = b + 1
                    for t in range(TT):
                        act.wait_ge(q_raw, a.count(TT, t + 1))
                        if a.register is None and a.offset == 0 and t == 0:
                            act.wait_ge(k_ss, NB)
                        if t or not a.first:
                            act.wait_ge(q_ss, a.count(TT, t))
                        act.activation(sq[:], bk2(2 * t), ACT.Square).then_inc(q_sq, 1)
                if live(b):
                    act.wait_ge(xnT_raw, b.count(1, 1))
                    if not b.first:
                        act.wait_ge(xnT_split, b.count(1, 0))
                    for k in range(KC):
                        last = act.activation(xnTf[:, k * NQ:(k + 1) * NQ], ring[3][:, k * NQ:(k + 1) * NQ], ACT.Identity,
                                              bias=b2l[:, k:k + 1], scale=g2[:, k:k + 1])
                    last.then_inc(xnTf_made, 1)
                if live(b + 1):
                    a = b + 1
                    for j in range(4):
                        act.wait_ge(w_raw, a.count(4, j + 1))
                        act.activation(W[0][:, 2 * j:2 * j + 2, :].rearrange("p c n -> p (c n)"), ring[j],
                                       ACT.Copy).then_inc(W_hi, 1)
            over_batches(act, step)

            def unit(o, register=None):
                def n(k):
                    return o + k if register is None else register * (2 * TB) + (o + k)
                act.wait_ge(g_raw, n(1))
                if register is not None or o > 1:
                    act.wait_ge(hf_made, n(-1))
                act.activation(sq[:, (o % 2) * BLK:(o % 2 + 1) * BLK], bk(2 * (o % 2)), ACT.Silu).then_inc(silu, 1)
                act.wait_ge(hf_made, n(1))
                if register is None and o < SH * TB + 4:
                    if o > 3:
                        act.wait_ge(dn_raw, o // SH - 1)
                else:
                    act.wait_ge(dn_raw, n(TB - SH * TB - 3))
                act.activation(hT[0][:, o % 4, :], hf[:, o % 4, :], ACT.Copy).then_inc(hT_hi, 1)
            def expert_hi(n, register=None):
                if register is None:
                    act.wait_ge(e_in[n % 2], 16 * (n // 2 + 1))
                    if n > 3:
                        act.wait_ge(dn_raw, TB * (n - 2) if n >= 4 else 0)
                else:
                    act.wait_ge(e_in[n % 2], register * 16 + 16 * (n // 2 + 1))
                    act.wait_ge(dn_raw, register * (2 * TB) + TB * (n - 2))
                dst = e_w[2 + n if n < SH and register is None else n % 2][0]
                act.activation(dst, e_raw[n % 2], ACT.Copy).then_inc(e_hi, 1)

            act.wait_ge(attn_raw, NB)
            for n in range(2 * SH):
                expert_hi(n)
            for tb in range(TB):
                act.wait_ge(zT_made, BB * (tb + 1))
                act.activation(z[0][:, BB * tb:BB * (tb + 1)].rearrange("p b k n -> p (b k n)"),
                               kvf[:, BB * tb * 512:BB * (tb + 1) * 512], ACT.Copy).then_inc(z_hi, 1)
            for tb in range(TB):
                act.wait_ge(router_raw, tb + 1)
                act.activation(sT[0:E, tb * BLK:(tb + 1) * BLK], ring[tb][0:E, :], ACT.Sigmoid).then_inc(sig_made, 1)

            def expert_pair(register):
                for o in range(SH * TB, SH * TB + 2 * TB):
                    unit(o, register)
                    if o % TB == 1:
                        s = (o - SH * TB) // TB
                        expert_hi(3 + s, register)
            for o in range(SH * TB + TB):
                unit(o)
            for o in range(SH * TB + TB, SH * TB + 2 * TB):
                unit(o)
                if o % TB == 1:
                    expert_hi(4)
            with act.Fori(1, E // 2 - 1) as i:
                expert_pair(i)
            last_pair = SH * TB + (E - 2) * TB
            for o in range(last_pair, last_pair + 2 * TB):
                unit(o)
                if o == last_pair + 1:
                    expert_hi(E + 1)

        @block.vector
        def _(dve):
            dve.wait_ge(ctx_loaded, 32)
            for c in range(CT):
                r = P if c < CT - 1 else CLAST
                dve.bn_stats(stat[0:r, c, :], c0[0:r, c, :]).then_inc(c_part, 1)
            dve.wait_ge(c_part, CT)
            for c in range(CT):
                r = P if c < CT - 1 else CLAST
                last = dve.bn_aggr(mv[0:r, c, :], stat[0:r, c, :])
            last.then_inc(c_stats, 1)
            dve.wait_ge(c_rstd, 1)
            for c in range(CT):
                r = P if c < CT - 1 else CLAST
                dve.tensor_scalar(c0[0:r, c, :], c0[0:r, c, :], mv[0:r, c, 0:1], rs_c[0:r, c:c + 1],
                                  ALU.subtract, ALU.mult).then_inc(c_norm, 1)
            dve.wait_ge(cTf_made, KC)
            for k in range(KC):
                dve.tensor_copy(cT[0][:, k, :], cTf[:, k, :]).then_inc(cT_hi, 1)
            dve.wait_ge(cT_hi, KC)
            split_lo(dve, cT[1], cTf, cT[0]).then_inc(cT_split, 1)

            def weight_lo(n, lo, hi):
                dve.wait_ge(w_hi, n + 1)
                split_lo(dve, lo, stage[n % 2], hi).then_inc(w_split, 1)
            flat = [[w[:].rearrange("p c n -> p (c n)") for w in v] for v in (qnT, h)]
            flat += [[w[:, i, :] for w in v] for i, v in ((0, w_io), (0, w_mlp), (1, w_io), (1, w_mlp))]
            weight_lo(0, flat[0][1], flat[0][0])
            weight_lo(1, flat[1][1], flat[1][0])
            dve.wait_ge(small_in, 48)
            dve.tensor_copy(rw[0][:], rwf[:]).then_inc(rw_split, 1)
            dve.wait_ge(rw_split, 1)
            split_lo(dve, rw[1][:], rwf[:], rw[0][:]).then_inc(rw_split, 1)

            def heads(a):
                return a.rearrange("p (h d) -> p h d", h=NH)

            def stats_x(b):
                if b.register is None:
                    dve.wait_ge(x_in, 16 * (b.offset // 2 + 1))
                else:
                    dve.wait_ge(x_in, 16 * (NB // 2))
                for t in range(TT):
                    dve.bn_stats(st_x[:, t, :], acc[:, b.index, t * D:(t + 1) * D]).then_inc(d_chain, 1)

            def finish_stats(at, st, mv_):
                dve.wait_ge(d_chain, at)
                for t in range(TT):
                    last = dve.bn_aggr(mv_[:, t, :], st[:, t, :])
                return last

            for b in range(NB):
                dve.wait_ge(k_sq, b + 1)
                dve.tensor_reduce(ss[0:NK, 0, :], heads(sq[0:NK, :]), AX.X, ALU.add).then_inc(k_ss, 1)
                if b in (1, 2, 3, 4):
                    weight_lo(b + 1, flat[b + 1][1], flat[b + 1][0])
                dve.wait_ge(k_rs, b + 1)
                if b:
                    dve.wait_ge(m_raw, b)
                dve.tensor_tensor(heads(kn[0:NK, :]), heads(bk2(2 * (b % 2))[0:NK, :]),
                                  rs_n[0:NK, 0, :].unsqueeze(2).broadcast_to([NK, NH, HEAD]), ALU.mult).then_inc(kn_made, 1)

            def step(b):
                def links(kind):
                    def batches(first, last):
                        return 2 * max(0, min(NB, last) - max(0, first))
                    o = b.offset
                    total = batches(0, o + 2) + batches(0, o) + batches(0, o + 2) + batches(0, o - 1)
                    order = ["x", "x1", "Q", "x3"]
                    lives = {"x": o + 2, "x1": o, "Q": o + 2, "x3": o - 1}
                    for n in order:
                        if 0 <= lives[n] < NB:
                            total += 2
                        if n == kind:
                            break
                    return total if b.register is None else b.register * 16 + total

                if live(b):
                    for j in range(4):
                        t = j // 2
                        dve.wait_ge(qnT_hi, b.count(4, j + 1))
                        sl = [u[:, 4 * (j % 2):4 * (j % 2) + 4, t * P:(t + 1) * P] for u in qnT]
                        split_lo(dve, sl[1], ring[j].rearrange("p (c n) -> p c n", c=4), sl[0]).then_inc(qnT_split, 1)
                if live(b + -1):
                    a = b + -1
                    for j in range(5):
                        if j < 4:
                            dve.wait_ge(gelu, a.count(4, j + 1))
                            dve.tensor_copy(h[0][:, 2 * j:2 * j + 2, :].rearrange("p c n -> p (c n)"),
                                            hf[:, j, :]).then_inc(h_hi, 1)
                        if j:
                            dve.wait_ge(h_hi, a.count(4, j))
                            sl = [u[:, 2 * j - 2:2 * j, :].rearrange("p c n -> p (c n)") for u in h]
                            split_lo(dve, sl[1], hf[:, j - 1, :], sl[0]).then_inc(h_split, 1)
                if live(b + 2):
                    stats_x(b + 2)
                if live(b + 1):
                    a = b + 1
                    dve.wait_ge(QnTf_made, a.count(1, 1))
                    u = [w[:].rearrange("p k n -> p (k n)") for w in QnT]
                    dve.tensor_copy(u[0], QnTf).then_inc(QnT_hi, 1)
                if live(b + 2):
                    finish_stats(links("x"), st_x, mv_x).then_inc(x_stats, 1)
                if live(b + 1):
                    dve.wait_ge(QnT_hi, a.count(1, 1))
                    split_lo(dve, u[1], QnTf, u[0]).then_inc(QnT_split, 1)
                if live(b + 1):
                    a = b + 1
                    dve.wait_ge(kvd_hi, a.count(1, 1))
                    for s in (0, HEAD):
                        last = split_lo(dve, kvd[1][s:s + HEAD, :, s:s + HEAD],
                                        kv_z[s:s + HEAD, a.index, :].rearrange("p (c d) -> p c d", c=IC),
                                        kvd[0][s:s + HEAD, :, s:s + HEAD])
                    last.then_inc(kvd_split, 1)
                if live(b):
                    dve.wait_ge(attn_raw, b.count(1, 1))
                    dve.wait_ge(Qb_made, b.count(1, 1))
                    if b.offset > 1:
                        dve.wait_ge(acc_x1, b.count(1, -1))
                    dve.tensor_tensor(x1[b.parity], ring[1], Q[b.parity], ALU.add).then_inc(x1_made, 1)
                    dve.wait_ge(x1_made, b.count(1, 1))
                    for t in range(TT):
                        dve.bn_stats(st_1[:, t, :], x1[b.parity][:, t * D:(t + 1) * D]).then_inc(d_chain, 1)
                    finish_stats(links("x1"), st_1, mv_1).then_inc(x1_stats, 1)
                if live(b + 2):
                    a = b + 2
                    dve.wait_ge(x_rstd, a.count(1, 1))
                    for t in range(TT):
                        last = dve.tensor_scalar(Q[a.parity][:, t * D:(t + 1) * D], acc[:, a.index, t * D:(t + 1) * D],
                                                 mv_x[:, t, 0:1], rs_x[:, t:t + 1], ALU.subtract, ALU.mult)
                    last.then_inc(Q_made, 1)
                if live(b + 1):
                    a = b + 1
                    for t in range(TT):
                        dve.wait_ge(q_sq, a.count(TT, t + 1))
                        dve.tensor_reduce(ss[:, t, :], heads(sq[:]), AX.X, ALU.add).then_inc(q_ss, 1)
                if live(b + 2):
                    a = b + 2
                    dve.wait_ge(Q_made, a.count(1, 1))
                    for t in range(TT):
                        dve.bn_stats(st_q[:, t, :], Q[a.parity][:, t * D:(t + 1) * D]).then_inc(d_chain, 1)
                    finish_stats(links("Q"), st_q, mv_q).then_inc(q_stats, 1)
                if live(b + 1):
                    a = b + 1
                    for t in range(TT):
                        dve.wait_ge(q_rs, a.count(TT, t + 1))
                        if not a.first:
                            dve.wait_ge(qnT_raw, a.count(4, 0))
                        if a.register is None and a.offset == 0 and t == 0:
                            dve.wait_ge(w_split, 6)
                        dve.tensor_tensor(heads(qn[:, t, :]), heads(bk2(2 * t)),
                                          rs_n[:, t, :].unsqueeze(2).broadcast_to([P, NH, HEAD]), ALU.mult).then_inc(qn_made, 1)
                if live(b + -1):
                    a = b + -1
                    dve.wait_ge(y_raw, a.count(1, 1))
                    dve.wait_ge(acc_x1, a.count(1, 1))
                    dve.tensor_tensor(acc[:, a.index, :], ring[2], acc[:, a.index, :], ALU.add).then_inc(x3_made, 1)
                    dve.wait_ge(x3_made, a.count(1, 1))
                    for t in range(TT):
                        dve.bn_stats(st_3[:, t, :], acc[:, a.index, t * D:(t + 1) * D]).then_inc(d_chain, 1)
                    finish_stats(links("x3"), st_3, mv_3).then_inc(x3_stats, 1)
                if live(b):
                    dve.wait_ge(xnTf_made, b.count(1, 1))
                    u = [w[:].rearrange("p k n -> p (k n)") for w in xnT]
                    dve.tensor_copy(u[0], xnTf).then_inc(xnT_hi, 1)
                    dve.wait_ge(xnT_hi, b.count(1, 1))
                    split_lo(dve, u[1], xnTf, u[0]).then_inc(xnT_split, 1)
                if live(b + 1):
                    a = b + 1
                    for j in range(4):
                        dve.wait_ge(W_hi, a.count(4, j + 1))
                        sl = [u_[:, 2 * j:2 * j + 2, :].rearrange("p c n -> p (c n)") for u_ in W]
                        split_lo(dve, sl[1], ring[j], sl[0]).then_inc(W_split, 1)
                if live(b + -1):
                    a = b + -1
                    dve.wait_ge(x3_rstd, a.count(1, 1))
                    if not a.first:
                        dve.wait_ge(z_raw, a.count(1, 0))
                    for t in range(TT):
                        last = dve.tensor_scalar(z0[:, t * D:(t + 1) * D], acc[:, a.index, t * D:(t + 1) * D],
                                                 mv_3[:, t, 0:1], rs_3[:, t:t + 1], ALU.subtract, ALU.mult)
                    last.then_inc(z0_made, 1)
            over_batches(dve, step)

            for tb in range(TB):
                dve.wait_ge(z_hi, tb + 1)
                zs = [u[:, BB * tb:BB * (tb + 1)].rearrange("p b k n -> p (b k n)") for u in z]
                split_lo(dve, zs[1], kvf[:, BB * tb * 512:BB * (tb + 1) * 512], zs[0]).then_inc(z_split, 1)

            linked = [0]

            def link(ins):
                linked[0] += 1
                ins.then_inc(r_chain, 1)
                dve.wait_ge(r_chain, linked[0])

            def route_groups():
                link(dve.tensor_tensor(biased, score, ebias.unsqueeze(1).broadcast_to([P, NT, E]), ALU.add))
                v = biased.rearrange("p t (q c) -> p (t q) c", c=2)
                h2, l2 = (w.rearrange("p t g a -> p (t g a)") for w in (hi2, lo2))
                link(dve.tensor_tensor(h2, v[:, :, 0], v[:, :, 1], ALU.max))
                link(dve.tensor_tensor(l2, v[:, :, 0], v[:, :, 1], ALU.min))
                link(dve.tensor_tensor(gs, hi2[:, :, :, 0], hi2[:, :, :, 1], ALU.min))
                link(dve.tensor_tensor(g_b, lo2[:, :, :, 0], lo2[:, :, :, 1], ALU.max))
                link(dve.tensor_tensor(gs, gs, g_b, ALU.max))
                link(dve.tensor_tensor(g_b, hi2[:, :, :, 0], hi2[:, :, :, 1], ALU.max))
                link(dve.tensor_tensor(gs, gs, g_b, ALU.add))

            def rank_start(r, n):
                for e in range(n):
                    last = dve.memset(r[:, :, e:e + 1], float(n - 1 - e))
                link(last)

            def rank_steps(r, c, v, n, shifts):
                for d in shifts:
                    link(dve.tensor_tensor(c[:, :, 0:n - d], v[:, :, 0:n - d], v[:, :, d:n], ALU.is_ge))
                    link(dve.tensor_tensor(r[:, :, d:n], r[:, :, d:n], c[:, :, 0:n - d], ALU.add))
                    link(dve.tensor_tensor(r[:, :, 0:n - d], r[:, :, 0:n - d], c[:, :, 0:n - d], ALU.subtract))

            def mask_groups():
                link(dve.tensor_scalar(grank, grank, float(TOPG), None, ALU.is_lt))
                link(dve.tensor_tensor(biased.rearrange("p t (g e) -> p (t g) e", g=GROUPS),
                                       biased.rearrange("p t (g e) -> p (t g) e", g=GROUPS),
                                       grank.rearrange("p t g -> p (t g)").unsqueeze(2).broadcast_to([P, NT * GROUPS, EG]), ALU.mult))

            def combine():
                link(dve.tensor_scalar(rank, rank, float(TOPK), None, ALU.is_lt))
                link(dve.tensor_tensor(rank, rank, score, ALU.mult))
                link(dve.tensor_reduce(wsum, rank, AX.X, ALU.add))
                link(dve.tensor_scalar(wsum, wsum, 1e-20, None, ALU.add))
                link(dve.reciprocal(winv, wsum))
                link(dve.tensor_tensor(rank, rank, winv.unsqueeze(2).broadcast_to([P, NT, E]), ALU.mult))
                dve.tensor_scalar(C_all.rearrange("p e t -> p t e"), rank, SCALE, None, ALU.mult).then_inc(c_made, 1)

            def product_gu(o, register=None):
                def n(k):
                    return o + k if register is None else register * (2 * TB) + (o + k)
                dve.wait_ge(silu, n(1))
                dve.wait_ge(u_raw, n(1))
                if register is not None or o > 3:
                    dve.wait_ge(hT_split, n(-3))
                dve.tensor_tensor(hf[:, o % 4, :], bk(2 * (o % 2) + 1), sq[:, (o % 2) * BLK:(o % 2 + 1) * BLK],
                                  ALU.mult).then_inc(hf_made, 1)

            def low_half(o, register=None):
                dve.wait_ge(hT_hi, o + 1 if register is None else register * (2 * TB) + (o + 1))
                split_lo(dve, hT[1][:, o % 4, :], hf[:, o % 4, :], hT[0][:, o % 4, :]).then_inc(hT_split, 1)

            def add_shared(tb):
                dve.wait_ge(dn_raw, tb + 1)
                a = acc[:, BB * tb:BB * (tb + 1), :].rearrange("p b n -> p (b n)")
                dve.tensor_tensor(a, bk2(4 + 2 * (tb % 2)), a, ALU.add).then_inc(y_added, 1)

            def add_expert(o, register=None):
                tb, s = o % TB, (o // TB) % 2
                d = TB + o - SH * TB
                dve.wait_ge(dn_raw, d + 1 if register is None else register * (2 * TB) + (d + 1))
                if tb == 0:
                    dve.wait_ge(c_copied, s + 1 if register is None else register * 2 + (s + 1))
                dve.wait_ge(y_added, d + 1 - TB if register is None else register * (2 * TB) + (d + 1 - TB))
                a = acc[:, BB * tb:BB * (tb + 1), :].rearrange("p b n -> p (b n)")
                for t in range(TPB):
                    last = dve.scalar_tensor_tensor(out=a[:, t * D:(t + 1) * D], in0=bk2(4 + 2 * (tb % 2))[:, t * D:(t + 1) * D],
                                                    scalar=c_now[s][:, TPB * tb + t:TPB * tb + t + 1],
                                                    in1=a[:, t * D:(t + 1) * D], op0=ALU.mult, op1=ALU.add)
                last.then_inc(y_added, 1)

            for tb in range(TB):
                for s in range(SH):
                    o = SH * tb + s
                    product_gu(o)
                    if o == 0:
                        dve.wait_ge(scoreT_raw, 1)
                        dve.tensor_copy(score, ring[0][:, 0:NT * E].rearrange("p (t e) -> p t e", e=E)).then_inc(score_made, 1)
                        dve.wait_ge(score_made, 1)
                        low_half(o)
                        route_groups()
                    elif o == 1:
                        low_half(o)
                        rank_start(grank, GROUPS)
                        rank_steps(grank, gcmp, gs, GROUPS, range(1, GROUPS))
                        mask_groups()
                        rank_start(rank, E)
                    else:
                        if s == 1:
                            add_shared(tb - 1)
                        low_half(o)
                        rank_steps(rank, cmp, biased, E, {2: range(1, 3), 3: range(3, 5), 4: range(5, 8), 5: range(8, 10),
                                                          6: range(10, 13), 7: range(13, 16)}[o])
            combine()
            o0 = SH * TB
            product_gu(o0)
            add_shared(TB - 1)
            low_half(o0)
            for o in range(o0 + 1, o0 + 2 * TB):
                product_gu(o)
                add_expert(o - 1)
                low_half(o)
            with dve.Fori(1, E // 2) as i:
                for o in range(o0, o0 + 2 * TB):
                    product_gu(o, i)
                    add_expert(o - 1, i)
                    low_half(o, i)
            add_expert(o0 + E * TB - 1)

        @block.gpsimd
        def _(pool):
            pool.memset(ident[:], 0.0).then_inc(ident_zero, 1)
            pool.wait_ge(ident_zero, 1)
            pool.affine_select(out=ident[:], in_=ident[:], compare_op=ALU.not_equal, fill=1.0, base=0,
                               pattern=[[-1, P]], channel_multiplier=1).then_inc(ident_made, 1)
            pool.memset(half[:], -0.5).then_inc(p_chain, 1)
            for u in kvd:
                last = pool.memset(u[:].rearrange("p c n -> p (c n)").bitcast(F32), 0.0)
            last.then_inc(kvd_zero, 1)
            chained = [1]

            def power(dst, src, add, op, chain=None):
                n = dst.shape[1]
                pool.tensor_scalar(dst, src, add, None, op).then_inc(p_chain, 1)
                chained[0] += 1
                pool.wait_ge(p_chain, chain if chain is not None else chained[0])
                return pool.tensor_tensor(dst, dst, half[0:dst.shape[0], 0:n], ALU.pow)

            pool.wait_ge(c_stats, 1)
            power(rs_c[:, 0:CT - 1], mv[:, 0:CT - 1, 1], EPS, ALU.add).then_inc(p_chain, 1)
            chained[0] += 1
            power(rs_c[0:CLAST, CT - 1:CT], mv[0:CLAST, CT - 1, 1:2], EPS, ALU.add).then_inc(c_rstd, 1)
            for b in range(NB):
                pool.wait_ge(k_ss, b + 1)
                power(rs_n[0:NK, 0, :], ss[0:NK, 0, :], 1e-24, ALU.max).then_inc(k_rs, 1)

            base = chained[0]

            def step(b):
                o = b.offset

                def batches(last):
                    return max(0, min(NB, last))
                before = 2 * batches(o + 2) + batches(o) + 2 * batches(o + 1) + batches(o - 1)
                here = [before]

                def chain():
                    here[0] += 1
                    v = base + here[0]
                    return v if b.register is None else b.register * 12 + v

                if live(b + 2):
                    pool.wait_ge(x_stats, (b + 2).count(1, 1))
                    power(rs_x[:], mv_x[:, :, 1], EPS, ALU.add, chain()).then_inc(x_rstd, 1)
                if live(b):
                    pool.wait_ge(x1_stats, b.count(1, 1))
                    power(rs_1[:], mv_1[:, :, 1], EPS, ALU.add, chain()).then_inc(x1_rstd, 1)
                    pool.wait_ge(x1_rstd, b.count(1, 1))
                    if not b.first:
                        pool.wait_ge(xnT_raw, b.count(1, 0))
                    for t in range(TT):
                        last = pool.tensor_scalar(xn0[:, t * D:(t + 1) * D], x1[b.parity][:, t * D:(t + 1) * D],
                                                  mv_1[:, t, 0:1], rs_1[:, t:t + 1], ALU.subtract, ALU.mult)
                    last.then_inc(xn0_made, 1)
                if live(b + 1):
                    a = b + 1
                    for t in range(TT):
                        pool.wait_ge(q_ss, a.count(TT, t + 1))
                        power(rs_n[:, t, :], ss[:, t, :], 1e-24, ALU.max, chain()).then_inc(q_rs, 1)
                if live(b):
                    pool.wait_ge(acc_b2, b.count(1, 1))
                    pool.tensor_tensor(acc[:, b.index, :], acc[:, b.index, :], x1[b.parity], ALU.add).then_inc(acc_x1, 1)
                if live(b + 2):
                    a = b + 2
                    pool.wait_ge(q_stats, a.count(1, 1))
                    power(rs_q2[:], mv_q[:, :, 1], EPS, ALU.add, chain()).then_inc(q2_rstd, 1)
                    pool.wait_ge(q2_rstd, a.count(1, 1))
                    if not a.first:
                        pool.wait_ge(a_raw, a.count(1, 0))
                    for t in range(TT):
                        last = pool.tensor_scalar(Qn0[:, t * D:(t + 1) * D], Q[a.parity][:, t * D:(t + 1) * D],
                                                  mv_q[:, t, 0:1], rs_q2[:, t:t + 1], ALU.subtract, ALU.mult)
                    last.then_inc(Qn0_made, 1)
                    pool.wait_ge(Qn0_made, a.count(1, 1))
                    if b.register is None:
                        pool.wait_ge(small_in, 48)
                    q3 = Q[a.parity].rearrange("p (t d) -> p t d", t=TT)
                    pool.tensor_tensor(q3, q3, bo_r.unsqueeze(1).broadcast_to([P, TT, D]), ALU.add).then_inc(Qb_made, 1)
                    a3 = acc[:, a.index, :].rearrange("p (t d) -> p t d", t=TT)
                    pool.tensor_tensor(a3, a3, b2_r.unsqueeze(1).broadcast_to([P, TT, D]), ALU.add).then_inc(acc_b2, 1)
                if live(b + -1):
                    pool.wait_ge(x3_stats, (b + -1).count(1, 1))
                    power(rs_3[:], mv_3[:, :, 1], EPS, ALU.add, chain()).then_inc(x3_rstd, 1)
            over_batches(pool, step)

            def expert_lo(n, register=None):
                pool.wait_ge(e_hi, n + 1 if register is None else register * 2 + (n + 1))
                w = e_w[2 + n if n < SH and register is None else n % 2]
                split_lo(pool, w[1], e_raw[n % 2], w[0]).then_inc(e_split, 1)

            def expert_rows(s, register=None):
                if register is not None:
                    pool.wait_ge(y_added, register * (2 * TB) + TB * s)
                pool.tensor_copy(c_now[s], C_all[:, s if register is None else register * 2 + s, :]).then_inc(c_copied, 1)
            for n in range(2 * SH):
                expert_lo(n)
            pool.wait_ge(c_made, 1)
            for s in range(2):
                expert_rows(s)
            with pool.Fori(1, E // 2) as i:
                for s in range(2):
                    expert_lo(SH + s, i)
                    expert_rows(s, i)


_INS = ["x", "ctx_1024", "L0_xattn_wq", "L0_xattn_wk", "L0_xattn_wv", "L0_xattn_wo", "L0_xattn_w1", "L0_xattn_w2"]


def kernel(**inputs):
    import numpy as np
    import concourse.bacc as bacc
    from concourse.bass_utils import run_bass_kernel_spmd as run

    def given(name):
        return np.ascontiguousarray(inputs[name])

    def chunks(v):
        return v.reshape(-1, P).T

    def expert_layout(gate, up, down):
        n, inner, d = gate.shape
        g, u = (np.transpose(w, (0, 2, 1)).reshape(n, d // P, P, inner).transpose(0, 2, 1, 3).reshape(n, P, -1) for w in (gate, up))
        return np.concatenate([g, u, np.transpose(down, (0, 2, 1))], axis=2)

    arrays = {f"in_{n}": given(n) for n in _INS}
    arrays["in_router_t"] = np.ascontiguousarray(given("L0_ffn_router_weight").T)
    arrays["in_columns"] = np.ascontiguousarray(np.concatenate(
        [chunks(given("L0_xattn_" + n)) for n in ("ln1_g", "ln1_b", "ln2_g", "ln2_b", "b1")], axis=1))
    arrays["in_rows"] = np.concatenate([given("L0_xattn_bo"), given("L0_xattn_b2"), given("L0_ffn_e_bias")])[None, :]
    gate, up, down = (given("L0_ffn_" + n) for n in ("gate_w", "up_w", "down_w"))
    inner, d = gate.shape[1:]
    sg, su, sd = (given("L0_ffn_sh_" + n) for n in ("gate_w", "up_w", "down_w"))
    shared = expert_layout(sg.reshape(-1, inner, d), su.reshape(-1, inner, d), sd.reshape(d, -1, inner).transpose(1, 0, 2))
    arrays["in_experts"] = np.ascontiguousarray(np.concatenate([shared, expert_layout(gate, up, down)], axis=0))

    nc = bacc.Bacc("TRN2", target_bir_lowering=False, num_devices=1)
    args = [nc.dram_tensor(n, a.shape, mybir.dt.from_np(a.dtype), kind="ExternalInput").ap() for n, a in arrays.items()]
    args.append(nc.dram_tensor("out_0", arrays["in_x"].shape, F32, kind="ExternalOutput").ap())
    bass_cross_attention_ffn_moe_kernel(nc, *args)
    result = run(nc, [arrays], core_ids=[0])
    return result.results[0]["out_0"]
```

```python
from contextlib import ExitStack

import concourse.bass as bass
from concourse import mybir

ALU = mybir.AluOpType
ACT = mybir.ActivationFunctionType
AX = mybir.AxisListType
F32 = mybir.dt.float32
F32R = mybir.dt.float32r

P = 128

def bass_cross_attention_ffn_moe_kernel(nc, x, context, wq, wk, wv, wo, w1, w2, router_t, columns, rows, experts, out):
    NB, NQ, D = x.shape
    _, NK, _ = context.shape
    INNER = wq.shape[1]
    MLP = w1.shape[1]
    E = router_t.shape[1]
    NX = experts.shape[0]
    SH = NX - E
    HEAD = 64
    NH = INNER // HEAD
    KC = D // P
    IC = INNER // P
    MC = MLP // P
    TT = NQ // P
    NT = NB * TT
    CROWS = NB * NK
    CT = (CROWS + P - 1) // P
    CLAST = CROWS - (CT - 1) * P
    BLK = 512
    TB = NB * NQ // BLK
    TPB = BLK // P
    BB = BLK // NQ
    GROUPS, TOPG, TOPK, SCALE = 4, 2, 4, 2.5
    EG = E // GROUPS
    EPS = 1e-5
    assert D == 256 and INNER == 1024 and MLP == 1024 and TT == 2 and NB == 8 and SH == 2 and TOPG == 2

    x_v = x.rearrange("b (t p) d -> p b t d", p=P)
    out_v = out.rearrange("b (t p) d -> p b t d", p=P)
    ctx_v = context.rearrange("b s d -> (b s) d")

    with ExitStack() as ctx:
        def sb(name, shape, dt=F32):
            return ctx.enter_context(nc.sbuf_tensor(name, shape, dt))

        def sem(name):
            return ctx.enter_context(nc.semaphore(name))

        w_io = [sb(f"w_io_{s}", [P, 2, IC * D], F32R) for s in ("hi", "lo")]
        w_mlp = [sb(f"w_mlp_{s}", [P, 2, MC * D], F32R) for s in ("hi", "lo")]
        W = [sb(f"W_{s}", [P, IC, D], F32R) for s in ("hi", "lo")]
        kvd = [sb(f"kvd_{s}", [P, IC, P], F32R) for s in ("hi", "lo")]
        qnT = [sb(f"qnT_{s}", [P, IC, NQ], F32R) for s in ("hi", "lo")]
        h = [sb(f"h_{s}", [P, MC, NQ], F32R) for s in ("hi", "lo")]
        QnT = [sb(f"QnT_{s}", [P, KC, NQ], F32R) for s in ("hi", "lo")]
        xnT = [sb(f"xnT_{s}", [P, KC, NQ], F32R) for s in ("hi", "lo")]
        rw = [sb(f"rw_{s}", [P, KC, E], F32R) for s in ("hi", "lo")]
        acc = sb("acc", [P, NB, TT * D])
        kv_z = sb("kv_z", [P, NB, TT * D])
        hf = sb("hf", [P, 4, BLK])
        qn = sb("qn", [P, TT, INNER])
        sq = sb("sq", [P, INNER])
        arena = sb("arena", [P, 9 * 512])
        ident = sb("ident", [P, P])
        cols = sb("cols", [P, columns.shape[1]])
        rowsb = sb("rowsb", [P, rows.shape[1]])
        rwf = sb("rwf", [P, KC, E])
        stat = sb("stat", [P, CT, 6])
        mv = sb("mv", [P, CT, 2])
        st_x, mv_x = sb("st_x", [P, TT, 6]), sb("mv_x", [P, TT, 2])
        st_q, mv_q = sb("st_q", [P, TT, 6]), sb("mv_q", [P, TT, 2])
        st_1, mv_1 = sb("st_1", [P, TT, 6]), sb("mv_1", [P, TT, 2])
        st_3, mv_3 = sb("st_3", [P, TT, 6]), sb("mv_3", [P, TT, 2])
        rs_c = sb("rs_c", [P, CT])
        rs_x, rs_q2, rs_1, rs_3 = (sb(n, [P, TT]) for n in ("rs_x", "rs_q2", "rs_1", "rs_3"))
        ss = sb("ss", [P, TT, NH])
        rs_n = sb("rs_n", [P, TT, NH])
        half = sb("half", [P, 32])

        g1, b1l, g2, b2l = (cols[:, KC * i:KC * i + KC] for i in range(4))
        b1c = cols[:, 4 * KC:4 * KC + MC]
        bo_r, b2_r = rowsb[:, 0:D], rowsb[:, D:2 * D]
        ebias = rowsb[:, 2 * D:2 * D + E]

        def part(i, n=1):
            return arena[:, 512 * i:512 * (i + n)]
        Q = [part(0), part(1)]
        x1 = [part(2), part(3)]
        xn0, z0, Qn0, QnTf, xnTf = (part(i) for i in range(4, 9))
        kn = [part(2, 2), hf[:, 0:2, :].rearrange("p a n -> p (a n)")]
        vc = [part(4, 2), hf[:, 2:4, :].rearrange("p a n -> p (a n)")]
        wq_s = [w[:, 0, :].rearrange("p (k n) -> p k n", k=KC) for w in w_io]
        wo_s = [w[:, 1, :].rearrange("p (c n) -> p c n", c=IC) for w in w_io]
        w1_s = [w[:, 0, :].rearrange("p (k n) -> p k n", k=KC) for w in w_mlp]
        w2_s = [w[:, 1, :].rearrange("p (c n) -> p c n", c=MC) for w in w_mlp]
        wk_s = [w[:].rearrange("p c n -> p (c n)").rearrange("p (k n) -> p k n", k=KC) for w in qnT]
        wv_s = [w[:].rearrange("p c n -> p (c n)").rearrange("p (k n) -> p k n", k=KC) for w in h]
        kvf = kv_z[:].rearrange("p b n -> p (b n)")
        c0 = kvf[:, 5 * 512:5 * 512 + CT * D].rearrange("p (c n) -> p c n", c=CT)
        cTf = kvf[:, 1280:1280 + KC * CROWS].rearrange("p (k n) -> p k n", k=KC)
        cT = [w[:].rearrange("p c n -> p (c n)")[:, 0:KC * CROWS].rearrange("p (k n) -> p k n", k=KC) for w in W]
        stage = [qn[:].rearrange("p t n -> p (t n)"), hf[:].rearrange("p t n -> p (t n)")]
        z = [w[:].rearrange("p a n -> p (a n)").rearrange("p (b k n) -> p b k n", b=NB, k=KC) for w in w_io]
        EW = 3 * D
        e_raw = [stage[0][:, s * EW:(s + 1) * EW] for s in range(2)]
        e_w = [[w[:].rearrange("p c n -> p (c n)")[:, (s % 2) * EW:(s % 2 + 1) * EW] for w in (qnT, W)[s // 2]] for s in range(4)]
        hT = [w[:].rearrange("p c n -> p (c n)").rearrange("p (s n) -> p s n", s=4) for w in h]
        sT = part(0, 4)
        C_all = part(4)[:, 0:NT * E].rearrange("p (e t) -> p e t", e=E)
        score = part(5)[:, 0:256].rearrange("p (t e) -> p t e", e=E)
        biased = part(5)[:, 256:512].rearrange("p (t e) -> p t e", e=E)
        rank = part(6)[:, 0:256].rearrange("p (t e) -> p t e", e=E)
        ahead, at = [None], 0
        for d in range(1, E):
            ahead.append(sT[:, at:at + NT * (E - d)].rearrange("p (t e) -> p t e", e=E - d))
            at += NT * (E - d)
        hi2 = part(7)[:, 0:128].rearrange("p (t g a) -> p t g a", g=GROUPS, a=2)
        lo2 = part(7)[:, 128:256].rearrange("p (t g a) -> p t g a", g=GROUPS, a=2)
        gs = part(7)[:, 256:320].rearrange("p (t g) -> p t g", g=GROUPS)
        g_b = part(7)[:, 320:384].rearrange("p (t g) -> p t g", g=GROUPS)
        grank = part(7)[:, 384:448].rearrange("p (t g) -> p t g", g=GROUPS)
        gcmp = part(7)[:, 448:512].rearrange("p (t g) -> p t g", g=GROUPS)
        wsum = part(8)[:, 0:NT]
        winv = part(8)[:, NT:2 * NT]
        c_now = [part(8)[:, (2 + s) * NT:(3 + s) * NT] for s in range(2)]

        bank = [ctx.enter_context(nc.psum_tensor(f"bank{i}", [P, 2, 512], F32)) for i in range(4)]

        def bk(i):
            return bank[i // 2][:, i % 2, :]

        def bk2(i):
            return bank[i // 2][:].rearrange("p a n -> p (a n)")
        ring = [bk(4 + i) for i in range(4)]

        ctx_loaded = sem("ctx_loaded")
        small_in = sem("small_in")
        x_in = sem("x_in")
        stage_in = [sem(f"stage_in{i}") for i in range(2)]
        ident_zero = sem("ident_zero")
        ident_made = sem("ident_made")
        c_stats = sem("c_stats")
        c_part = sem("c_part")
        c_rstd = sem("c_rstd")
        c_norm = sem("c_norm")
        cT_raw = sem("cT_raw")
        cTf_made = sem("cTf_made")
        cT_hi = sem("cT_hi")
        cT_split = sem("cT_split")
        w_hi = sem("w_hi")
        wk_split = sem("wk_split")
        wv_split = sem("wv_split")
        w_split = sem("w_split")
        wk_hi = sem("wk_hi")
        wv_hi = sem("wv_hi")
        rw_split = sem("rw_split")
        k_raw = sem("k_raw")
        v_raw = sem("v_raw")
        m_raw = sem("m_raw")
        k_sq = sem("k_sq")
        k_ss = sem("k_ss")
        k_rs = sem("k_rs")
        kn_made = sem("kn_made")
        v_made = sem("v_made")
        kv_made = sem("kv_made")
        p_chain = sem("p_chain")
        x_part = sem("x_part")
        q_part = sem("q_part")
        x1_part = sem("x1_part")
        x3_part = sem("x3_part")
        x_stats = sem("x_stats")
        x_rstd = sem("x_rstd")
        Q_made = sem("Q_made")
        q_stats = sem("q_stats")
        Qn0_made = sem("Qn0_made")
        Qb_made = sem("Qb_made")
        acc_b2 = sem("acc_b2")
        a_raw = sem("a_raw")
        QnTf_made = sem("QnTf_made")
        QnT_hi = sem("QnT_hi")
        QnT_split = sem("QnT_split")
        q_raw = sem("q_raw")
        q_sq = sem("q_sq")
        q_ss = sem("q_ss")
        q_rs = sem("q_rs")
        qn_made = sem("qn_made")
        qnT_raw = sem("qnT_raw")
        qnT_hi = sem("qnT_hi")
        qnT_split = sem("qnT_split")
        kvd_zero = sem("kvd_zero")
        kvd_hi = sem("kvd_hi")
        kvd_split = sem("kvd_split")
        w_raw = sem("w_raw")
        W_hi = sem("W_hi")
        W_split = sem("W_split")
        attn_raw = sem("attn_raw")
        x1_made = sem("x1_made")
        x1_stats = sem("x1_stats")
        xn0_made = sem("xn0_made")
        acc_x1 = sem("acc_x1")
        x1_rstd = sem("x1_rstd")
        q2_rstd = sem("q2_rstd")
        xnT_raw = sem("xnT_raw")
        xnTf_made = sem("xnTf_made")
        xnT_hi = sem("xnT_hi")
        xnT_split = sem("xnT_split")
        mlp_raw = sem("mlp_raw")
        gelu = sem("gelu")
        h_hi = sem("h_hi")
        h_split = sem("h_split")
        y_raw = sem("y_raw")
        x3_made = sem("x3_made")
        x3_stats = sem("x3_stats")
        x3_rstd = sem("x3_rstd")
        z0_made = sem("z0_made")
        z_raw = sem("z_raw")
        zT_made = sem("zT_made")
        z_hi = sem("z_hi")
        z_split = sem("z_split")
        e_in = [sem(f"e_in{i}") for i in range(2)]
        e_hi = sem("e_hi")
        e_split = sem("e_split")
        router_raw = sem("router_raw")
        logits_made = sem("logits_made")
        scoreT_raw = sem("scoreT_raw")
        score_made = sem("score_made")
        c_made = sem("c_made")
        c_copied = sem("c_copied")
        r_chain = sem("r_chain")
        compared = sem("compared")
        rank_chain = sem("rank_chain")
        g_raw = sem("g_raw")
        u_raw = sem("u_raw")
        silu = sem("silu")
        hf_made = sem("hf_made")
        hT_hi = sem("hT_hi")
        hT_split = sem("hT_split")
        dn_raw = sem("dn_raw")
        y_added = sem("y_added")
        out_done = sem("out_done")

        def split_lo(eng, out_lo, full, hi):
            return eng.tensor_tensor(out_lo, full, hi.bitcast(F32), ALU.subtract)

        def passes(pair_l, pair_r):
            return ((pair_l[0], pair_r[0]), (pair_l[0], pair_r[1]), (pair_l[1], pair_r[0]))

        def over_batches(step):
            for b in range(-2, NB + 2):
                step(b)

        def live(b):
            return 0 <= b < NB

        def last_bank(b):
            return ring[0] if b < NB - 1 else ring[2]

        block = ctx.enter_context(nc.Block())

        @block.sync
        def _(sp):
            sp.dma_start(c0[:, 0:CT - 1, :], ctx_v[0:(CT - 1) * P, :].rearrange("(c p) d -> p c d", p=P)).then_inc(ctx_loaded, 16)
            sp.dma_start(c0[0:CLAST, CT - 1, :], ctx_v[(CT - 1) * P:CROWS, :]).then_inc(ctx_loaded, 16)
            sp.dma_start(cols[:], columns).then_inc(small_in, 16)
            sp.dma_start(stage[0].rearrange("p (k n) -> p k n", k=KC), wk.rearrange("(k p) n -> p k n", p=P)).then_inc(stage_in[0], 16)
            sp.dma_start(stage[1].rearrange("p (k n) -> p k n", k=KC), wv.rearrange("(k p) n -> p k n", p=P)).then_inc(stage_in[1], 16)
            for b in range(0, NB, 2):
                sp.dma_start(acc[:, b:b + 2, :].rearrange("p b (t d) -> p b t d", t=TT), x_v[:, b:b + 2]).then_inc(x_in, 16)
            sp.wait_ge(wk_split, 1)
            for n, (w, kc) in enumerate(((wq, KC), (wo, IC), (w1, KC), (w2, MC))):
                sp.wait_ge(w_split, n)
                sp.dma_start(stage[0].rearrange("p (k n) -> p k n", k=kc),
                             w.rearrange("(k p) n -> p k n", p=P)).then_inc(stage_in[0], 16)
            sp.wait_ge(qnT_raw, 4 * NB)
            for n in range(SH):
                sp.dma_start(e_raw[n % 2], experts[n]).then_inc(e_in[n % 2], 16)
            with sp.Fori(0, E // 2) as i:
                for s in range(2):
                    sp.wait_ge(e_split, i * 2 + (s + 1))
                    sp.dma_start(e_raw[s], experts[i * 2 + (SH + s)]).then_inc(e_in[s], 16)
            for tb in range(TB):
                sp.wait_ge(y_added, TB + E * TB - TB + tb + 1)
                sp.dma_start(out_v[:, BB * tb:BB * (tb + 1)],
                             acc[:, BB * tb:BB * (tb + 1), :].rearrange("p b (t d) -> p b t d", t=TT)).then_inc(out_done, 16)
            sp.wait_ge(out_done, 16 * TB)

        @block.tensor
        def _(pe):
            def product(out_, lhs, rhs, chunks):
                for n, c in enumerate(chunks):
                    for m, (a, b) in enumerate(passes(lhs(c), rhs(c))):
                        last = pe.matmul(out_, a, b, start=(n == 0 and m == 0), stop=(n == len(chunks) - 1 and m == 2))
                return last

            pe.wait_ge(ident_made, 1)
            for c in range(CT):
                pe.wait_ge(c_norm, c + 1)
                r = P if c < CT - 1 else CLAST
                for k in range(KC):
                    last = pe.transpose(bk2(2 * k)[:, c * P:c * P + r], c0[0:r, c, k * P:(k + 1) * P], ident[0:r, 0:r])
            last.then_inc(cT_raw, 1)

            def keys(b):
                if b > 1:
                    pe.wait_ge(kn_made, b - 1)
                for n in range(2):
                    for k in range(KC):
                        if b == 0 and n == 0:
                            pe.wait_ge(cT_split, k + 1)
                        for m, (u, w) in enumerate(passes([t[:, k, b * NK:(b + 1) * NK] for t in cT],
                                                          [t[:, k, n * 512:(n + 1) * 512] for t in wk_s])):
                            last = pe.matmul(bk(2 * (b % 2) + n)[0:NK, :], u, w, start=(k == 0 and m == 0),
                                             stop=(k == KC - 1 and m == 2))
                last.then_inc(k_raw, 1)

            def values(b):
                if b:
                    pe.wait_ge(v_made, b)
                for n in range(2):
                    last = product(bk(4 + n)[0:NK, :], lambda k: [t[:, k, b * NK:(b + 1) * NK] for t in cT],
                                   lambda k: [t[:, k, n * 512:(n + 1) * 512] for t in wv_s], range(KC))
                last.then_inc(v_raw, 1)

            def values_keys(b):
                pe.wait_ge(kn_made, b + 1)
                pe.wait_ge(v_made, b + 1)
                if b:
                    pe.wait_ge(kv_made, b)
                for c in range(IC):
                    last = pe.matmul(bk2(6)[:, c * P:(c + 1) * P], vc[b % 2][0:NK, c * P:(c + 1) * P],
                                     kn[b % 2][0:NK, c * P:(c + 1) * P], start=True, stop=True)
                last.then_inc(m_raw, 1)

            pe.wait_ge(wk_split, 1)
            for b in range(NB):
                keys(b)
                if b > 1:
                    values_keys(b - 2)
                if b == 0:
                    pe.wait_ge(wv_split, 1)
                values(b)
            values_keys(NB - 2)
            values_keys(NB - 1)

            def q_transposes(b, t):
                pe.wait_ge(qn_made, TT * b + t + 1)
                for j in range(2):
                    if t == 0:
                        pe.wait_ge(W_split, 4 * b + 3 + j)
                    else:
                        pe.wait_ge(qnT_split, 4 * b + 1 + j)
                    for c in range(4):
                        last = pe.transpose(ring[j][:, c * P:(c + 1) * P],
                                            qn[:, t, (4 * j + c) * P:(4 * j + c + 1) * P], ident[:])
                    last.then_inc(qnT_raw, 1)

            def mlp_up(b, j):
                if j == 0:
                    pe.wait_ge(xnT_split, b + 1)
                elif j == 1 and b:
                    pe.wait_ge(x3_made, b)
                elif j > 1:
                    pe.wait_ge(gelu, 4 * b + j - 1)
                for c in range(2 * j, 2 * j + 2):
                    last = product(ring[2 + j % 2][:, (c % 2) * NQ:(c % 2 + 1) * NQ],
                                   lambda k: [t[:, k, c * P:(c + 1) * P] for t in w1_s],
                                   lambda k: [t[:, k, :] for t in xnT], range(KC))
                last.then_inc(mlp_raw, 1)

            def first_transposes(b):
                pe.wait_ge(Qn0_made, b + 1)
                if b == 0:
                    pe.wait_ge(kn_made, NB)
                for k in range(KC):
                    for t in range(TT):
                        last = pe.transpose(bk(0)[:, k * NQ + t * P:k * NQ + (t + 1) * P],
                                            Qn0[:, t * D + k * P:t * D + (k + 1) * P], ident[:])
                last.then_inc(a_raw, 1)

            def last_transposes(b):
                pe.wait_ge(z0_made, b + 1)
                if live(b + 2):
                    pe.wait_ge(qnT_split, 4 * (b + 2) + 3)
                elif live(b + 1):
                    pe.wait_ge(zT_made, b)
                else:
                    pe.wait_ge(gelu, 4 * NB - 1)
                for k in range(KC):
                    for t in range(TT):
                        last = pe.transpose(last_bank(b)[:, k * NQ + t * P:k * NQ + (t + 1) * P],
                                            z0[:, t * D + k * P:t * D + (k + 1) * P], ident[:])
                last.then_inc(z_raw, 1)

            def attend(b):
                pe.wait_ge(qnT_split, 4 * b + 4)
                for t in range(TT):
                    last = product(ring[1][:, t * D:(t + 1) * D], lambda c: [u[:, c, t * P:(t + 1) * P] for u in qnT],
                                   lambda c: [u[:, c, :] for u in W], range(IC))
                last.then_inc(attn_raw, 1)

            def fold_wo(b):
                pe.wait_ge(kvd_split, b + 1)
                if b == 0:
                    pe.wait_ge(w_split, 2)
                    pe.wait_ge(kv_made, NB)
                for j in range(4):
                    if j < 2 and b > 1:
                        pe.wait_ge(gelu, 4 * (b - 2) + 3 + j)
                    elif j == 2 and b > 2:
                        pe.wait_ge(zT_made, b - 2)
                    elif j == 3 and b:
                        pe.wait_ge(x1_made, b)
                    for c in range(2 * j, 2 * j + 2):
                        last = product(ring[(2 + j) % 4][:, (c % 2) * D:(c % 2 + 1) * D], lambda c_: [u[:, c_, :] for u in kvd],
                                       lambda c_: [u[:, c_, :] for u in wo_s], [c])
                    last.then_inc(w_raw, 1)

            def queries(b):
                pe.wait_ge(QnT_split, b + 1)
                if b == 0:
                    pe.wait_ge(w_split, 1)
                for t in range(TT):
                    for n in range(2):
                        last = product(bk(2 * t + n), lambda k: [u[:, k, t * P:(t + 1) * P] for u in QnT],
                                       lambda k: [u[:, k, n * 512:(n + 1) * 512] for u in wq_s], range(KC))
                    last.then_inc(q_raw, 1)

            def middle_transposes(b):
                pe.wait_ge(xn0_made, b + 1)
                if live(b + 1):
                    pe.wait_ge(W_split, 4 * (b + 1) + 1)
                else:
                    pe.wait_ge(gelu, 4 * b - 1)
                for k in range(KC):
                    for t in range(TT):
                        last = pe.transpose(ring[2][:, k * NQ + t * P:k * NQ + (t + 1) * P],
                                            xn0[:, t * D + k * P:t * D + (k + 1) * P], ident[:])
                last.then_inc(xnT_raw, 1)

            def mlp_down(b):
                if live(b + 2):
                    pe.wait_ge(W_split, 4 * (b + 2) + 2)
                else:
                    pe.wait_ge(gelu, 4 * b + 4)
                for t in range(TT):
                    for c in range(MC):
                        if t == 0 and c % 2 == 0:
                            pe.wait_ge(h_split, 4 * b + c // 2 + 1)
                        for m, (a, w) in enumerate(passes([u[:, c, t * P:(t + 1) * P] for u in h], [u[:, c, :] for u in w2_s])):
                            last = pe.matmul(ring[3][:, t * D:(t + 1) * D], a, w, start=(c == 0 and m == 0),
                                             stop=(c == MC - 1 and m == 2))
                last.then_inc(y_raw, 1)

            def route(tb, out_):
                pe.wait_ge(z_split, tb + 1)
                product(out_[0:E, :], lambda k: [u[:, k, :] for u in rw],
                        lambda k: [u[:, BB * tb:BB * (tb + 1), k, :] for u in z], range(KC)).then_inc(router_raw, 1)

            def up(u, wait_w):
                if wait_w is not None:
                    pe.wait_ge(e_split, wait_w)
                if u.register is None and u.offset == 0:
                    pe.wait_ge(logits_made, TB - 1)
                if u.register is not None or u.offset > 1:
                    pe.wait_ge(hf_made, u(-1))
                for m, done in ((0, g_raw), (1, u_raw)):
                    product(bk(2 * u.parity + m),
                            lambda k: [w[:, m * D + k * P:m * D + (k + 1) * P] for w in e_w[u.slot]],
                            lambda k: [v[:, BB * u.tb:BB * (u.tb + 1), k, :] for v in z], range(KC)).then_inc(done, 1)

            def down(d, slots, tb):
                pe.wait_ge(hT_split, d.units)
                if d.register is None and d.offset == 0:
                    pe.wait_ge(zT_made, NB - 1)
                if d.register is None and d.offset == 1:
                    pe.wait_ge(score_made, 1)
                if d.register is not None or d.offset > 1:
                    pe.wait_ge(y_added, d.count(-1))
                for t in range(TPB):
                    last = product(bk2(4 + 2 * (tb % 2))[:, t * D:(t + 1) * D],
                                   lambda i: [w[:, i[1], t * P:(t + 1) * P] for w in hT],
                                   lambda i: [w[:, 2 * D:3 * D] for w in e_w[i[0]]], slots)
                last.then_inc(dn_raw, 1)

            class Unit:

                def __init__(self, offset, slot, tb, register):
                    self.offset, self.slot, self.tb, self.register = offset, slot, tb, register
                    self.parity = offset % 2

                def __call__(self, n):
                    value = self.offset + n
                    return value if self.register is None else self.register * (2 * TB) + value

            class Down:
                def __init__(self, offset, units, register=None):
                    self.offset, self.register, self._units = offset, register, units

                @property
                def units(self):
                    return self._units if self.register is None else self.register * (2 * TB) + self._units

                def count(self, n):
                    value = self.offset + n
                    return value if self.register is None else self.register * (2 * TB) + value

            def step(b):
                if live(b):
                    q_transposes(b, 0)
                if live(b - 1):
                    if b == 1:
                        pe.wait_ge(w_split, 4)
                    mlp_up(b - 1, 0)
                    mlp_up(b - 1, 1)
                if live(b):
                    q_transposes(b, 1)
                if live(b - 1):
                    mlp_up(b - 1, 2)
                    mlp_up(b - 1, 3)
                if live(b + 1):
                    first_transposes(b + 1)
                if live(b - 2) and live(b):
                    last_transposes(b - 2)
                if live(b):
                    attend(b)
                if live(b + 1):
                    fold_wo(b + 1)
                    queries(b + 1)
                if b == NB - 1:
                    mlp_down(b - 1)
                if live(b):
                    middle_transposes(b)
                if b == NB - 1:
                    pe.wait_ge(rw_split, 2)
                    for tb in range(TB - 1):
                        route(tb, bk(tb))
                    last_transposes(b - 1)
                if b == NB:
                    for n in range(SH):
                        up(Unit(n, SH + n, 0, None), n + 1)
                if live(b - 1) and b != NB - 1:
                    mlp_down(b - 1)
            over_batches(step)

            def shared_up(tb):
                for n in range(SH):
                    up(Unit(SH * tb + n, SH + n, tb, None), None)

            def shared_down(tb):
                down(Down(tb, SH * (tb + 1)), [(SH + n, (SH * tb + n) % 4) for n in range(SH)], tb)

            shared_up(1)
            last_transposes(NB - 1)
            shared_down(0)
            up(Unit(2 * SH, SH, 2, None), None)
            route(TB - 1, ring[2])
            up(Unit(2 * SH + 1, SH + 1, 2, None), None)
            pe.wait_ge(logits_made, TB)
            for t in range(NT):
                last = pe.transpose(ring[3][:, t * E:(t + 1) * E], sT[0:E, t * P:(t + 1) * P], ident[0:E, 0:E])
            last.then_inc(scoreT_raw, 1)
            up(Unit(3 * SH, SH, 3, None), None)
            shared_down(1)
            up(Unit(3 * SH + 1, SH + 1, 3, None), None)
            shared_down(2)

            def expert(s, first, register):
                for tb in range(TB):
                    o = SH * TB + TB * s + tb
                    up(Unit(o, s, tb, register),
                       None if tb else (SH + 1 + s if register is None else register * 2 + (SH + 1 + s)))
                    if first and tb == 0:
                        shared_down(TB - 1)
                    else:
                        p = (o - 1) % (2 * TB)
                        down(Down(TB + (o - 1 - SH * TB), o, register), [(p // TB, (o - 1) % 4)], p % TB)
            assert SH * TB % (2 * TB) == 0
            expert(0, True, None)
            expert(1, False, None)
            with pe.Fori(1, E // 2) as i:
                expert(0, False, i)
                expert(1, False, i)
            o = SH * TB + E * TB
            down(Down(TB + E * TB - 1, o), [(1, (o - 1) % 4)], TB - 1)

        @block.scalar
        def _(act):
            act.dma_start(rowsb[:], rows.broadcast_to([P, rows.shape[1]])).then_inc(small_in, 16)
            act.dma_start(rwf[:], router_t.rearrange("(k p) e -> p k e", p=P)).then_inc(small_in, 16)

            wk_flat, wv_flat = (u[0][:].rearrange("p c n -> p (c n)") for u in (qnT, h))
            act.wait_ge(stage_in[0], 16)
            act.activation(wk_flat, stage[0], ACT.Copy).then_inc(wk_hi, 1)
            act.wait_ge(small_in, 48)
            act.wait_ge(cT_raw, 1)
            for k in range(KC):
                act.activation(cTf[:, k, :], bk2(2 * k)[:, 0:CROWS], ACT.Identity,
                               bias=b1l[:, k:k + 1], scale=g1[:, k:k + 1]).then_inc(cTf_made, 1)
            act.wait_ge(stage_in[1], 16)
            act.activation(wv_flat, stage[1], ACT.Copy).then_inc(wv_hi, 1)

            def kv_out(b):
                act.wait_ge(m_raw, b + 1)
                m = bk2(6).rearrange("p (c d) -> p c d", c=IC)
                for s in (0, HEAD):
                    last = act.activation(kv_z[s:s + HEAD, b, :].rearrange("p (c d) -> p c d", c=IC),
                                          m[s:s + HEAD, :, s:s + HEAD], ACT.Copy)
                last.then_inc(kv_made, 1)

            act.wait_ge(cT_split, KC)
            for b in range(NB):
                act.wait_ge(k_raw, b + 1)
                if b:
                    act.wait_ge(k_ss, b)
                act.activation(sq[0:NK, :], bk2(2 * (b % 2))[0:NK, :], ACT.Square).then_inc(k_sq, 1)
                if b > 1:
                    kv_out(b - 2)
                act.wait_ge(v_raw, b + 1)
                if b == 1:
                    act.wait_ge(wv_split, 1)
                act.activation(vc[b % 2][0:NK, :], bk2(4)[0:NK, :], ACT.Copy).then_inc(v_made, 1)
                if 1 <= b <= 4:
                    act.wait_ge(stage_in[0], 16 * (b + 1))
                    act.activation((w_io[0][:, 0, :], w_io[0][:, 1, :], w_mlp[0][:, 0, :], w_mlp[0][:, 1, :])[b - 1],
                                   stage[0], ACT.Copy).then_inc(w_hi, 1)
            kv_out(NB - 2)
            kv_out(NB - 1)

            def queries_hi(b, t):
                for j in range(2):
                    act.wait_ge(qnT_raw, 4 * b + 2 * t + j + 1)
                    act.activation(qnT[0][:, 4 * j:4 * j + 4, t * P:(t + 1) * P],
                                   ring[j].rearrange("p (c n) -> p c n", c=4), ACT.Copy).then_inc(qnT_hi, 1)

            def gelus(b, j):
                act.wait_ge(mlp_raw, 4 * b + j + 1)
                if b:
                    act.wait_ge(h_split, 4 * b + j - 3)
                for c in range(2 * j, 2 * j + 2):
                    last = act.activation(hf[:, j, (c % 2) * NQ:(c % 2 + 1) * NQ], ring[2 + j % 2][:, (c % 2) * NQ:(c % 2 + 1) * NQ],
                                          ACT.Gelu, bias=b1c[:, c:c + 1])
                last.then_inc(gelu, 1)

            def h_high(b, j):
                act.wait_ge(gelu, 4 * b + j + 1)
                act.activation(h[0][:, 2 * j:2 * j + 2, :].rearrange("p c n -> p (c n)"), hf[:, j, :], ACT.Copy).then_inc(h_hi, 1)

            def z_high(tb):
                act.wait_ge(zT_made, BB * (tb + 1))
                act.activation(z[0][:, BB * tb:BB * (tb + 1)].rearrange("p b k n -> p (b k n)"),
                               kvf[:, BB * tb * 512:BB * (tb + 1) * 512], ACT.Copy).then_inc(z_hi, 1)

            def z_copy(a):
                act.wait_ge(z_raw, a + 1)
                act.wait_ge(kvd_split, min(a + 3, NB))
                act.activation(kv_z[:, a, :], last_bank(a), ACT.Copy).then_inc(zT_made, 1)

            def logits(tb, src):
                act.wait_ge(router_raw, tb + 1)
                act.activation(sT[0:E, tb * BLK:(tb + 1) * BLK], src[0:E, :], ACT.Copy).then_inc(logits_made, 1)

            def expert_hi(n, register=None):
                if register is None:
                    act.wait_ge(e_in[n % 2], 16 * (n // 2 + 1))
                    if n > 3:
                        act.wait_ge(dn_raw, TB * (n - 2))
                else:
                    act.wait_ge(e_in[n % 2], register * 16 + 16 * (n // 2 + 1))
                    act.wait_ge(dn_raw, register * (2 * TB) + TB * (n - 2))
                dst = e_w[2 + n if n < SH and register is None else n % 2][0]
                act.activation(dst, e_raw[n % 2], ACT.Copy).then_inc(e_hi, 1)

            def step(b):
                if b == NB:
                    z_copy(b - 2)
                if live(b):
                    queries_hi(b, 0)
                if live(b - 1):
                    gelus(b - 1, 0)
                    gelus(b - 1, 1)
                    h_high(b - 1, 0)
                if live(b):
                    queries_hi(b, 1)
                if live(b - 1):
                    h_high(b - 1, 1)
                    gelus(b - 1, 2)
                    gelus(b - 1, 3)
                    h_high(b - 1, 2)
                    h_high(b - 1, 3)
                if live(b + 1):
                    a = b + 1
                    act.wait_ge(a_raw, a + 1)
                    if a:
                        act.wait_ge(QnT_split, a)
                    for k in range(KC):
                        last = act.activation(QnTf[:, k * NQ:(k + 1) * NQ], bk(0)[:, k * NQ:(k + 1) * NQ], ACT.Identity,
                                              bias=b1l[:, k:k + 1], scale=g1[:, k:k + 1])
                    last.then_inc(QnTf_made, 1)
                    act.wait_ge(QnTf_made, a + 1)
                    act.activation(QnT[0][:].rearrange("p k n -> p (k n)"), QnTf, ACT.Copy).then_inc(QnT_hi, 1)
                if live(b - 2) and live(b):
                    z_copy(b - 2)
                if live(b + 1):
                    if a == 0:
                        act.wait_ge(kvd_zero, 1)
                        act.wait_ge(kv_made, NB)
                    else:
                        act.wait_ge(w_raw, 4 * a)
                    for s in (0, HEAD):
                        last = act.activation(kvd[0][s:s + HEAD, :, s:s + HEAD],
                                              kv_z[s:s + HEAD, a, :].rearrange("p (c d) -> p c d", c=IC), ACT.Copy)
                    last.then_inc(kvd_hi, 1)
                    for j in range(4):
                        act.wait_ge(w_raw, 4 * a + j + 1)
                        act.activation(W[0][:, 2 * j:2 * j + 2, :].rearrange("p c n -> p (c n)"), ring[(2 + j) % 4],
                                       ACT.Copy).then_inc(W_hi, 1)
                    for t in range(TT):
                        act.wait_ge(q_raw, TT * a + t + 1)
                        if a == 0 and t == 0:
                            act.wait_ge(k_ss, NB)
                        if a or t:
                            act.wait_ge(q_ss, TT * a + t)
                        act.activation(sq[:], bk2(2 * t), ACT.Square).then_inc(q_sq, 1)
                if b == NB - 1:
                    z_high(2)
                    act.wait_ge(attn_raw, NB)
                    expert_hi(0)
                    expert_hi(1)
                if live(b):
                    act.wait_ge(xnT_raw, b + 1)
                    if b:
                        act.wait_ge(xnT_split, b)
                    for k in range(KC):
                        last = act.activation(xnTf[:, k * NQ:(k + 1) * NQ], ring[2][:, k * NQ:(k + 1) * NQ], ACT.Identity,
                                              bias=b2l[:, k:k + 1], scale=g2[:, k:k + 1])
                    last.then_inc(xnTf_made, 1)
                    act.wait_ge(xnTf_made, b + 1)
                    act.activation(xnT[0][:].rearrange("p k n -> p (k n)"), xnTf, ACT.Copy).then_inc(xnT_hi, 1)
                if b == NB - 2:
                    z_high(0)
                    z_high(1)
                if b == NB - 1:
                    act.wait_ge(acc_x1, NB)
                    for tb in range(TB - 1):
                        logits(tb, bk(tb))
            over_batches(step)

            def unit(o, register=None):
                def n(k):
                    return o + k if register is None else register * (2 * TB) + (o + k)
                act.wait_ge(g_raw, n(1))
                if register is not None or o > 1:
                    act.wait_ge(hf_made, n(-1))
                act.activation(sq[:, (o % 2) * BLK:(o % 2 + 1) * BLK], bk(2 * (o % 2)), ACT.Silu).then_inc(silu, 1)
                act.wait_ge(hf_made, n(1))
                if register is None and o < SH * TB + 4:
                    if o == 0:
                        act.wait_ge(y_raw, NB)
                    if o > 3:
                        act.wait_ge(dn_raw, o // SH - 1)
                else:
                    act.wait_ge(dn_raw, n(TB - SH * TB - 3))
                act.activation(hT[0][:, o % 4, :], hf[:, o % 4, :], ACT.Copy).then_inc(hT_hi, 1)

            def expert_pair(register):
                for o in range(SH * TB, SH * TB + 2 * TB):
                    unit(o, register)
                    if o % TB == 1:
                        s = (o - SH * TB) // TB
                        expert_hi(3 + s, register)
            for o in range(SH * TB + TB):
                unit(o)
                if o == 1:
                    expert_hi(2)
                if o == 3:
                    z_copy(NB - 1)
                    z_high(TB - 1)
                    expert_hi(3)
                if o == 4:
                    logits(TB - 1, ring[2])
                if o == 5:
                    act.wait_ge(scoreT_raw, 1)
                    act.activation(score, ring[3][:, 0:NT * E].rearrange("p (t e) -> p t e", e=E), ACT.Sigmoid).then_inc(score_made, 1)
            for o in range(SH * TB + TB, SH * TB + 2 * TB):
                unit(o)
                if o % TB == 1:
                    expert_hi(4)
            with act.Fori(1, E // 2 - 1) as i:
                expert_pair(i)
            last_pair = SH * TB + (E - 2) * TB
            for o in range(last_pair, last_pair + 2 * TB):
                unit(o)
                if o == last_pair + 1:
                    expert_hi(E + 1)

        @block.vector
        def _(dve):
            dve.wait_ge(ctx_loaded, 32)
            for c in range(CT):
                r = P if c < CT - 1 else CLAST
                dve.bn_stats(stat[0:r, c, :], c0[0:r, c, :]).then_inc(c_part, 1)
            dve.wait_ge(c_part, CT)
            for c in range(CT):
                r = P if c < CT - 1 else CLAST
                last = dve.bn_aggr(mv[0:r, c, :], stat[0:r, c, :])
            last.then_inc(c_stats, 1)
            dve.wait_ge(c_rstd, 1)
            for c in range(CT):
                r = P if c < CT - 1 else CLAST
                dve.tensor_scalar(c0[0:r, c, :], c0[0:r, c, :], mv[0:r, c, 0:1], rs_c[0:r, c:c + 1],
                                  ALU.subtract, ALU.mult).then_inc(c_norm, 1)
            for k in range(KC):
                dve.wait_ge(cTf_made, k + 1)
                dve.tensor_copy(cT[0][:, k, :], cTf[:, k, :]).then_inc(cT_hi, 1)
                dve.wait_ge(cT_hi, k + 1)
                split_lo(dve, cT[1][:, k, :], cTf[:, k, :], cT[0][:, k, :]).then_inc(cT_split, 1)
            dve.wait_ge(wv_hi, 1)
            wv_flat = [u[:].rearrange("p c n -> p (c n)") for u in h]
            split_lo(dve, wv_flat[1], stage[1], wv_flat[0]).then_inc(wv_split, 1)
            dve.wait_ge(small_in, 48)
            dve.tensor_copy(rw[0][:], rwf[:]).then_inc(rw_split, 1)
            dve.wait_ge(rw_split, 1)
            split_lo(dve, rw[1][:], rwf[:], rw[0][:]).then_inc(rw_split, 1)

            def heads(a):
                return a.rearrange("p (h d) -> p h d", h=NH)

            def keys_norm(b):
                dve.wait_ge(k_rs, b + 1)
                if b > 1:
                    dve.wait_ge(m_raw, b - 1)
                elif b == 1:
                    dve.wait_ge(wv_split, 1)
                dve.tensor_tensor(heads(kn[b % 2][0:NK, :]), heads(bk2(2 * (b % 2))[0:NK, :]),
                                  rs_n[0:NK, b % 2, :].unsqueeze(2).broadcast_to([NK, NH, HEAD]), ALU.mult).then_inc(kn_made, 1)

            for b in range(NB):
                dve.wait_ge(k_sq, b + 1)
                dve.tensor_reduce(ss[0:NK, b % 2, :], heads(sq[0:NK, :]), AX.X, ALU.add).then_inc(k_ss, 1)
                if b:
                    keys_norm(b - 1)
                if 1 <= b <= 4:
                    dve.wait_ge(w_hi, b)
                    sl = [(w_io[i][:, 0, :], w_io[i][:, 1, :], w_mlp[i][:, 0, :], w_mlp[i][:, 1, :])[b - 1] for i in range(2)]
                    split_lo(dve, sl[1], stage[0], sl[0]).then_inc(w_split, 1)
            keys_norm(NB - 1)

            def queries_lo(b, t):
                for j in range(2):
                    dve.wait_ge(qnT_hi, 4 * b + 2 * t + j + 1)
                    sl = [u[:, 4 * j:4 * j + 4, t * P:(t + 1) * P] for u in qnT]
                    split_lo(dve, sl[1], ring[j].rearrange("p (c n) -> p c n", c=4), sl[0]).then_inc(qnT_split, 1)

            def h_low(b, j):
                dve.wait_ge(h_hi, 4 * b + j + 1)
                sl = [u[:, 2 * j:2 * j + 2, :].rearrange("p c n -> p (c n)") for u in h]
                split_lo(dve, sl[1], hf[:, j, :], sl[0]).then_inc(h_split, 1)

            def stats(st, rows_, done):
                for t in range(TT):
                    dve.bn_stats(st[:, t, :], rows_[:, t * D:(t + 1) * D]).then_inc(done, 1)

            def mean_variance(st, mv_, done, b):
                dve.wait_ge(done, TT * (b + 1))
                for t in range(TT):
                    last = dve.bn_aggr(mv_[:, t, :], st[:, t, :])
                return last

            def normalize(dst, src, mv_, rs):
                for t in range(TT):
                    last = dve.tensor_scalar(dst[:, t * D:(t + 1) * D], src[:, t * D:(t + 1) * D],
                                             mv_[:, t, 0:1], rs[:, t:t + 1], ALU.subtract, ALU.mult)
                return last

            def queries_norm(a, t):
                dve.wait_ge(q_rs, TT * a + t + 1)
                if a:
                    dve.wait_ge(qnT_raw, 4 * a)
                elif t == 0:
                    dve.wait_ge(w_split, 4)
                dve.tensor_tensor(heads(qn[:, t, :]), heads(bk2(2 * t)),
                                  rs_n[:, t, :].unsqueeze(2).broadcast_to([P, NH, HEAD]), ALU.mult).then_inc(qn_made, 1)

            def z_norm(a):
                dve.wait_ge(x3_rstd, a + 1)
                if a:
                    dve.wait_ge(z_raw, a)
                normalize(z0, acc[:, a, :], mv_3, rs_3).then_inc(z0_made, 1)

            def rows_out(a):
                dve.wait_ge(y_raw, a + 1)
                dve.wait_ge(acc_x1, a + 1)
                dve.tensor_tensor(acc[:, a, :], ring[3], acc[:, a, :], ALU.add).then_inc(x3_made, 1)

            def rows_stats(a):
                dve.wait_ge(x3_made, a + 1)
                stats(st_3, acc[:, a, :], x3_part)
                mean_variance(st_3, mv_3, x3_part, a).then_inc(x3_stats, 1)

            def product_gu(o, register=None):
                def n(k):
                    return o + k if register is None else register * (2 * TB) + (o + k)
                dve.wait_ge(silu, n(1))
                if register is None and o == 0:
                    dve.wait_ge(h_split, 4 * NB)
                dve.wait_ge(u_raw, n(1))
                if register is not None or o > 3:
                    dve.wait_ge(hT_split, n(-3))
                dve.tensor_tensor(hf[:, o % 4, :], bk(2 * (o % 2) + 1), sq[:, (o % 2) * BLK:(o % 2 + 1) * BLK],
                                  ALU.mult).then_inc(hf_made, 1)

            def z_low(tb):
                dve.wait_ge(z_hi, tb + 1)
                zs = [u[:, BB * tb:BB * (tb + 1)].rearrange("p b k n -> p (b k n)") for u in z]
                split_lo(dve, zs[1], kvf[:, BB * tb * 512:BB * (tb + 1) * 512], zs[0]).then_inc(z_split, 1)

            def W_low(a, j):
                dve.wait_ge(W_hi, 4 * a + j + 1)
                sl = [u_[:, 2 * j:2 * j + 2, :].rearrange("p c n -> p (c n)") for u_ in W]
                split_lo(dve, sl[1], ring[(2 + j) % 4], sl[0]).then_inc(W_split, 1)

            def step(b):
                if live(b):
                    queries_lo(b, 0)
                if live(b - 1):
                    h_low(b - 1, 0)
                if live(b - 2) and live(b):
                    z_norm(b - 2)
                if live(b + 2):
                    dve.wait_ge(x_in, 16 * ((b + 2) // 2 + 1))
                    stats(st_x, acc[:, b + 2, :], x_part)
                if live(b):
                    queries_lo(b, 1)
                if live(b + 2):
                    mean_variance(st_x, mv_x, x_part, b + 2).then_inc(x_stats, 1)
                if live(b - 1):
                    h_low(b - 1, 1)
                if live(b - 1):
                    h_low(b - 1, 2)
                    h_low(b - 1, 3)
                if live(b + 1):
                    a = b + 1
                    dve.wait_ge(QnT_hi, a + 1)
                    u = [w[:].rearrange("p k n -> p (k n)") for w in QnT]
                    split_lo(dve, u[1], QnTf, u[0]).then_inc(QnT_split, 1)
                    dve.wait_ge(kvd_hi, a + 1)
                    for s in (0, HEAD):
                        last = split_lo(dve, kvd[1][s:s + HEAD, :, s:s + HEAD],
                                        kv_z[s:s + HEAD, a, :].rearrange("p (c d) -> p c d", c=IC),
                                        kvd[0][s:s + HEAD, :, s:s + HEAD])
                    last.then_inc(kvd_split, 1)
                if b == NB - 1:
                    z_low(0)
                    z_low(1)
                    z_low(2)
                if b == NB:
                    product_gu(0)
                if live(b):
                    dve.wait_ge(attn_raw, b + 1)
                    dve.wait_ge(Qb_made, b + 1)
                    if b > 1:
                        dve.wait_ge(acc_x1, b - 1)
                    dve.tensor_tensor(x1[b % 2], ring[1], Q[b % 2], ALU.add).then_inc(x1_made, 1)
                    dve.wait_ge(x1_made, b + 1)
                    stats(st_1, x1[b % 2], x1_part)
                if live(b + 1):
                    W_low(b + 1, 0)
                if live(b):
                    mean_variance(st_1, mv_1, x1_part, b).then_inc(x1_stats, 1)
                if live(b + 1):
                    W_low(b + 1, 1)
                if live(b + 2):
                    a = b + 2
                    dve.wait_ge(x_rstd, a + 1)
                    normalize(Q[a % 2], acc[:, a, :], mv_x, rs_x).then_inc(Q_made, 1)
                if live(b + 1):
                    W_low(b + 1, 2)
                if live(b):
                    dve.wait_ge(x1_rstd, b + 1)
                    if b:
                        dve.wait_ge(xnT_raw, b)
                    normalize(xn0, x1[b % 2], mv_1, rs_1).then_inc(xn0_made, 1)
                if live(b + 1):
                    W_low(b + 1, 3)
                if live(b + 2):
                    a = b + 2
                    dve.wait_ge(Q_made, a + 1)
                    stats(st_q, Q[a % 2], q_part)
                    mean_variance(st_q, mv_q, q_part, a).then_inc(q_stats, 1)
                if live(b + 1):
                    a = b + 1
                    dve.wait_ge(q_sq, TT * a + 1)
                    dve.tensor_reduce(ss[:, 0, :], heads(sq[:]), AX.X, ALU.add).then_inc(q_ss, 1)
                if live(b + 2):
                    a = b + 2
                    dve.wait_ge(q2_rstd, a + 1)
                    if a:
                        dve.wait_ge(a_raw, a)
                    normalize(Qn0, Q[a % 2], mv_q, rs_q2).then_inc(Qn0_made, 1)
                if live(b + 1):
                    a = b + 1
                    dve.wait_ge(q_sq, TT * a + 2)
                    dve.tensor_reduce(ss[:, 1, :], heads(sq[:]), AX.X, ALU.add).then_inc(q_ss, 1)
                if b == NB - 1:
                    rows_out(b - 1)
                    rows_stats(b - 1)
                if live(b):
                    dve.wait_ge(xnT_hi, b + 1)
                    u = [w[:].rearrange("p k n -> p (k n)") for w in xnT]
                    split_lo(dve, u[1], xnTf, u[0]).then_inc(xnT_split, 1)
                if live(b + 1):
                    queries_norm(b + 1, 0)
                if live(b - 1) and b != NB - 1:
                    rows_out(b - 1)
                if live(b + 1):
                    queries_norm(b + 1, 1)
                if live(b - 1) and b != NB - 1:
                    rows_stats(b - 1)
                if b == NB - 1:
                    z_norm(b - 1)
                if b == NB:
                    product_gu(1)
                    z_norm(b - 1)

            over_batches(step)

            linked = [0]

            def link(ins):
                linked[0] += 1
                ins.then_inc(r_chain, 1)
                dve.wait_ge(r_chain, linked[0])

            def route_groups():
                link(dve.tensor_tensor(biased, score, ebias.unsqueeze(1).broadcast_to([P, NT, E]), ALU.add))
                v = biased.rearrange("p t (q c) -> p (t q) c", c=2)
                h2, l2 = (w.rearrange("p t g a -> p (t g a)") for w in (hi2, lo2))
                link(dve.tensor_tensor(h2, v[:, :, 0], v[:, :, 1], ALU.max))
                link(dve.tensor_tensor(l2, v[:, :, 0], v[:, :, 1], ALU.min))
                link(dve.tensor_tensor(gs, hi2[:, :, :, 0], hi2[:, :, :, 1], ALU.min))
                link(dve.tensor_tensor(g_b, lo2[:, :, :, 0], lo2[:, :, :, 1], ALU.max))
                link(dve.tensor_tensor(gs, gs, g_b, ALU.max))
                link(dve.tensor_tensor(g_b, hi2[:, :, :, 0], hi2[:, :, :, 1], ALU.max))
                link(dve.tensor_tensor(gs, gs, g_b, ALU.add))

            def rank_groups():
                n = GROUPS
                for g in range(n):
                    last = dve.memset(grank[:, :, g:g + 1], float(n - 1 - g))
                link(last)
                for d in range(1, n):
                    link(dve.tensor_tensor(gcmp[:, :, 0:n - d], gs[:, :, 0:n - d], gs[:, :, d:n], ALU.is_ge))
                    link(dve.tensor_tensor(grank[:, :, d:n], grank[:, :, d:n], gcmp[:, :, 0:n - d], ALU.add))
                    link(dve.tensor_tensor(grank[:, :, 0:n - d], grank[:, :, 0:n - d], gcmp[:, :, 0:n - d], ALU.subtract))

            def compare():
                for d in range(1, E):
                    dve.tensor_tensor(ahead[d], biased[:, :, 0:E - d], biased[:, :, d:E], ALU.is_ge).then_inc(compared, 1)

            def mask_groups():
                link(dve.tensor_scalar(grank, grank, float(TOPG), None, ALU.is_lt))
                link(dve.tensor_tensor(biased.rearrange("p t (g e) -> p (t g) e", g=GROUPS),
                                       biased.rearrange("p t (g e) -> p (t g) e", g=GROUPS),
                                       grank.rearrange("p t g -> p (t g)").unsqueeze(2).broadcast_to([P, NT * GROUPS, EG]), ALU.mult))

            def combine():
                dve.wait_ge(rank_chain, 1 + 2 * (E - 1))
                link(dve.tensor_scalar(rank, rank, float(TOPK), None, ALU.is_lt))
                link(dve.tensor_tensor(rank, rank, score, ALU.mult))
                link(dve.tensor_reduce(wsum, rank, AX.X, ALU.add))
                link(dve.tensor_scalar(wsum, wsum, 1e-20, None, ALU.add))
                link(dve.reciprocal(winv, wsum))
                link(dve.tensor_tensor(rank, rank, winv.unsqueeze(2).broadcast_to([P, NT, E]), ALU.mult))
                dve.tensor_scalar(C_all.rearrange("p e t -> p t e"), rank, SCALE, None, ALU.mult).then_inc(c_made, 1)

            def low_half(o, register=None):
                dve.wait_ge(hT_hi, o + 1 if register is None else register * (2 * TB) + (o + 1))
                split_lo(dve, hT[1][:, o % 4, :], hf[:, o % 4, :], hT[0][:, o % 4, :]).then_inc(hT_split, 1)

            def add_shared(tb):
                dve.wait_ge(dn_raw, tb + 1)
                a = acc[:, BB * tb:BB * (tb + 1), :].rearrange("p b n -> p (b n)")
                dve.tensor_tensor(a, bk2(4 + 2 * (tb % 2)), a, ALU.add).then_inc(y_added, 1)

            def add_expert(o, register=None):
                tb, s = o % TB, (o // TB) % 2
                d = TB + o - SH * TB
                dve.wait_ge(dn_raw, d + 1 if register is None else register * (2 * TB) + (d + 1))
                if tb == 0:
                    dve.wait_ge(c_copied, s + 1 if register is None else register * 2 + (s + 1))
                dve.wait_ge(y_added, d + 1 - TB if register is None else register * (2 * TB) + (d + 1 - TB))
                a = acc[:, BB * tb:BB * (tb + 1), :].rearrange("p b n -> p (b n)")
                for t in range(TPB):
                    last = dve.scalar_tensor_tensor(out=a[:, t * D:(t + 1) * D], in0=bk2(4 + 2 * (tb % 2))[:, t * D:(t + 1) * D],
                                                    scalar=c_now[s][:, TPB * tb + t:TPB * tb + t + 1],
                                                    in1=a[:, t * D:(t + 1) * D], op0=ALU.mult, op1=ALU.add)
                last.then_inc(y_added, 1)

            low_half(0)
            low_half(1)
            product_gu(2)
            low_half(2)
            product_gu(3)
            low_half(3)
            z_low(TB - 1)
            add_shared(0)
            product_gu(4)
            low_half(4)
            product_gu(5)
            low_half(5)
            product_gu(6)
            dve.wait_ge(score_made, 1)
            route_groups()
            add_shared(1)
            low_half(6)
            rank_groups()
            mask_groups()
            product_gu(7)
            compare()
            low_half(7)
            add_shared(2)
            o0 = SH * TB
            assert o0 == 8
            product_gu(o0)
            low_half(o0)
            add_shared(TB - 1)
            product_gu(o0 + 1)
            combine()
            add_expert(o0)
            low_half(o0 + 1)
            for o in range(o0 + 2, o0 + 2 * TB):
                product_gu(o)
                add_expert(o - 1)
                low_half(o)
            with dve.Fori(1, E // 2) as i:
                for o in range(o0, o0 + 2 * TB):
                    product_gu(o, i)
                    add_expert(o - 1, i)
                    low_half(o, i)
            add_expert(o0 + E * TB - 1)

        @block.gpsimd
        def _(pool):
            pool.memset(ident[:], 0.0).then_inc(ident_zero, 1)
            pool.wait_ge(ident_zero, 1)
            pool.affine_select(out=ident[:], in_=ident[:], compare_op=ALU.not_equal, fill=1.0, base=0,
                               pattern=[[-1, P]], channel_multiplier=1).then_inc(ident_made, 1)
            pool.memset(half[:], -0.5).then_inc(p_chain, 1)
            for u in kvd:
                last = pool.memset(u[:].rearrange("p c n -> p (c n)").bitcast(F32), 0.0)
            last.then_inc(kvd_zero, 1)
            chained = [1]

            def power(dst, src, add, op):
                n = dst.shape[1]
                pool.tensor_scalar(dst, src, add, None, op).then_inc(p_chain, 1)
                chained[0] += 1
                pool.wait_ge(p_chain, chained[0])
                return pool.tensor_tensor(dst, dst, half[0:dst.shape[0], 0:n], ALU.pow)

            pool.wait_ge(c_stats, 1)
            power(rs_c[:, 0:CT - 1], mv[:, 0:CT - 1, 1], EPS, ALU.add).then_inc(p_chain, 1)
            chained[0] += 1
            power(rs_c[0:CLAST, CT - 1:CT], mv[0:CLAST, CT - 1, 1:2], EPS, ALU.add).then_inc(c_rstd, 1)
            pool.wait_ge(wk_hi, 1)
            wk_flat = [u[:].rearrange("p c n -> p (c n)") for u in qnT]
            split_lo(pool, wk_flat[1], stage[0], wk_flat[0]).then_inc(wk_split, 1)
            for b in range(NB):
                pool.wait_ge(k_ss, b + 1)
                if b > 1:
                    pool.wait_ge(kn_made, b - 1)
                power(rs_n[0:NK, b % 2, :], ss[0:NK, b % 2, :], 1e-24, ALU.max).then_inc(k_rs, 1)

            def expert_lo(n, register=None):
                pool.wait_ge(e_hi, n + 1 if register is None else register * 2 + (n + 1))
                w = e_w[2 + n if n < SH and register is None else n % 2]
                split_lo(pool, w[1], e_raw[n % 2], w[0]).then_inc(e_split, 1)

            def step(b):
                if live(b + 2):
                    pool.wait_ge(x_stats, b + 3)
                    power(rs_x[:], mv_x[:, :, 1], EPS, ALU.add).then_inc(x_rstd, 1)
                if live(b):
                    pool.wait_ge(x1_stats, b + 1)
                    power(rs_1[:], mv_1[:, :, 1], EPS, ALU.add).then_inc(x1_rstd, 1)
                    pool.wait_ge(acc_b2, b + 1)
                    pool.tensor_tensor(acc[:, b, :], acc[:, b, :], x1[b % 2], ALU.add).then_inc(acc_x1, 1)
                if live(b + 2):
                    a = b + 2
                    pool.wait_ge(q_stats, a + 1)
                    power(rs_q2[:], mv_q[:, :, 1], EPS, ALU.add).then_inc(q2_rstd, 1)
                if live(b + 1):
                    a = b + 1
                    pool.wait_ge(q_ss, TT * a + 1)
                    power(rs_n[:, 0, :], ss[:, 0, :], 1e-24, ALU.max).then_inc(q_rs, 1)
                    pool.wait_ge(q_ss, TT * a + 2)
                    power(rs_n[:, 1, :], ss[:, 1, :], 1e-24, ALU.max).then_inc(q_rs, 1)
                if live(b + 2):
                    a = b + 2
                    pool.wait_ge(Qn0_made, a + 1)
                    if a == 0:
                        pool.wait_ge(small_in, 48)
                    q3 = Q[a % 2].rearrange("p (t d) -> p t d", t=TT)
                    pool.tensor_tensor(q3, q3, bo_r.unsqueeze(1).broadcast_to([P, TT, D]), ALU.add).then_inc(Qb_made, 1)
                    a3 = acc[:, a, :].rearrange("p (t d) -> p t d", t=TT)
                    pool.tensor_tensor(a3, a3, b2_r.unsqueeze(1).broadcast_to([P, TT, D]), ALU.add).then_inc(acc_b2, 1)
                if live(b - 1):
                    pool.wait_ge(x3_stats, b)
                    power(rs_3[:], mv_3[:, :, 1], EPS, ALU.add).then_inc(x3_rstd, 1)
                if b == NB - 1:
                    for n in range(SH):
                        expert_lo(n)
            over_batches(step)

            def count_ranks():
                for e in range(E):
                    last = pool.memset(rank[:, :, e:e + 1], float(E - 1 - e))
                last.then_inc(rank_chain, 1)
                for d in range(1, E):
                    pool.wait_ge(compared, d)
                    pool.wait_ge(rank_chain, 2 * d - 1)
                    pool.tensor_tensor(rank[:, :, d:E], rank[:, :, d:E], ahead[d], ALU.add).then_inc(rank_chain, 1)
                    pool.wait_ge(rank_chain, 2 * d)
                    pool.tensor_tensor(rank[:, :, 0:E - d], rank[:, :, 0:E - d], ahead[d], ALU.subtract).then_inc(rank_chain, 1)

            def expert_rows(s, register=None):
                if register is not None:
                    pool.wait_ge(y_added, register * (2 * TB) + TB * s)
                pool.tensor_copy(c_now[s], C_all[:, s if register is None else register * 2 + s, :]).then_inc(c_copied, 1)
            for n in range(SH, 2 * SH):
                expert_lo(n)
            count_ranks()
            pool.wait_ge(c_made, 1)
            for s in range(2):
                expert_rows(s)
            with pool.Fori(1, E // 2) as i:
                for s in range(2):
                    expert_lo(SH + s, i)
                    expert_rows(s, i)


_INS = ["x", "ctx_1024", "L0_xattn_wq", "L0_xattn_wk", "L0_xattn_wv", "L0_xattn_wo", "L0_xattn_w1", "L0_xattn_w2"]


def kernel(**inputs):
    import numpy as np
    import concourse.bacc as bacc
    from concourse.bass_utils import run_bass_kernel_spmd as run

    def given(name):
        return np.ascontiguousarray(inputs[name])

    def chunks(v):
        return v.reshape(-1, P).T

    def expert_layout(gate, up, down):
        n, inner, d = gate.shape
        g, u = (np.transpose(w, (0, 2, 1)).reshape(n, d // P, P, inner).transpose(0, 2, 1, 3).reshape(n, P, -1) for w in (gate, up))
        return np.concatenate([g, u, np.transpose(down, (0, 2, 1))], axis=2)

    arrays = {f"in_{n}": given(n) for n in _INS}
    arrays["in_router_t"] = np.ascontiguousarray(given("L0_ffn_router_weight").T)
    arrays["in_columns"] = np.ascontiguousarray(np.concatenate(
        [chunks(given("L0_xattn_" + n)) for n in ("ln1_g", "ln1_b", "ln2_g", "ln2_b", "b1")], axis=1))
    arrays["in_rows"] = np.concatenate([given("L0_xattn_bo"), given("L0_xattn_b2"), given("L0_ffn_e_bias")])[None, :]
    gate, up, down = (given("L0_ffn_" + n) for n in ("gate_w", "up_w", "down_w"))
    inner, d = gate.shape[1:]
    sg, su, sd = (given("L0_ffn_sh_" + n) for n in ("gate_w", "up_w", "down_w"))
    shared = expert_layout(sg.reshape(-1, inner, d), su.reshape(-1, inner, d), sd.reshape(d, -1, inner).transpose(1, 0, 2))
    arrays["in_experts"] = np.ascontiguousarray(np.concatenate([shared, expert_layout(gate, up, down)], axis=0))

    nc = bacc.Bacc("TRN2", target_bir_lowering=False, num_devices=1)
    args = [nc.dram_tensor(n, a.shape, mybir.dt.from_np(a.dtype), kind="ExternalInput").ap() for n, a in arrays.items()]
    args.append(nc.dram_tensor("out_0", arrays["in_x"].shape, F32, kind="ExternalOutput").ap())
    bass_cross_attention_ffn_moe_kernel(nc, *args)
    result = run(nc, [arrays], core_ids=[0])
    return result.results[0]["out_0"]
```

```python
from contextlib import ExitStack

import concourse.bass as bass
from concourse import mybir

ALU = mybir.AluOpType
ACT = mybir.ActivationFunctionType
AX = mybir.AxisListType
F32 = mybir.dt.float32
F32R = mybir.dt.float32r

P = 128

def bass_cross_attention_ffn_moe_kernel(nc, x, context, wq, wk, wv, wo, w1, w2, router_t, columns, rows, experts, out):
    NB, NQ, D = x.shape
    _, NK, _ = context.shape
    INNER = wq.shape[1]
    MLP = w1.shape[1]
    E = router_t.shape[1]
    NX = experts.shape[0]
    SH = NX - E
    HEAD = 64
    NH = INNER // HEAD
    KC = D // P
    IC = INNER // P
    MC = MLP // P
    TT = NQ // P
    NT = NB * TT
    CROWS = NB * NK
    CT = (CROWS + P - 1) // P
    CLAST = CROWS - (CT - 1) * P
    BLK = 512
    TB = NB * NQ // BLK
    TPB = BLK // P
    BB = BLK // NQ
    GROUPS, TOPG, TOPK, SCALE = 4, 2, 4, 2.5
    EG = E // GROUPS
    EPS = 1e-5
    WARM_START, WARM_WEIGHTS = 16, 30
    assert D == 256 and INNER == 1024 and MLP == 1024 and TT == 2 and NB == 8 and SH == 2 and TOPG == 2

    x_v = x.rearrange("b (t p) d -> p b t d", p=P)
    out_v = out.rearrange("b (t p) d -> p b t d", p=P)
    ctx_v = context.rearrange("b s d -> (b s) d")

    with ExitStack() as ctx:
        def sb(name, shape, dt=F32):
            return ctx.enter_context(nc.sbuf_tensor(name, shape, dt))

        def sem(name):
            return ctx.enter_context(nc.semaphore(name))

        w_io = [sb(f"w_io_{s}", [P, 2, IC * D], F32R) for s in ("hi", "lo")]
        w_mlp = [sb(f"w_mlp_{s}", [P, 2, MC * D], F32R) for s in ("hi", "lo")]
        W = [sb(f"W_{s}", [P, IC, D], F32R) for s in ("hi", "lo")]
        kvd = [sb(f"kvd_{s}", [P, IC, P], F32R) for s in ("hi", "lo")]
        qnT = [sb(f"qnT_{s}", [P, IC, NQ], F32R) for s in ("hi", "lo")]
        h = [sb(f"h_{s}", [P, MC, NQ], F32R) for s in ("hi", "lo")]
        QnT = [sb(f"QnT_{s}", [P, KC, NQ], F32R) for s in ("hi", "lo")]
        xnT = [sb(f"xnT_{s}", [P, KC, NQ], F32R) for s in ("hi", "lo")]
        rw = [sb(f"rw_{s}", [P, KC, E], F32R) for s in ("hi", "lo")]
        acc = sb("acc", [P, NB, TT * D])
        kv_z = sb("kv_z", [P, NB, TT * D])
        hf = sb("hf", [P, 4, BLK])
        qn = sb("qn", [P, TT, INNER])
        sq = sb("sq", [P, INNER])
        arena = sb("arena", [P, 9 * 512])
        ident = sb("ident", [P, P])
        cols = sb("cols", [P, columns.shape[1]])
        rowsb = sb("rowsb", [P, rows.shape[1]])
        rwf = sb("rwf", [P, KC, E])
        stat = sb("stat", [P, CT, 6])
        mv = sb("mv", [P, CT, 2])
        st_x, mv_x = sb("st_x", [P, TT, 6]), sb("mv_x", [P, TT, 2])
        st_q, mv_q = sb("st_q", [P, TT, 6]), sb("mv_q", [P, TT, 2])
        st_1, mv_1 = sb("st_1", [P, TT, 6]), sb("mv_1", [P, TT, 2])
        st_3, mv_3 = sb("st_3", [P, TT, 6]), sb("mv_3", [P, TT, 2])
        rs_c = sb("rs_c", [P, CT])
        rs_x, rs_q2, rs_1, rs_3 = (sb(n, [P, TT]) for n in ("rs_x", "rs_q2", "rs_1", "rs_3"))
        ss = sb("ss", [P, TT, NH])
        rs_n = sb("rs_n", [P, TT, NH])
        half = sb("half", [P, 32])

        g1, b1l, g2, b2l = (cols[:, KC * i:KC * i + KC] for i in range(4))
        b1c = cols[:, 4 * KC:4 * KC + MC]
        bo_r, b2_r = rowsb[:, 0:D], rowsb[:, D:2 * D]
        ebias = rowsb[:, 2 * D:2 * D + E]

        def part(i, n=1):
            return arena[:, 512 * i:512 * (i + n)]
        Q = [part(0), part(1)]
        x1 = [part(2), part(3)]
        xn0, z0, Qn0, QnTf, xnTf = (part(i) for i in range(4, 9))
        kn = [part(2, 2), hf[:, 0:2, :].rearrange("p a n -> p (a n)")]
        vc = [part(4, 2), hf[:, 2:4, :].rearrange("p a n -> p (a n)")]
        wq_s = [w[:, 0, :].rearrange("p (k n) -> p k n", k=KC) for w in w_io]
        wo_s = [w[:, 1, :].rearrange("p (c n) -> p c n", c=IC) for w in w_io]
        w1_s = [w[:, 0, :].rearrange("p (k n) -> p k n", k=KC) for w in w_mlp]
        w2_s = [w[:, 1, :].rearrange("p (c n) -> p c n", c=MC) for w in w_mlp]
        wk_s = [w[:].rearrange("p c n -> p (c n)").rearrange("p (k n) -> p k n", k=KC) for w in qnT]
        wv_s = [w[:].rearrange("p c n -> p (c n)").rearrange("p (k n) -> p k n", k=KC) for w in h]
        kvf = kv_z[:].rearrange("p b n -> p (b n)")
        c0 = kvf[:, 5 * 512:5 * 512 + CT * D].rearrange("p (c n) -> p c n", c=CT)
        cTf = kvf[:, 1280:1280 + KC * CROWS].rearrange("p (k n) -> p k n", k=KC)
        cT = [w[:].rearrange("p c n -> p (c n)")[:, 0:KC * CROWS].rearrange("p (k n) -> p k n", k=KC) for w in W]
        HALF = KC * INNER // 2
        w_halves = [[w[:, j, n * HALF:(n + 1) * HALF] for w in ws] for ws in (w_io, w_mlp) for j in range(2) for n in range(2)]
        stage = [qn[:].rearrange("p t n -> p (t n)"), hf[:].rearrange("p t n -> p (t n)")]
        z = [w[:].rearrange("p a n -> p (a n)").rearrange("p (b k n) -> p b k n", b=NB, k=KC) for w in w_io]
        EW = 3 * D
        e_raw = [stage[0][:, s * EW:(s + 1) * EW] for s in range(2)]
        e_w = [[w[:].rearrange("p c n -> p (c n)")[:, (s % 2) * EW:(s % 2 + 1) * EW] for w in (qnT, W)[s // 2]] for s in range(4)]
        hT = [w[:].rearrange("p c n -> p (c n)").rearrange("p (s n) -> p s n", s=4) for w in h]
        sT = part(0, 4)
        C_all = part(4)[:, 0:NT * E].rearrange("p (e t) -> p e t", e=E)
        score = part(5)[:, 0:256].rearrange("p (t e) -> p t e", e=E)
        biased = part(5)[:, 256:512].rearrange("p (t e) -> p t e", e=E)
        rank = part(6)[:, 0:256].rearrange("p (t e) -> p t e", e=E)
        later = part(6)[:, 256:512].rearrange("p (t e) -> p t e", e=E)
        ahead, at = [None], 0
        for d in range(1, E):
            ahead.append(sT[:, at:at + NT * (E - d)].rearrange("p (t e) -> p t e", e=E - d))
            at += NT * (E - d)
        pair_max = part(7)[:, 0:128].rearrange("p (t g a) -> p t g a", g=GROUPS, a=2)
        pair_sum = part(7)[:, 128:256].rearrange("p (t g a) -> p t g a", g=GROUPS, a=2)
        gs = part(7)[:, 256:320].rearrange("p (t g) -> p t g", g=GROUPS)
        grank = part(7)[:, 384:448].rearrange("p (t g) -> p t g", g=GROUPS)
        gcmp = part(7)[:, 448:512].rearrange("p (t g) -> p t g", g=GROUPS)
        wsum = part(8)[:, 0:NT]
        winv = part(8)[:, NT:2 * NT]
        c_now = [part(8)[:, (2 + s) * NT:(3 + s) * NT] for s in range(2)]

        bank = [ctx.enter_context(nc.psum_tensor(f"bank{i}", [P, 2, 512], F32)) for i in range(4)]

        def bk(i):
            return bank[i // 2][:, i % 2, :]

        def bk2(i):
            return bank[i // 2][:].rearrange("p a n -> p (a n)")
        ring = [bk(4 + i) for i in range(4)]

        ctx_first = sem("ctx_first")
        ctx_loaded = sem("ctx_loaded")
        small_in = sem("small_in")
        columns_in = sem("columns_in")
        x_in = sem("x_in")
        wk_in = [sem(f"wk_in{i}") for i in range(2)]
        wv_in = [sem(f"wv_in{i}") for i in range(2)]
        w_in = [sem(f"w_in{i}") for i in range(2)]
        ident_zero = sem("ident_zero")
        ident_made = sem("ident_made")
        c_stats = sem("c_stats")
        c_part = sem("c_part")
        c_rstd = sem("c_rstd")
        c_norm = sem("c_norm")
        cT_raw = sem("cT_raw")
        cTf_made = sem("cTf_made")
        cT_hi = sem("cT_hi")
        cT_split = sem("cT_split")
        w_hi = sem("w_hi")
        wk_split = [sem(f"wk_split{i}") for i in range(2)]
        wv_split = [sem(f"wv_split{i}") for i in range(2)]
        w_split = [sem(f"w_split{i}") for i in range(2)]
        wk_hi = sem("wk_hi")
        wv_hi = sem("wv_hi")
        rw_split = sem("rw_split")
        k_raw = sem("k_raw")
        v_raw = sem("v_raw")
        m_raw = sem("m_raw")
        k_sq = sem("k_sq")
        k_ss = sem("k_ss")
        k_rs = sem("k_rs")
        kn_made = sem("kn_made")
        v_made = sem("v_made")
        kv_made = sem("kv_made")
        p_chain = sem("p_chain")
        x_part = sem("x_part")
        q_part = sem("q_part")
        x1_part = sem("x1_part")
        x3_part = sem("x3_part")
        x_stats = sem("x_stats")
        x_rstd = sem("x_rstd")
        Q_made = sem("Q_made")
        q_stats = sem("q_stats")
        Qn0_made = sem("Qn0_made")
        Qb_made = sem("Qb_made")
        acc_b2 = sem("acc_b2")
        a_raw = sem("a_raw")
        QnTf_made = sem("QnTf_made")
        QnT_hi = sem("QnT_hi")
        QnT_split = sem("QnT_split")
        q_raw = sem("q_raw")
        q_sq = sem("q_sq")
        q_ss = sem("q_ss")
        q_rs = sem("q_rs")
        qn_made = sem("qn_made")
        qnT_raw = sem("qnT_raw")
        qnT_hi = sem("qnT_hi")
        qnT_split = sem("qnT_split")
        kvd_zero = sem("kvd_zero")
        kvd_hi = sem("kvd_hi")
        kvd_split = sem("kvd_split")
        w_raw = sem("w_raw")
        W_hi = sem("W_hi")
        W_split = sem("W_split")
        attn_raw = sem("attn_raw")
        x1_made = sem("x1_made")
        x1_stats = sem("x1_stats")
        xn0_made = sem("xn0_made")
        acc_x1 = sem("acc_x1")
        x1_rstd = sem("x1_rstd")
        q2_rstd = sem("q2_rstd")
        xnT_raw = sem("xnT_raw")
        xnTf_made = sem("xnTf_made")
        xnT_hi = sem("xnT_hi")
        xnT_split = sem("xnT_split")
        mlp_raw = sem("mlp_raw")
        gelu = sem("gelu")
        h_hi = sem("h_hi")
        h_split = sem("h_split")
        y_raw = sem("y_raw")
        x3_made = sem("x3_made")
        x3_stats = sem("x3_stats")
        x3_rstd = sem("x3_rstd")
        z0_made = sem("z0_made")
        z_raw = sem("z_raw")
        zT_made = sem("zT_made")
        z_hi = sem("z_hi")
        z_split = sem("z_split")
        e_in = [sem(f"e_in{i}") for i in range(2)]
        e_hi = sem("e_hi")
        e_split = sem("e_split")
        router_raw = sem("router_raw")
        logits_made = sem("logits_made")
        scoreT_raw = sem("scoreT_raw")
        score_made = sem("score_made")
        c_made = sem("c_made")
        c_copied = sem("c_copied")
        r_chain = sem("r_chain")
        compared = sem("compared")
        earlier_counted = sem("earlier_counted")
        later_counted = sem("later_counted")
        g_raw = sem("g_raw")
        u_raw = sem("u_raw")
        silu = sem("silu")
        hf_made = sem("hf_made")
        hT_hi = sem("hT_hi")
        hT_split = sem("hT_split")
        dn_raw = sem("dn_raw")
        y_added = sem("y_added")
        out_done = sem("out_done")

        def split_lo(eng, out_lo, full, hi):
            return eng.tensor_tensor(out_lo, full, hi.bitcast(F32), ALU.subtract)

        def passes(pair_l, pair_r):
            return ((pair_l[0], pair_r[0]), (pair_l[0], pair_r[1]), (pair_l[1], pair_r[0]))

        def over_batches(step):
            for b in range(NB + 2):
                step(b)

        def live(b):
            return 0 <= b < NB

        def queries_bank(b, t, j):
            return bk(2 + j) if b == 0 and t == 1 else ring[j]

        def last_bank(b):
            return ring[0] if b < NB - 1 else ring[2]

        block = ctx.enter_context(nc.Block())

        @block.sync
        def _(sp):
            sp.dma_start(c0[:, 0, :], ctx_v[0:P, :]).then_inc(ctx_first, 16)
            sp.dma_start(c0[:, 1:CT - 1, :], ctx_v[P:(CT - 1) * P, :].rearrange("(c p) d -> p c d", p=P)).then_inc(ctx_loaded, 16)
            sp.dma_start(c0[0:CLAST, CT - 1, :], ctx_v[(CT - 1) * P:CROWS, :]).then_inc(ctx_loaded, 16)
            for w, buffer, done in ((wk, stage[0], wk_in), (wv, stage[1], wv_in)):
                for n in range(2):
                    sp.dma_start(buffer.rearrange("p (k n) -> p k n", k=KC)[:, :, n * 512:(n + 1) * 512],
                                 w.rearrange("(k p) n -> p k n", p=P)[:, :, n * 512:(n + 1) * 512]).then_inc(done[n], 16)
            sp.wait_ge(wk_split[0], 1)
            sp.wait_ge(wk_split[1], 1)
            for n in range(8):
                w = (wq, wo, w1, w2)[n // 2]
                if n > 1:
                    sp.wait_ge(w_split[n % 2], n // 2)
                rows_ = w.shape[0] // 2
                sp.dma_start(stage[0][:, (n % 2) * HALF:(n % 2 + 1) * HALF].rearrange("p (k n) -> p k n", k=rows_ // P),
                             w[(n % 2) * rows_:(n % 2 + 1) * rows_, :].rearrange("(k p) n -> p k n", p=P)).then_inc(w_in[n % 2], 16)
                if n > 3:
                    b = 2 * (n - 4)
                    sp.dma_start(acc[:, b:b + 2, :].rearrange("p b (t d) -> p b t d", t=TT), x_v[:, b:b + 2]).then_inc(x_in, 16)
            sp.wait_ge(qnT_raw, 4 * NB)
            for n in range(SH):
                sp.dma_start(e_raw[n % 2], experts[n]).then_inc(e_in[n % 2], 16)
            with sp.Fori(0, E // 2) as i:
                for s in range(2):
                    sp.wait_ge(e_split, i * 2 + (s + 1))
                    sp.dma_start(e_raw[s], experts[i * 2 + (SH + s)]).then_inc(e_in[s], 16)
            for tb in range(TB):
                sp.wait_ge(y_added, TB + E * TB - TB + tb + 1)
                sp.dma_start(out_v[:, BB * tb:BB * (tb + 1)],
                             acc[:, BB * tb:BB * (tb + 1), :].rearrange("p b (t d) -> p b t d", t=TT)).then_inc(out_done, 16)
            sp.wait_ge(out_done, 16 * TB)

        @block.tensor
        def _(pe):
            def product(out_, lhs, rhs, chunks):
                for n, c in enumerate(chunks):
                    for m, (a, b) in enumerate(passes(lhs(c), rhs(c))):
                        last = pe.matmul(out_, a, b, start=(n == 0 and m == 0), stop=(n == len(chunks) - 1 and m == 2))
                return last

            pe.wait_ge(ident_made, 1)
            for n in range(WARM_START):
                pe.transpose(ring[3][:, 0:P], ident[:], ident[:])

            pe.wait_ge(c_norm, 1)
            for k in range(KC):
                last = pe.transpose(ring[2][:, k * P:(k + 1) * P], c0[:, 0, k * P:(k + 1) * P], ident[:])
            last.then_inc(cT_raw, 1)
            for n in range(WARM_WEIGHTS):
                pe.transpose(ring[3][:, 0:P], ident[:], ident[:])

            def other_context():
                pe.wait_ge(cTf_made, KC)
                for c in range(1, CT):
                    pe.wait_ge(c_norm, c + 1)
                    r = P if c < CT - 1 else CLAST
                    for k in range(KC):
                        last = pe.transpose(ring[2 + k][:, (c - 1) * P:(c - 1) * P + r], c0[0:r, c, k * P:(k + 1) * P], ident[0:r, 0:r])
                last.then_inc(cT_raw, 1)

            def keys(b):
                if b > 1:
                    pe.wait_ge(kn_made, b - 1)
                if b < 2:
                    pe.wait_ge(cT_split, KC * (b + 1))
                for n in range(2):
                    if b == 0:
                        pe.wait_ge(wk_split[n], 1)
                    for k in range(KC):
                        for m, (u, w) in enumerate(passes([t[:, k, b * NK:(b + 1) * NK] for t in cT],
                                                          [t[:, k, n * 512:(n + 1) * 512] for t in wk_s])):
                            last = pe.matmul(bk(2 * (b % 2) + n)[0:NK, :], u, w, start=(k == 0 and m == 0),
                                             stop=(k == KC - 1 and m == 2))
                last.then_inc(k_raw, 1)

            def values(b):
                if b:
                    pe.wait_ge(v_made, b)
                for n in range(2):
                    if b == 0:
                        pe.wait_ge(wv_split[n], 1)
                    last = product(bk(4 + n)[0:NK, :], lambda k: [t[:, k, b * NK:(b + 1) * NK] for t in cT],
                                   lambda k: [t[:, k, n * 512:(n + 1) * 512] for t in wv_s], range(KC))
                last.then_inc(v_raw, 1)

            def values_keys(b):
                pe.wait_ge(kn_made, b + 1)
                pe.wait_ge(v_made, b + 1)
                if b:
                    pe.wait_ge(kv_made, b)
                for c in range(IC):
                    last = pe.matmul(bk2(6)[:, c * P:(c + 1) * P], vc[b % 2][0:NK, c * P:(c + 1) * P],
                                     kn[b % 2][0:NK, c * P:(c + 1) * P], start=True, stop=True)
                last.then_inc(m_raw, 1)

            for b in range(NB):
                keys(b)
                if b == 0:
                    other_context()
                if b > 1:
                    values_keys(b - 2)
                if b < NB - 1:
                    values(b)

            def q_transposes(b, t):
                pe.wait_ge(qn_made, TT * b + t + 1)
                for j in range(2):
                    if t == 0:
                        pe.wait_ge(W_split, 4 * b + 3 + j)
                    elif b:
                        pe.wait_ge(qnT_split, 4 * b + 1 + j)
                    for c in range(4):
                        last = pe.transpose(queries_bank(b, t, j)[:, c * P:(c + 1) * P],
                                            qn[:, t, (4 * j + c) * P:(4 * j + c + 1) * P], ident[:])
                    last.then_inc(qnT_raw, 1)

            def mlp_up(b, j):
                if j == 0:
                    pe.wait_ge(xnT_split, b + 1)
                elif j == 1 and b:
                    pe.wait_ge(x3_made, b)
                elif j > 1:
                    pe.wait_ge(gelu, 4 * b + j - 1)
                for c in range(2 * j, 2 * j + 2):
                    last = product(ring[2 + j % 2][:, (c % 2) * NQ:(c % 2 + 1) * NQ],
                                   lambda k: [t[:, k, c * P:(c + 1) * P] for t in w1_s],
                                   lambda k: [t[:, k, :] for t in xnT], range(KC))
                last.then_inc(mlp_raw, 1)

            def first_transposes(b):
                pe.wait_ge(Qn0_made, b + 1)
                if b == 0:
                    pe.wait_ge(kn_made, NB - 1)
                for k in range(KC):
                    for t in range(TT):
                        last = pe.transpose(bk(0)[:, k * NQ + t * P:k * NQ + (t + 1) * P],
                                            Qn0[:, t * D + k * P:t * D + (k + 1) * P], ident[:])
                last.then_inc(a_raw, 1)

            def last_transposes(b):
                pe.wait_ge(z0_made, b + 1)
                if live(b + 2):
                    pe.wait_ge(qnT_split, 4 * (b + 2) + 3)
                elif live(b + 1):
                    pe.wait_ge(zT_made, b)
                else:
                    pe.wait_ge(gelu, 4 * NB - 1)
                for k in range(KC):
                    for t in range(TT):
                        last = pe.transpose(last_bank(b)[:, k * NQ + t * P:k * NQ + (t + 1) * P],
                                            z0[:, t * D + k * P:t * D + (k + 1) * P], ident[:])
                last.then_inc(z_raw, 1)

            def attend(b):
                pe.wait_ge(qnT_split, 4 * b + 4)
                for t in range(TT):
                    last = product(ring[1][:, t * D:(t + 1) * D], lambda c: [u[:, c, t * P:(t + 1) * P] for u in qnT],
                                   lambda c: [u[:, c, :] for u in W], range(IC))
                last.then_inc(attn_raw, 1)

            def fold_wo(b):
                pe.wait_ge(kvd_split, b + 1)
                if b == 0:
                    pe.wait_ge(w_split[0], 2)
                    pe.wait_ge(w_split[1], 2)
                    pe.wait_ge(kv_made, NB)
                for j in range(4):
                    if j < 2 and b > 1:
                        pe.wait_ge(gelu, 4 * (b - 2) + 3 + j)
                    elif j == 2 and b > 2:
                        pe.wait_ge(zT_made, b - 2)
                    elif j == 3 and b:
                        pe.wait_ge(x1_made, b)
                    for c in range(2 * j, 2 * j + 2):
                        last = product(ring[(2 + j) % 4][:, (c % 2) * D:(c % 2 + 1) * D], lambda c_: [u[:, c_, :] for u in kvd],
                                       lambda c_: [u[:, c_, :] for u in wo_s], [c])
                    last.then_inc(w_raw, 1)

            def queries(b, t):
                pe.wait_ge(QnT_split, b + 1)
                if b == 0:
                    pe.wait_ge(w_split[0], 1)
                    pe.wait_ge(w_split[1], 1)
                    pe.wait_ge(kn_made, NB - 1 + t)
                for n in range(2):
                    last = product(bk(2 * t + n), lambda k: [u[:, k, t * P:(t + 1) * P] for u in QnT],
                                   lambda k: [u[:, k, n * 512:(n + 1) * 512] for u in wq_s], range(KC))
                last.then_inc(q_raw, 1)

            def middle_transposes(b):
                pe.wait_ge(xn0_made, b + 1)
                if live(b + 1):
                    pe.wait_ge(W_split, 4 * (b + 1) + 1)
                else:
                    pe.wait_ge(gelu, 4 * b - 1)
                for k in range(KC):
                    for t in range(TT):
                        last = pe.transpose(ring[2][:, k * NQ + t * P:k * NQ + (t + 1) * P],
                                            xn0[:, t * D + k * P:t * D + (k + 1) * P], ident[:])
                last.then_inc(xnT_raw, 1)

            def mlp_down(b):
                if live(b + 2):
                    pe.wait_ge(W_split, 4 * (b + 2) + 2)
                else:
                    pe.wait_ge(gelu, 4 * b + 4)
                for t in range(TT):
                    for c in range(MC):
                        if t == 0 and c % 2 == 0:
                            pe.wait_ge(h_split, 4 * b + c // 2 + 1)
                        for m, (a, w) in enumerate(passes([u[:, c, t * P:(t + 1) * P] for u in h], [u[:, c, :] for u in w2_s])):
                            last = pe.matmul(ring[3][:, t * D:(t + 1) * D], a, w, start=(c == 0 and m == 0),
                                             stop=(c == MC - 1 and m == 2))
                last.then_inc(y_raw, 1)

            def route(tb, out_):
                pe.wait_ge(z_split, tb + 1)
                product(out_[0:E, :], lambda k: [u[:, k, :] for u in rw],
                        lambda k: [u[:, BB * tb:BB * (tb + 1), k, :] for u in z], range(KC)).then_inc(router_raw, 1)

            def up(u, wait_w):
                if wait_w is not None:
                    pe.wait_ge(e_split, wait_w)
                if u.register is None and u.offset == 0:
                    pe.wait_ge(logits_made, TB - 1)
                if u.register is not None or u.offset > 1:
                    pe.wait_ge(hf_made, u(-1))
                for m, done in ((0, g_raw), (1, u_raw)):
                    product(bk(2 * u.parity + m),
                            lambda k: [w[:, m * D + k * P:m * D + (k + 1) * P] for w in e_w[u.slot]],
                            lambda k: [v[:, BB * u.tb:BB * (u.tb + 1), k, :] for v in z], range(KC)).then_inc(done, 1)

            def down(d, slots, tb):
                pe.wait_ge(hT_split, d.units)
                if d.register is None and d.offset == 0:
                    pe.wait_ge(zT_made, NB - 1)
                if d.register is None and d.offset == 1:
                    pe.wait_ge(score_made, 1)
                if d.register is not None or d.offset > 1:
                    pe.wait_ge(y_added, d.count(-1))
                for t in range(TPB):
                    last = product(bk2(4 + 2 * (tb % 2))[:, t * D:(t + 1) * D],
                                   lambda i: [w[:, i[1], t * P:(t + 1) * P] for w in hT],
                                   lambda i: [w[:, 2 * D:3 * D] for w in e_w[i[0]]], slots)
                last.then_inc(dn_raw, 1)

            class Unit:

                def __init__(self, offset, slot, tb, register):
                    self.offset, self.slot, self.tb, self.register = offset, slot, tb, register
                    self.parity = offset % 2

                def __call__(self, n):
                    value = self.offset + n
                    return value if self.register is None else self.register * (2 * TB) + value

            class Down:

                def __init__(self, offset, units, register=None):
                    self.offset, self.register, self._units = offset, register, units

                @property
                def units(self):
                    return self._units if self.register is None else self.register * (2 * TB) + self._units

                def count(self, n):
                    value = self.offset + n
                    return value if self.register is None else self.register * (2 * TB) + value

            def step(b):
                if live(b) and b != 1:
                    q_transposes(b, 0)
                if live(b - 1):
                    if b == 1:
                        pe.wait_ge(w_split[0], 4)
                        pe.wait_ge(w_split[1], 4)
                    mlp_up(b - 1, 0)
                    mlp_up(b - 1, 1)
                if b == 1:
                    q_transposes(b, 0)
                elif live(b):
                    q_transposes(b, 1)
                if live(b - 1):
                    mlp_up(b - 1, 2)
                if b == 1:
                    q_transposes(b, 1)
                if live(b - 1):
                    mlp_up(b - 1, 3)
                if live(b + 1):
                    first_transposes(b + 1)
                if live(b - 2) and live(b):
                    last_transposes(b - 2)
                if live(b):
                    attend(b)
                if live(b + 1):
                    fold_wo(b + 1)
                    queries(b + 1, 0)
                if b == NB - 1:
                    mlp_down(b - 1)
                if live(b):
                    middle_transposes(b)
                if live(b + 1):
                    queries(b + 1, 1)
                if b == NB - 1:
                    pe.wait_ge(rw_split, 2)
                    for tb in range(TB - 1):
                        route(tb, bk(tb))
                    last_transposes(b - 1)
                if b == NB:
                    for n in range(SH):
                        up(Unit(n, SH + n, 0, None), n + 1)
                if live(b - 1) and b != NB - 1:
                    mlp_down(b - 1)

            first_transposes(0)
            values(NB - 1)
            queries(0, 0)
            values_keys(NB - 2)
            queries(0, 1)
            values_keys(NB - 1)
            fold_wo(0)
            over_batches(step)

            def shared_up(tb):
                for n in range(SH):
                    up(Unit(SH * tb + n, SH + n, tb, None), None)

            def shared_down(tb):
                down(Down(tb, SH * (tb + 1)), [(SH + n, (SH * tb + n) % 4) for n in range(SH)], tb)

            shared_up(1)
            last_transposes(NB - 1)
            shared_down(0)
            route(TB - 1, ring[2])
            up(Unit(2 * SH, SH, 2, None), None)
            pe.wait_ge(logits_made, TB)
            for t in range(NT):
                last = pe.transpose(ring[3][:, t * E:(t + 1) * E], sT[0:E, t * P:(t + 1) * P], ident[0:E, 0:E])
            last.then_inc(scoreT_raw, 1)
            up(Unit(2 * SH + 1, SH + 1, 2, None), None)
            shared_down(1)
            shared_up(3)
            shared_down(2)

            def expert(s, first, register):
                for tb in range(TB):
                    o = SH * TB + TB * s + tb
                    up(Unit(o, s, tb, register),
                       None if tb else (SH + 1 + s if register is None else register * 2 + (SH + 1 + s)))
                    if first and tb == 0:
                        shared_down(TB - 1)
                    else:
                        p = (o - 1) % (2 * TB)
                        down(Down(TB + (o - 1 - SH * TB), o, register), [(p // TB, (o - 1) % 4)], p % TB)
            assert SH * TB % (2 * TB) == 0
            expert(0, True, None)
            expert(1, False, None)
            with pe.Fori(1, E // 2) as i:
                expert(0, False, i)
                expert(1, False, i)
            o = SH * TB + E * TB
            down(Down(TB + E * TB - 1, o), [(1, (o - 1) % 4)], TB - 1)

        @block.scalar
        def _(act):
            act.dma_start(cols[:], columns).then_inc(columns_in, 16)
            act.dma_start(rowsb[:], rows.broadcast_to([P, rows.shape[1]])).then_inc(small_in, 16)
            act.dma_start(rwf[:], router_t.rearrange("(k p) e -> p k e", p=P)).then_inc(small_in, 16)

            act.wait_ge(p_chain, 1)
            def key_value_hi(target, source, n, loaded, done):
                act.wait_ge(loaded[n], 16)
                act.activation(target[0][:, :, n * 512:(n + 1) * 512],
                               source.rearrange("p (k n) -> p k n", k=KC)[:, :, n * 512:(n + 1) * 512], ACT.Copy).then_inc(done, 1)

            act.activation(sq[:, 0:1], half[:, 0:1], ACT.Identity)
            act.wait_ge(columns_in, 16)
            act.wait_ge(cT_raw, 1)
            for k in range(KC):
                act.activation(cTf[:, k, 0:P], ring[2][:, k * P:(k + 1) * P], ACT.Identity,
                               bias=b1l[:, k:k + 1], scale=g1[:, k:k + 1]).then_inc(cTf_made, 1)
            for n in range(2):
                key_value_hi(wk_s, stage[0], n, wk_in, wk_hi)
            for n in range(2):
                key_value_hi(wv_s, stage[1], n, wv_in, wv_hi)
            act.wait_ge(cT_raw, 2)
            for k in range(KC):
                act.activation(cTf[:, k, P:CROWS], ring[2 + k][:, 0:CROWS - P], ACT.Identity,
                               bias=b1l[:, k:k + 1], scale=g1[:, k:k + 1]).then_inc(cTf_made, 1)

            def kv_out(b):
                act.wait_ge(m_raw, b + 1)
                m = bk2(6).rearrange("p (c d) -> p c d", c=IC)
                for s in (0, HEAD):
                    last = act.activation(kv_z[s:s + HEAD, b, :].rearrange("p (c d) -> p c d", c=IC),
                                          m[s:s + HEAD, :, s:s + HEAD], ACT.Copy)
                last.then_inc(kv_made, 1)

            def queries_in(a):
                act.wait_ge(a_raw, a + 1)
                if a:
                    act.wait_ge(QnT_split, a)
                for k in range(KC):
                    last = act.activation(QnTf[:, k * NQ:(k + 1) * NQ], bk(0)[:, k * NQ:(k + 1) * NQ], ACT.Identity,
                                          bias=b1l[:, k:k + 1], scale=g1[:, k:k + 1])
                last.then_inc(QnTf_made, 1)
                act.wait_ge(QnTf_made, a + 1)
                act.activation(QnT[0][:].rearrange("p k n -> p (k n)"), QnTf, ACT.Copy).then_inc(QnT_hi, 1)

            def weights_hi(n):
                act.wait_ge(w_in[n % 2], 16 * (n // 2 + 1))
                act.activation(w_halves[n][0], stage[0][:, (n % 2) * HALF:(n % 2 + 1) * HALF], ACT.Copy).then_inc(w_hi, 1)

            for b in range(NB):
                act.wait_ge(k_raw, b + 1)
                if b == 2:
                    act.wait_ge(cT_split, 2 * KC)
                if b:
                    act.wait_ge(k_ss, b)
                act.activation(sq[0:NK, :], bk2(2 * (b % 2))[0:NK, :], ACT.Square).then_inc(k_sq, 1)
                if b > 1:
                    kv_out(b - 2)
                if 1 <= b <= 4:
                    weights_hi(2 * (b - 1))
                if b == NB - 1:
                    queries_in(0)
                act.wait_ge(v_raw, b + 1)
                if b == 1:
                    act.wait_ge(wv_split[0], 1)
                    act.wait_ge(wv_split[1], 1)
                act.activation(vc[b % 2][0:NK, :], bk2(4)[0:NK, :], ACT.Copy).then_inc(v_made, 1)
                if 1 <= b <= 4:
                    weights_hi(2 * (b - 1) + 1)

            def queries_hi(b, t):
                for j in range(2):
                    act.wait_ge(qnT_raw, 4 * b + 2 * t + j + 1)
                    act.activation(qnT[0][:, 4 * j:4 * j + 4, t * P:(t + 1) * P],
                                   queries_bank(b, t, j).rearrange("p (c n) -> p c n", c=4), ACT.Copy).then_inc(qnT_hi, 1)

            def blocks_hi(a):
                if a == 0:
                    act.wait_ge(kvd_zero, 1)
                    act.wait_ge(kv_made, 1)
                else:
                    act.wait_ge(w_raw, 4 * a)
                for s in (0, HEAD):
                    last = act.activation(kvd[0][s:s + HEAD, :, s:s + HEAD],
                                          kv_z[s:s + HEAD, a, :].rearrange("p (c d) -> p c d", c=IC), ACT.Copy)
                last.then_inc(kvd_hi, 1)

            def W_high(a):
                for j in range(4):
                    act.wait_ge(w_raw, 4 * a + j + 1)
                    act.activation(W[0][:, 2 * j:2 * j + 2, :].rearrange("p c n -> p (c n)"), ring[(2 + j) % 4],
                                   ACT.Copy).then_inc(W_hi, 1)

            def squares(a, t):
                act.wait_ge(q_raw, TT * a + t + 1)
                if a == 0 and t == 0:
                    act.wait_ge(k_ss, NB)
                if a or t:
                    act.wait_ge(q_ss, TT * a + t)
                act.activation(sq[:], bk2(2 * t), ACT.Square).then_inc(q_sq, 1)

            def gelus(b, j):
                act.wait_ge(mlp_raw, 4 * b + j + 1)
                if b:
                    act.wait_ge(h_split, 4 * b + j - 3)
                for c in range(2 * j, 2 * j + 2):
                    last = act.activation(hf[:, j, (c % 2) * NQ:(c % 2 + 1) * NQ], ring[2 + j % 2][:, (c % 2) * NQ:(c % 2 + 1) * NQ],
                                          ACT.Gelu, bias=b1c[:, c:c + 1])
                last.then_inc(gelu, 1)

            def h_high(b, j):
                act.wait_ge(gelu, 4 * b + j + 1)
                act.activation(h[0][:, 2 * j:2 * j + 2, :].rearrange("p c n -> p (c n)"), hf[:, j, :], ACT.Copy).then_inc(h_hi, 1)

            def z_high(tb):
                act.wait_ge(zT_made, BB * (tb + 1))
                act.activation(z[0][:, BB * tb:BB * (tb + 1)].rearrange("p b k n -> p (b k n)"),
                               kvf[:, BB * tb * 512:BB * (tb + 1) * 512], ACT.Copy).then_inc(z_hi, 1)

            def z_copy(a):
                act.wait_ge(z_raw, a + 1)
                act.wait_ge(kvd_split, min(a + 3, NB))
                act.activation(kv_z[:, a, :], last_bank(a), ACT.Copy).then_inc(zT_made, 1)

            def logits(tb, src):
                act.wait_ge(router_raw, tb + 1)
                act.activation(sT[0:E, tb * BLK:(tb + 1) * BLK], src[0:E, :], ACT.Copy).then_inc(logits_made, 1)

            def expert_hi(n, register=None):
                if register is None:
                    act.wait_ge(e_in[n % 2], 16 * (n // 2 + 1))
                    if n > 3:
                        act.wait_ge(dn_raw, TB * (n - 2))
                else:
                    act.wait_ge(e_in[n % 2], register * 16 + 16 * (n // 2 + 1))
                    act.wait_ge(dn_raw, register * (2 * TB) + TB * (n - 2))
                dst = e_w[2 + n if n < SH and register is None else n % 2][0]
                act.activation(dst, e_raw[n % 2], ACT.Copy).then_inc(e_hi, 1)

            squares(0, 0)
            kv_out(NB - 2)
            blocks_hi(0)
            squares(0, 1)
            kv_out(NB - 1)
            W_high(0)

            def step(b):
                if b == NB:
                    z_copy(b - 2)
                if live(b) and b != 1:
                    queries_hi(b, 0)
                if live(b + 1) and b > 1:
                    blocks_hi(b + 1)
                if live(b - 1):
                    gelus(b - 1, 0)
                    gelus(b - 1, 1)
                    h_high(b - 1, 0)
                if b == 1:
                    queries_hi(b, 0)
                if live(b) and b != 1:
                    queries_hi(b, 1)
                if live(b - 1):
                    h_high(b - 1, 1)
                    gelus(b - 1, 2)
                if b == 1:
                    queries_hi(b, 1)
                if live(b - 1):
                    gelus(b - 1, 3)
                    h_high(b - 1, 2)
                    h_high(b - 1, 3)
                if live(b + 1):
                    queries_in(b + 1)
                if live(b - 2) and live(b):
                    z_copy(b - 2)
                if live(b + 1):
                    if b < 2:
                        blocks_hi(b + 1)
                    W_high(b + 1)
                    squares(b + 1, 0)
                if b == NB - 1:
                    z_high(2)
                    act.wait_ge(attn_raw, NB)
                    expert_hi(0)
                    expert_hi(1)
                if live(b):
                    act.wait_ge(xnT_raw, b + 1)
                    if b:
                        act.wait_ge(xnT_split, b)
                    for k in range(KC):
                        last = act.activation(xnTf[:, k * NQ:(k + 1) * NQ], ring[2][:, k * NQ:(k + 1) * NQ], ACT.Identity,
                                              bias=b2l[:, k:k + 1], scale=g2[:, k:k + 1])
                    last.then_inc(xnTf_made, 1)
                    act.wait_ge(xnTf_made, b + 1)
                    act.activation(xnT[0][:].rearrange("p k n -> p (k n)"), xnTf, ACT.Copy).then_inc(xnT_hi, 1)
                if live(b + 1):
                    squares(b + 1, 1)
                if b == NB - 2:
                    z_high(0)
                    z_high(1)
                if b == NB - 1:
                    act.wait_ge(acc_x1, NB)
                    for tb in range(TB - 1):
                        logits(tb, bk(tb))
            over_batches(step)

            def unit(o, register=None):
                def n(k):
                    return o + k if register is None else register * (2 * TB) + (o + k)
                act.wait_ge(g_raw, n(1))
                if register is not None or o > 1:
                    act.wait_ge(hf_made, n(-1))
                act.activation(sq[:, (o % 2) * BLK:(o % 2 + 1) * BLK], bk(2 * (o % 2)), ACT.Silu).then_inc(silu, 1)
                act.wait_ge(hf_made, n(1))
                if register is None and o < SH * TB + 4:
                    if o == 0:
                        act.wait_ge(y_raw, NB)
                    if o > 3:
                        act.wait_ge(dn_raw, o // SH - 1)
                else:
                    act.wait_ge(dn_raw, n(TB - SH * TB - 3))
                act.activation(hT[0][:, o % 4, :], hf[:, o % 4, :], ACT.Copy).then_inc(hT_hi, 1)

            def expert_pair(register):
                for o in range(SH * TB, SH * TB + 2 * TB):
                    unit(o, register)
                    if o % TB == 1:
                        s = (o - SH * TB) // TB
                        expert_hi(3 + s, register)
            for o in range(SH * TB + TB):
                unit(o)
                if o == 1:
                    expert_hi(2)
                if o == 2:
                    z_copy(NB - 1)
                    z_high(TB - 1)
                if o == 3:
                    expert_hi(3)
                    logits(TB - 1, ring[2])
                if o == 4:
                    act.wait_ge(scoreT_raw, 1)
                    act.activation(score, ring[3][:, 0:NT * E].rearrange("p (t e) -> p t e", e=E), ACT.Sigmoid).then_inc(score_made, 1)
            for o in range(SH * TB + TB, SH * TB + 2 * TB):
                unit(o)
                if o % TB == 1:
                    expert_hi(4)
            with act.Fori(1, E // 2 - 1) as i:
                expert_pair(i)
            last_pair = SH * TB + (E - 2) * TB
            for o in range(last_pair, last_pair + 2 * TB):
                unit(o)
                if o == last_pair + 1:
                    expert_hi(E + 1)

        @block.vector
        def _(dve):
            def context_norm(c):
                r = P if c < CT - 1 else CLAST
                dve.tensor_scalar(c0[0:r, c, :], c0[0:r, c, :], mv[0:r, c, 0:1], rs_c[0:r, c:c + 1],
                                  ALU.subtract, ALU.mult).then_inc(c_norm, 1)

            def context_halves(k, part_, n):
                dve.wait_ge(cTf_made, n + 1)
                dve.tensor_copy(cT[0][:, k, part_], cTf[:, k, part_]).then_inc(cT_hi, 1)
                dve.wait_ge(cT_hi, n + 1)
                split_lo(dve, cT[1][:, k, part_], cTf[:, k, part_], cT[0][:, k, part_]).then_inc(cT_split, 1)

            dve.wait_ge(ctx_first, 16)
            dve.bn_stats(stat[:, 0, :], c0[:, 0, :]).then_inc(c_part, 1)
            dve.wait_ge(c_part, 1)
            dve.bn_aggr(mv[:, 0, :], stat[:, 0, :]).then_inc(c_stats, 1)
            dve.wait_ge(c_rstd, 1)
            context_norm(0)
            dve.wait_ge(ctx_loaded, 32)
            for c in range(1, CT):
                r = P if c < CT - 1 else CLAST
                dve.bn_stats(stat[0:r, c, :], c0[0:r, c, :]).then_inc(c_part, 1)
            dve.wait_ge(c_part, CT)
            for c in range(1, CT):
                r = P if c < CT - 1 else CLAST
                last = dve.bn_aggr(mv[0:r, c, :], stat[0:r, c, :])
            last.then_inc(c_stats, 1)

            def key_value_lo(target, source, hi, done):
                dve.wait_ge(hi, 1)
                sl = [w[:, :, 0:512] for w in target]
                split_lo(dve, sl[1], source.rearrange("p (k n) -> p k n", k=KC)[:, :, 0:512], sl[0]).then_inc(done[0], 1)

            for k in range(KC):
                context_halves(k, slice(0, P), k)
            key_value_lo(wk_s, stage[0], wk_hi, wk_split)
            dve.wait_ge(c_rstd, 2)
            for c in range(1, CT):
                context_norm(c)
            key_value_lo(wv_s, stage[1], wv_hi, wv_split)
            for k in range(KC):
                context_halves(k, slice(P, CROWS), KC + k)
            def heads(a):
                return a.rearrange("p (h d) -> p h d", h=NH)

            def keys_norm(b):
                dve.wait_ge(k_rs, b + 1)
                if b > 1:
                    dve.wait_ge(m_raw, b - 1)
                elif b == 1:
                    dve.wait_ge(wv_split[0], 1)
                    dve.wait_ge(wv_split[1], 1)
                dve.tensor_tensor(heads(kn[b % 2][0:NK, :]), heads(bk2(2 * (b % 2))[0:NK, :]),
                                  rs_n[0:NK, b % 2, :].unsqueeze(2).broadcast_to([NK, NH, HEAD]), ALU.mult).then_inc(kn_made, 1)

            def queries_lo(b, t):
                for j in range(2):
                    dve.wait_ge(qnT_hi, 4 * b + 2 * t + j + 1)
                    sl = [u[:, 4 * j:4 * j + 4, t * P:(t + 1) * P] for u in qnT]
                    split_lo(dve, sl[1], queries_bank(b, t, j).rearrange("p (c n) -> p c n", c=4), sl[0]).then_inc(qnT_split, 1)

            def h_low(b, j):
                dve.wait_ge(h_hi, 4 * b + j + 1)
                sl = [u[:, 2 * j:2 * j + 2, :].rearrange("p c n -> p (c n)") for u in h]
                split_lo(dve, sl[1], hf[:, j, :], sl[0]).then_inc(h_split, 1)

            def stats(st, rows_, done):
                for t in range(TT):
                    dve.bn_stats(st[:, t, :], rows_[:, t * D:(t + 1) * D]).then_inc(done, 1)

            def mean_variance(st, mv_, done, b):
                dve.wait_ge(done, TT * (b + 1))
                for t in range(TT):
                    last = dve.bn_aggr(mv_[:, t, :], st[:, t, :])
                return last

            def normalize(dst, src, mv_, rs):
                for t in range(TT):
                    last = dve.tensor_scalar(dst[:, t * D:(t + 1) * D], src[:, t * D:(t + 1) * D],
                                             mv_[:, t, 0:1], rs[:, t:t + 1], ALU.subtract, ALU.mult)
                return last

            def queries_norm(a, t):
                dve.wait_ge(q_rs, TT * a + t + 1)
                if a:
                    dve.wait_ge(qnT_raw, 4 * a)
                elif t == 0:
                    dve.wait_ge(w_split[0], 4)
                    dve.wait_ge(w_split[1], 4)
                dve.tensor_tensor(heads(qn[:, t, :]), heads(bk2(2 * t)),
                                  rs_n[:, t, :].unsqueeze(2).broadcast_to([P, NH, HEAD]), ALU.mult).then_inc(qn_made, 1)

            def z_norm(a):
                dve.wait_ge(x3_rstd, a + 1)
                if a:
                    dve.wait_ge(z_raw, a)
                normalize(z0, acc[:, a, :], mv_3, rs_3).then_inc(z0_made, 1)

            def rows_out(a):
                dve.wait_ge(y_raw, a + 1)
                dve.wait_ge(acc_x1, a + 1)
                dve.tensor_tensor(acc[:, a, :], ring[3], acc[:, a, :], ALU.add).then_inc(x3_made, 1)

            def rows_stats(a):
                dve.wait_ge(x3_made, a + 1)
                stats(st_3, acc[:, a, :], x3_part)
                mean_variance(st_3, mv_3, x3_part, a).then_inc(x3_stats, 1)

            def product_gu(o, register=None):
                def n(k):
                    return o + k if register is None else register * (2 * TB) + (o + k)
                dve.wait_ge(silu, n(1))
                if register is None and o == 0:
                    dve.wait_ge(h_split, 4 * NB)
                dve.wait_ge(u_raw, n(1))
                if register is not None or o > 3:
                    dve.wait_ge(hT_split, n(-3))
                dve.tensor_tensor(hf[:, o % 4, :], bk(2 * (o % 2) + 1), sq[:, (o % 2) * BLK:(o % 2 + 1) * BLK],
                                  ALU.mult).then_inc(hf_made, 1)

            def z_low(tb):
                dve.wait_ge(z_hi, tb + 1)
                zs = [u[:, BB * tb:BB * (tb + 1)].rearrange("p b k n -> p (b k n)") for u in z]
                split_lo(dve, zs[1], kvf[:, BB * tb * 512:BB * (tb + 1) * 512], zs[0]).then_inc(z_split, 1)

            def W_low(a, j):
                dve.wait_ge(W_hi, 4 * a + j + 1)
                sl = [u_[:, 2 * j:2 * j + 2, :].rearrange("p c n -> p (c n)") for u_ in W]
                split_lo(dve, sl[1], ring[(2 + j) % 4], sl[0]).then_inc(W_split, 1)

            def x_statistics(a):
                dve.wait_ge(x_in, 16 * (a // 2 + 1))
                stats(st_x, acc[:, a, :], x_part)

            def x_mean_variance(a):
                mean_variance(st_x, mv_x, x_part, a).then_inc(x_stats, 1)

            def x_normalize(a):
                dve.wait_ge(x_rstd, a + 1)
                normalize(Q[a % 2], acc[:, a, :], mv_x, rs_x).then_inc(Q_made, 1)

            def Q_statistics(a):
                dve.wait_ge(Q_made, a + 1)
                stats(st_q, Q[a % 2], q_part)
                mean_variance(st_q, mv_q, q_part, a).then_inc(q_stats, 1)

            def Q_normalize(a):
                dve.wait_ge(q2_rstd, a + 1)
                if a:
                    dve.wait_ge(a_raw, a)
                normalize(Qn0, Q[a % 2], mv_q, rs_q2).then_inc(Qn0_made, 1)

            def queries_in_low(a):
                dve.wait_ge(QnT_hi, a + 1)
                u = [w[:].rearrange("p k n -> p (k n)") for w in QnT]
                split_lo(dve, u[1], QnTf, u[0]).then_inc(QnT_split, 1)

            def blocks_low(a):
                dve.wait_ge(kvd_hi, a + 1)
                for s in (0, HEAD):
                    last = split_lo(dve, kvd[1][s:s + HEAD, :, s:s + HEAD],
                                    kv_z[s:s + HEAD, a, :].rearrange("p (c d) -> p c d", c=IC),
                                    kvd[0][s:s + HEAD, :, s:s + HEAD])
                last.then_inc(kvd_split, 1)

            def queries_sums(a, t):
                dve.wait_ge(q_sq, TT * a + t + 1)
                dve.tensor_reduce(ss[:, t, :], heads(sq[:]), AX.X, ALU.add).then_inc(q_ss, 1)

            for b in range(NB):
                if b:
                    keys_norm(b - 1)
                if b == NB - 1:
                    Q_normalize(0)
                dve.wait_ge(k_sq, b + 1)
                dve.tensor_reduce(ss[0:NK, b % 2, :], heads(sq[0:NK, :]), AX.X, ALU.add).then_inc(k_ss, 1)
                if 1 <= b <= 4:
                    n = 2 * (b - 1)
                    dve.wait_ge(w_hi, n + 1)
                    split_lo(dve, w_halves[n][1], stage[0][:, 0:HALF], w_halves[n][0]).then_inc(w_split[0], 1)
                if b == NB - 3:
                    x_statistics(0)
                    x_mean_variance(0)
                if b == NB - 2:
                    x_normalize(0)
                    Q_statistics(0)
                    x_statistics(1)
                    x_mean_variance(1)
                if b == NB - 1:
                    x_normalize(1)
                    Q_statistics(1)
            dve.wait_ge(small_in, 32)
            dve.tensor_copy(rw[0][:], rwf[:]).then_inc(rw_split, 1)
            dve.wait_ge(rw_split, 1)
            split_lo(dve, rw[1][:], rwf[:], rw[0][:]).then_inc(rw_split, 1)
            queries_in_low(0)
            keys_norm(NB - 1)
            queries_sums(0, 0)
            Q_normalize(1)
            blocks_low(0)
            queries_norm(0, 0)
            queries_sums(0, 1)
            for j in range(4):
                W_low(0, j)
            queries_norm(0, 1)

            def step(b):
                if live(b):
                    queries_lo(b, 0)
                if live(b + 1) and b > 1:
                    blocks_low(b + 1)
                if live(b - 1):
                    h_low(b - 1, 0)
                if live(b - 2) and live(b):
                    z_norm(b - 2)
                if live(b + 2):
                    x_statistics(b + 2)
                if live(b):
                    queries_lo(b, 1)
                if live(b + 2):
                    x_mean_variance(b + 2)
                if live(b - 1):
                    h_low(b - 1, 1)
                if live(b - 1):
                    h_low(b - 1, 2)
                    h_low(b - 1, 3)
                if live(b + 1):
                    queries_in_low(b + 1)
                    if b < 2:
                        blocks_low(b + 1)
                if b == NB - 1:
                    z_low(0)
                    z_low(1)
                    z_low(2)
                if b == NB:
                    product_gu(0)
                if live(b):
                    dve.wait_ge(attn_raw, b + 1)
                    dve.wait_ge(Qb_made, b + 1)
                    if b > 1:
                        dve.wait_ge(acc_x1, b - 1)
                    dve.tensor_tensor(x1[b % 2], ring[1], Q[b % 2], ALU.add).then_inc(x1_made, 1)
                    dve.wait_ge(x1_made, b + 1)
                    stats(st_1, x1[b % 2], x1_part)
                if live(b + 1):
                    W_low(b + 1, 0)
                if live(b):
                    mean_variance(st_1, mv_1, x1_part, b).then_inc(x1_stats, 1)
                if live(b + 1):
                    W_low(b + 1, 1)
                if live(b + 2):
                    x_normalize(b + 2)
                if live(b + 1):
                    W_low(b + 1, 2)
                if live(b):
                    dve.wait_ge(x1_rstd, b + 1)
                    if b:
                        dve.wait_ge(xnT_raw, b)
                    normalize(xn0, x1[b % 2], mv_1, rs_1).then_inc(xn0_made, 1)
                if live(b + 1):
                    W_low(b + 1, 3)
                if live(b + 2):
                    Q_statistics(b + 2)
                if live(b + 1):
                    queries_sums(b + 1, 0)
                if live(b + 2):
                    Q_normalize(b + 2)
                if b == NB - 1:
                    rows_out(b - 1)
                    rows_stats(b - 1)
                if live(b):
                    dve.wait_ge(xnT_hi, b + 1)
                    u = [w[:].rearrange("p k n -> p (k n)") for w in xnT]
                    split_lo(dve, u[1], xnTf, u[0]).then_inc(xnT_split, 1)
                if live(b + 1):
                    queries_sums(b + 1, 1)
                if live(b + 1):
                    queries_norm(b + 1, 0)
                if live(b - 1) and b != NB - 1:
                    rows_out(b - 1)
                if live(b + 1):
                    queries_norm(b + 1, 1)
                if live(b - 1) and b != NB - 1:
                    rows_stats(b - 1)
                if b == NB - 1:
                    z_norm(b - 1)
                if b == NB:
                    product_gu(1)
                    z_norm(b - 1)

            over_batches(step)

            linked = [0]

            def link(ins):
                linked[0] += 1
                ins.then_inc(r_chain, 1)
                dve.wait_ge(r_chain, linked[0])

            def route_groups():
                link(dve.tensor_tensor(biased, score, ebias.unsqueeze(1).broadcast_to([P, NT, E]), ALU.add))
                v = biased.rearrange("p t (q c) -> p (t q) c", c=2)
                larger, both = (w.rearrange("p t g a -> p (t g a)") for w in (pair_max, pair_sum))
                link(dve.tensor_tensor(larger, v[:, :, 0], v[:, :, 1], ALU.max))
                link(dve.tensor_tensor(both, v[:, :, 0], v[:, :, 1], ALU.add))
                link(dve.tensor_tensor(gs, pair_max[:, :, :, 0], pair_max[:, :, :, 1], ALU.add))
                link(dve.tensor_tensor(gs, gs, pair_sum[:, :, :, 0], ALU.max))
                link(dve.tensor_tensor(gs, gs, pair_sum[:, :, :, 1], ALU.max))

            def rank_groups():
                n = GROUPS
                for g in range(n):
                    last = dve.memset(grank[:, :, g:g + 1], float(n - 1 - g))
                link(last)
                for d in range(1, n):
                    link(dve.tensor_tensor(gcmp[:, :, 0:n - d], gs[:, :, 0:n - d], gs[:, :, d:n], ALU.is_ge))
                    link(dve.tensor_tensor(grank[:, :, d:n], grank[:, :, d:n], gcmp[:, :, 0:n - d], ALU.add))
                    link(dve.tensor_tensor(grank[:, :, 0:n - d], grank[:, :, 0:n - d], gcmp[:, :, 0:n - d], ALU.subtract))

            def compare(d):
                dve.tensor_tensor(ahead[d], biased[:, :, 0:E - d], biased[:, :, d:E], ALU.is_ge).then_inc(compared, 1)

            def count_earlier(d):
                dve.wait_ge(compared, d)
                dve.wait_ge(earlier_counted, d)
                dve.tensor_tensor(rank[:, :, d:E], rank[:, :, d:E], ahead[d], ALU.add).then_inc(earlier_counted, 1)

            def mask_groups():
                b4 = biased.rearrange("p t (g e) -> p (t g) e", g=GROUPS)
                link(dve.scalar_tensor_tensor(out=b4, in0=grank.rearrange("p t g -> p (t g)").unsqueeze(2).broadcast_to([P, NT * GROUPS, EG]),
                                              scalar=float(TOPG), in1=b4, op0=ALU.is_lt, op1=ALU.mult))

            def combine():
                dve.wait_ge(earlier_counted, E)
                dve.wait_ge(later_counted, E)
                link(dve.tensor_tensor(rank, rank, later, ALU.subtract))
                link(dve.scalar_tensor_tensor(out=rank, in0=rank, scalar=float(TOPK), in1=score, op0=ALU.is_lt, op1=ALU.mult))
                link(dve.tensor_reduce(wsum, rank, AX.X, ALU.add))
                link(dve.tensor_scalar(wsum, wsum, 1e-20, None, ALU.add))
                link(dve.reciprocal(winv, wsum))
                dve.scalar_tensor_tensor(out=C_all.rearrange("p e t -> p t e"), in0=rank, scalar=SCALE,
                                         in1=winv.unsqueeze(2).broadcast_to([P, NT, E]), op0=ALU.mult, op1=ALU.mult).then_inc(c_made, 1)

            def low_half(o, register=None):
                dve.wait_ge(hT_hi, o + 1 if register is None else register * (2 * TB) + (o + 1))
                split_lo(dve, hT[1][:, o % 4, :], hf[:, o % 4, :], hT[0][:, o % 4, :]).then_inc(hT_split, 1)

            def add_shared(tb):
                dve.wait_ge(dn_raw, tb + 1)
                a = acc[:, BB * tb:BB * (tb + 1), :].rearrange("p b n -> p (b n)")
                dve.tensor_tensor(a, bk2(4 + 2 * (tb % 2)), a, ALU.add).then_inc(y_added, 1)

            def add_expert(o, register=None):
                tb, s = o % TB, (o // TB) % 2
                d = TB + o - SH * TB
                dve.wait_ge(dn_raw, d + 1 if register is None else register * (2 * TB) + (d + 1))
                if tb == 0:
                    dve.wait_ge(c_copied, s + 1 if register is None else register * 2 + (s + 1))
                dve.wait_ge(y_added, d + 1 - TB if register is None else register * (2 * TB) + (d + 1 - TB))
                a = acc[:, BB * tb:BB * (tb + 1), :].rearrange("p b n -> p (b n)")
                for t in range(TPB):
                    last = dve.scalar_tensor_tensor(out=a[:, t * D:(t + 1) * D], in0=bk2(4 + 2 * (tb % 2))[:, t * D:(t + 1) * D],
                                                    scalar=c_now[s][:, TPB * tb + t:TPB * tb + t + 1],
                                                    in1=a[:, t * D:(t + 1) * D], op0=ALU.mult, op1=ALU.add)
                last.then_inc(y_added, 1)

            low_half(0)
            low_half(1)
            product_gu(2)
            low_half(2)
            z_low(TB - 1)
            product_gu(3)
            low_half(3)
            add_shared(0)
            product_gu(4)
            low_half(4)
            dve.wait_ge(score_made, 1)
            route_groups()
            product_gu(5)
            low_half(5)
            rank_groups()
            mask_groups()
            product_gu(6)
            ahead_of = E // 3
            for d in range(1, ahead_of + 1):
                compare(d)
            product_gu(7)
            low_half(6)
            add_shared(1)
            low_half(7)
            for d in range(1, E):
                if d + ahead_of < E:
                    compare(d + ahead_of)
                count_earlier(d)
                if d == E // 2:
                    product_gu(8)
                    add_shared(2)
                    low_half(8)
                if d == E - 4:
                    product_gu(9)
                    add_shared(TB - 1)
                    low_half(9)
            product_gu(10)
            combine()
            low_half(10)
            add_expert(8)
            add_expert(9)
            o0 = SH * TB
            assert o0 == 8
            for o in range(o0 + 3, o0 + 2 * TB):
                product_gu(o)
                low_half(o)
                add_expert(o - 1)
            with dve.Fori(1, E // 2) as i:
                for o in range(o0, o0 + 2 * TB):
                    product_gu(o, i)
                    low_half(o, i)
                    add_expert(o - 1, i)
            add_expert(o0 + E * TB - 1)

        @block.gpsimd
        def _(pool):
            pool.memset(ident[:], 0.0).then_inc(ident_zero, 1)
            pool.wait_ge(ident_zero, 1)
            pool.affine_select(out=ident[:], in_=ident[:], compare_op=ALU.not_equal, fill=1.0, base=0,
                               pattern=[[-1, P]], channel_multiplier=1).then_inc(ident_made, 1)
            pool.memset(half[:], -0.5).then_inc(p_chain, 1)
            for u in kvd:
                last = pool.memset(u[:].rearrange("p c n -> p (c n)").bitcast(F32), 0.0)
            last.then_inc(kvd_zero, 1)
            chained = [1]

            def power(dst, src, add, op):
                n = dst.shape[1]
                pool.tensor_scalar(dst, src, add, None, op).then_inc(p_chain, 1)
                chained[0] += 1
                pool.wait_ge(p_chain, chained[0])
                return pool.tensor_tensor(dst, dst, half[0:dst.shape[0], 0:n], ALU.pow)

            pool.wait_ge(c_stats, 1)
            power(rs_c[:, 0:1], mv[:, 0:1, 1], EPS, ALU.add).then_inc(c_rstd, 1)
            pool.wait_ge(c_rstd, 1)
            pool.wait_ge(c_stats, 2)
            power(rs_c[:, 1:CT - 1], mv[:, 1:CT - 1, 1], EPS, ALU.add).then_inc(p_chain, 1)
            chained[0] += 1
            power(rs_c[0:CLAST, CT - 1:CT], mv[0:CLAST, CT - 1, 1:2], EPS, ALU.add).then_inc(c_rstd, 1)

            def key_value_lo(target, source, hi, done):
                pool.wait_ge(hi, 2)
                sl = [w[:, :, 512:1024] for w in target]
                split_lo(pool, sl[1], source.rearrange("p (k n) -> p k n", k=KC)[:, :, 512:1024], sl[0]).then_inc(done[1], 1)
            key_value_lo(wk_s, stage[0], wk_hi, wk_split)
            key_value_lo(wv_s, stage[1], wv_hi, wv_split)

            def x_scales(a):
                pool.wait_ge(x_stats, a + 1)
                power(rs_x[:], mv_x[:, :, 1], EPS, ALU.add).then_inc(x_rstd, 1)

            def Q_scales(a):
                pool.wait_ge(q_stats, a + 1)
                power(rs_q2[:], mv_q[:, :, 1], EPS, ALU.add).then_inc(q2_rstd, 1)

            def queries_scales(a, t):
                pool.wait_ge(q_ss, TT * a + t + 1)
                power(rs_n[:, t, :], ss[:, t, :], 1e-24, ALU.max).then_inc(q_rs, 1)

            def biases(a):
                pool.wait_ge(Qn0_made, a + 1)
                if a == 0:
                    pool.wait_ge(small_in, 32)
                q3 = Q[a % 2].rearrange("p (t d) -> p t d", t=TT)
                pool.tensor_tensor(q3, q3, bo_r.unsqueeze(1).broadcast_to([P, TT, D]), ALU.add).then_inc(Qb_made, 1)
                a3 = acc[:, a, :].rearrange("p (t d) -> p t d", t=TT)
                pool.tensor_tensor(a3, a3, b2_r.unsqueeze(1).broadcast_to([P, TT, D]), ALU.add).then_inc(acc_b2, 1)

            for b in range(NB):
                pool.wait_ge(k_ss, b + 1)
                if b > 1:
                    pool.wait_ge(kn_made, b - 1)
                power(rs_n[0:NK, b % 2, :], ss[0:NK, b % 2, :], 1e-24, ALU.max).then_inc(k_rs, 1)
                if 1 <= b <= 4:
                    n = 2 * (b - 1) + 1
                    pool.wait_ge(w_hi, n + 1)
                    split_lo(pool, w_halves[n][1], stage[0][:, HALF:2 * HALF], w_halves[n][0]).then_inc(w_split[1], 1)
                if b == NB - 3:
                    x_scales(0)
                if b == NB - 2:
                    Q_scales(0)
                    x_scales(1)
            Q_scales(1)
            queries_scales(0, 0)
            queries_scales(0, 1)
            biases(0)
            biases(1)

            def expert_lo(n, register=None):
                pool.wait_ge(e_hi, n + 1 if register is None else register * 2 + (n + 1))
                w = e_w[2 + n if n < SH and register is None else n % 2]
                split_lo(pool, w[1], e_raw[n % 2], w[0]).then_inc(e_split, 1)

            def step(b):
                if live(b + 2):
                    x_scales(b + 2)
                if live(b):
                    pool.wait_ge(x1_stats, b + 1)
                    power(rs_1[:], mv_1[:, :, 1], EPS, ALU.add).then_inc(x1_rstd, 1)
                    pool.wait_ge(acc_b2, b + 1)
                    pool.tensor_tensor(acc[:, b, :], acc[:, b, :], x1[b % 2], ALU.add).then_inc(acc_x1, 1)
                if live(b + 2):
                    Q_scales(b + 2)
                if live(b + 1):
                    for t in range(TT):
                        queries_scales(b + 1, t)
                if live(b + 2):
                    biases(b + 2)
                if live(b - 1):
                    pool.wait_ge(x3_stats, b)
                    power(rs_3[:], mv_3[:, :, 1], EPS, ALU.add).then_inc(x3_rstd, 1)
                if b == NB - 1:
                    for n in range(SH):
                        expert_lo(n)
            over_batches(step)

            def count_later():
                for e in range(E):
                    last = pool.memset(rank[:, :, e:e + 1], float(E - 1 - e))
                last.then_inc(earlier_counted, 1)
                pool.memset(later, 0.0).then_inc(later_counted, 1)
                for d in range(1, E):
                    pool.wait_ge(compared, d)
                    pool.wait_ge(later_counted, d)
                    pool.tensor_tensor(later[:, :, 0:E - d], later[:, :, 0:E - d], ahead[d], ALU.add).then_inc(later_counted, 1)

            def expert_rows(s, register=None):
                if register is not None:
                    pool.wait_ge(y_added, register * (2 * TB) + TB * s)
                pool.tensor_copy(c_now[s], C_all[:, s if register is None else register * 2 + s, :]).then_inc(c_copied, 1)
            for n in range(SH, 2 * SH):
                expert_lo(n)
            count_later()
            pool.wait_ge(c_made, 1)
            for s in range(2):
                expert_rows(s)
            with pool.Fori(1, E // 2) as i:
                for s in range(2):
                    expert_lo(SH + s, i)
                    expert_rows(s, i)


_INS = ["x", "ctx_1024", "L0_xattn_wq", "L0_xattn_wk", "L0_xattn_wv", "L0_xattn_wo", "L0_xattn_w1", "L0_xattn_w2"]


def kernel(**inputs):
    import numpy as np
    import concourse.bacc as bacc
    from concourse.bass_utils import run_bass_kernel_spmd as run

    def given(name):
        return np.ascontiguousarray(inputs[name])

    def chunks(v):
        return v.reshape(-1, P).T

    def expert_layout(gate, up, down):
        n, inner, d = gate.shape
        g, u = (np.transpose(w, (0, 2, 1)).reshape(n, d // P, P, inner).transpose(0, 2, 1, 3).reshape(n, P, -1) for w in (gate, up))
        return np.concatenate([g, u, np.transpose(down, (0, 2, 1))], axis=2)

    arrays = {f"in_{n}": given(n) for n in _INS}
    arrays["in_router_t"] = np.ascontiguousarray(given("L0_ffn_router_weight").T)
    arrays["in_columns"] = np.ascontiguousarray(np.concatenate(
        [chunks(given("L0_xattn_" + n)) for n in ("ln1_g", "ln1_b", "ln2_g", "ln2_b", "b1")], axis=1))
    arrays["in_rows"] = np.concatenate([given("L0_xattn_bo"), given("L0_xattn_b2"), given("L0_ffn_e_bias")])[None, :]
    gate, up, down = (given("L0_ffn_" + n) for n in ("gate_w", "up_w", "down_w"))
    inner, d = gate.shape[1:]
    sg, su, sd = (given("L0_ffn_sh_" + n) for n in ("gate_w", "up_w", "down_w"))
    shared = expert_layout(sg.reshape(-1, inner, d), su.reshape(-1, inner, d), sd.reshape(d, -1, inner).transpose(1, 0, 2))
    arrays["in_experts"] = np.ascontiguousarray(np.concatenate([shared, expert_layout(gate, up, down)], axis=0))

    nc = bacc.Bacc("TRN2", target_bir_lowering=False, num_devices=1)
    args = [nc.dram_tensor(n, a.shape, mybir.dt.from_np(a.dtype), kind="ExternalInput").ap() for n, a in arrays.items()]
    args.append(nc.dram_tensor("out_0", arrays["in_x"].shape, F32, kind="ExternalOutput").ap())
    bass_cross_attention_ffn_moe_kernel(nc, *args)
    result = run(nc, [arrays], core_ids=[0])
    return result.results[0]["out_0"]
```
